# Optimizing a Trainium2 kernel written in Bass

```python
import numpy as np
import jax
import jax.numpy as jnp

def _softmax(x, axis=-1):
    return jax.nn.softmax(x, axis=axis)

def _gelu(x):
    return jax.nn.gelu(x, approximate=True)

def _silu(x):
    return jax.nn.silu(x)

def _sigmoid(x):
    return jax.nn.sigmoid(x)

def _layernorm(x, axis=-1, eps=1e-05):
    m = jnp.mean(x, axis=axis, keepdims=True)
    v = jnp.var(x, axis=axis, keepdims=True)
    return (x - m) / jnp.sqrt(v + eps)

def _scatter_add(tgt, idx, src, axis=0):
    return tgt.at[idx].add(src)

def _segment_sum(src, seg, n):
    return jax.ops.segment_sum(src, seg, n)
kernel_name = 'mk_adaln_d2_jaxref_r8_111f4b'

def setup_inputs(seed: int=0):
    np.random.seed(seed)
    _w = jnp.asarray

    def _L0_attn_setup():
        import jax, jax.numpy as jnp
        import numpy as np
        D_MODEL = 128
        N_HEADS = 16
        HEAD_DIM = D_MODEL // N_HEADS
        key = jax.random.key(seed)
        k1, k2, k3 = jax.random.split(key, 3)
        scale = 1.0 / np.sqrt(D_MODEL)
        x = jax.random.normal(k1, (4, 256, D_MODEL), dtype=jnp.float32)
        w_qkv = jax.random.normal(k2, (D_MODEL, 3 * D_MODEL), dtype=jnp.float32) * scale
        b_qkv = jnp.zeros((3 * D_MODEL,), dtype=jnp.float32)
        w_proj = jax.random.normal(k3, (D_MODEL, D_MODEL), dtype=jnp.float32) * scale
        b_proj = jnp.zeros((D_MODEL,), dtype=jnp.float32)
        return {'x': x, 'w_qkv': w_qkv, 'b_qkv': b_qkv, 'w_proj': w_proj, 'b_proj': b_proj}
    _L0_attn_in = _L0_attn_setup()

    def _L0_ffn_setup():
        import jax, jax.numpy as jnp
        import numpy as np
        B, S, D, H, E, K = (4, 128, 128, 256, 8, 2)
        key = jax.random.key(seed)
        ks = jax.random.split(key, 5)
        s = 0.02
        return {'x': jax.random.normal(ks[0], (B, S, D), jnp.float32), 'W1': jax.random.normal(ks[1], (E, H, D), jnp.float32) * s, 'b1': jnp.zeros((E, H), jnp.float32), 'W2': jax.random.normal(ks[2], (E, D, H), jnp.float32) * s, 'b2': jnp.zeros((E, D), jnp.float32), 'Wg': jax.random.normal(ks[3], (E, D), jnp.float32) * s, 'bg': jnp.zeros((E,), jnp.float32)}
    _L0_ffn_in = _L0_ffn_setup()
    _L0_c = _w((lambda *s: np.random.randn(*s).astype(np.float32) * 0.05)(8, 128))
    _L0_wmod = _w((lambda *s: np.random.randn(*s).astype(np.float32) * 0.05)(128, 6 * 128) * 128 ** (-0.5))

    def _L1_attn_setup():
        import jax, jax.numpy as jnp
        import numpy as np
        import math
        B, L, HID = (2, 512, 128)
        NH, DK, DV = (12, 64, 128)
        KD, VD, CS = (NH * DK, NH * DV, 4)
        SCALE = DK ** (-0.5)

        def _causal_depthwise_conv(x, w):
            c, k = w.shape
            xt = jnp.transpose(x, (0, 2, 1))
            out = jax.lax.conv_general_dilated(xt, w[:, None, :], window_strides=(1,), padding=[(k - 1, 0)], feature_group_count=c, dimension_numbers=('NCH', 'OIH', 'NCH'))
            return jnp.transpose(out, (0, 2, 1))

        def _l2norm(x, eps=1e-06):
            return x * jax.lax.rsqrt(jnp.sum(x * x, axis=-1, keepdims=True) + eps)

        def _gated_delta_net(hidden_states, Wq, Wk, Wv, Wg, Wo, conv_q, conv_k, conv_v, Wgk, Wb, b_b, A_log, dt_bias, g_norm_weight):
            b, l, _ = hidden_states.shape
            q = jax.nn.silu(_causal_depthwise_conv(hidden_states @ Wq, conv_q))
            k = jax.nn.silu(_causal_depthwise_conv(hidden_states @ Wk, conv_k))
            v = jax.nn.silu(_causal_depthwise_conv(hidden_states @ Wv, conv_v))
            gk = -jnp.exp(A_log) * jax.nn.softplus(hidden_states @ Wgk + dt_bias)
            beta = jax.nn.sigmoid(hidden_states @ Wb + b_b)
            q = jnp.transpose(q.reshape(b, l, NH, DK), (0, 2, 1, 3))
            k = jnp.transpose(k.reshape(b, l, NH, DK), (0, 2, 1, 3))
            v = jnp.transpose(v.reshape(b, l, NH, DV), (0, 2, 1, 3))
            q = _l2norm(q) * SCALE
            k = _l2norm(k)
            qs = jnp.moveaxis(q, 2, 0)
            ks_ = jnp.moveaxis(k, 2, 0)
            vs = jnp.moveaxis(v, 2, 0)
            bs = jnp.moveaxis(beta, 1, 0)
            gs = jnp.moveaxis(gk, 1, 0)

            def step(S, inp):
                qt, kt, vt, bt, gt = inp
                S = S * jnp.exp(gt)[..., None, None]
                kv = jnp.einsum('bhk,bhkv->bhv', kt, S)
                delta = (vt - kv) * bt[..., None]
                S = S + jnp.einsum('bhk,bhv->bhkv', kt, delta)
                ot = jnp.einsum('bhk,bhkv->bhv', qt, S)
                return (S, ot)
            S0 = jnp.zeros((b, NH, DK, DV), hidden_states.dtype)
            _, os_ = jax.lax.scan(step, S0, (qs, ks_, vs, bs, gs))
            o = jnp.moveaxis(os_, 0, 1)
            g = (hidden_states @ Wg).reshape(b, l, NH, DV)
            var = jnp.mean(o * o, axis=-1, keepdims=True)
            o = o * jax.lax.rsqrt(var + 1e-05) * g_norm_weight
            o = o * g * jax.nn.sigmoid(g)
            return o.reshape(b, l, VD) @ Wo
        key = jax.random.key(seed)
        ks = jax.random.split(key, 16)
        rn = lambda i, shape, s: jax.random.normal(ks[i], shape, jnp.float32) * s
        hidden_states = rn(0, (B, L, HID), 1.0)
        Wq = rn(1, (HID, KD), HID ** (-0.5))
        Wk = rn(2, (HID, KD), HID ** (-0.5))
        Wv = rn(3, (HID, VD), HID ** (-0.5))
        Wg = rn(4, (HID, VD), HID ** (-0.5))
        Wo = rn(5, (VD, HID), VD ** (-0.5))
        conv_q = rn(6, (KD, CS), 0.5)
        conv_k = rn(7, (KD, CS), 0.5)
        conv_v = rn(8, (VD, CS), 0.5)
        Wgk = rn(9, (HID, NH), HID ** (-0.5))
        Wb = rn(10, (HID, NH), HID ** (-0.5))
        b_b = rn(11, (NH,), 0.1)
        A = jax.random.uniform(ks[12], (NH,), jnp.float32, 0.5, 16.0)
        A_log = jnp.log(A)
        dt = jnp.exp(jax.random.uniform(ks[13], (NH,), jnp.float32) * (math.log(0.1) - math.log(0.001)) + math.log(0.001))
        dt = jnp.clip(dt, 0.0001, None)
        dt_bias = dt + jnp.log(-jnp.expm1(-dt))
        g_norm_weight = jnp.ones((DV,), jnp.float32)
        return dict(hidden_states=hidden_states, Wq=Wq, Wk=Wk, Wv=Wv, Wg=Wg, Wo=Wo, conv_q=conv_q, conv_k=conv_k, conv_v=conv_v, Wgk=Wgk, Wb=Wb, b_b=b_b, A_log=A_log, dt_bias=dt_bias, g_norm_weight=g_norm_weight)
    _L1_attn_in = _L1_attn_setup()

    def _L1_ffn_setup():
        import jax, jax.numpy as jnp
        import numpy as np
        NUM_EXPERTS = 8
        TOP_K = 2
        key = jax.random.key(seed)
        ks = jax.random.split(key, 4)
        B, S, H, F = (4, 512, 128, 512)
        x = jax.random.normal(ks[0], (B, S, H), dtype=jnp.float32)
        router_w = jax.random.normal(ks[1], (H, NUM_EXPERTS), dtype=jnp.float32) * 0.02
        w1 = jax.random.normal(ks[2], (H, F), dtype=jnp.float32) * 0.02
        b1 = jnp.zeros((F,), dtype=jnp.float32)
        w2 = jax.random.normal(ks[3], (F, H), dtype=jnp.float32) * 0.02
        b2 = jnp.zeros((H,), dtype=jnp.float32)
        return {'x': x, 'router_w': router_w, 'w1': w1, 'b1': b1, 'w2': w2, 'b2': b2}
    _L1_ffn_in = _L1_ffn_setup()
    _L1_c = _w((lambda *s: np.random.randn(*s).astype(np.float32) * 0.05)(8, 128))
    _L1_wmod = _w((lambda *s: np.random.randn(*s).astype(np.float32) * 0.05)(128, 6 * 128) * 128 ** (-0.5))
    _d = {'L0_attn_x': _L0_attn_in['x'], 'L0_attn_w_qkv': _L0_attn_in['w_qkv'], 'L0_attn_b_qkv': _L0_attn_in['b_qkv'], 'L0_attn_w_proj': _L0_attn_in['w_proj'], 'L0_attn_b_proj': _L0_attn_in['b_proj'], 'L0_ffn_W1': _L0_ffn_in['W1'], 'L0_ffn_b1': _L0_ffn_in['b1'], 'L0_ffn_W2': _L0_ffn_in['W2'], 'L0_ffn_b2': _L0_ffn_in['b2'], 'L0_ffn_Wg': _L0_ffn_in['Wg'], 'L0_ffn_bg': _L0_ffn_in['bg'], 'L0_c': _L0_c, 'L0_wmod': _L0_wmod, 'L1_attn_Wq': _L1_attn_in['Wq'], 'L1_attn_Wk': _L1_attn_in['Wk'], 'L1_attn_Wv': _L1_attn_in['Wv'], 'L1_attn_Wg': _L1_attn_in['Wg'], 'L1_attn_Wo': _L1_attn_in['Wo'], 'L1_attn_conv_q': _L1_attn_in['conv_q'], 'L1_attn_conv_k': _L1_attn_in['conv_k'], 'L1_attn_conv_v': _L1_attn_in['conv_v'], 'L1_attn_Wgk': _L1_attn_in['Wgk'], 'L1_attn_Wb': _L1_attn_in['Wb'], 'L1_attn_b_b': _L1_attn_in['b_b'], 'L1_attn_A_log': _L1_attn_in['A_log'], 'L1_attn_dt_bias': _L1_attn_in['dt_bias'], 'L1_attn_g_norm_weight': _L1_attn_in['g_norm_weight'], 'L1_ffn_router_w': _L1_ffn_in['router_w'], 'L1_ffn_w1': _L1_ffn_in['w1'], 'L1_ffn_b1': _L1_ffn_in['b1'], 'L1_ffn_w2': _L1_ffn_in['w2'], 'L1_ffn_b2': _L1_ffn_in['b2'], 'L1_c': _L1_c, 'L1_wmod': _L1_wmod}
    _x0 = _d['L0_attn_x']
    _d['L0_attn_x'] = jax.random.normal(jax.random.fold_in(jax.random.key(seed), 1), (8, 512, 128), dtype=_x0.dtype)
    del _x0
    return _d

def reference(L0_attn_x, L0_attn_w_qkv, L0_attn_b_qkv, L0_attn_w_proj, L0_attn_b_proj, L0_ffn_W1, L0_ffn_b1, L0_ffn_W2, L0_ffn_b2, L0_ffn_Wg, L0_ffn_bg, L0_c, L0_wmod, L1_attn_Wq, L1_attn_Wk, L1_attn_Wv, L1_attn_Wg, L1_attn_Wo, L1_attn_conv_q, L1_attn_conv_k, L1_attn_conv_v, L1_attn_Wgk, L1_attn_Wb, L1_attn_b_b, L1_attn_A_log, L1_attn_dt_bias, L1_attn_g_norm_weight, L1_ffn_router_w, L1_ffn_w1, L1_ffn_b1, L1_ffn_w2, L1_ffn_b2, L1_c, L1_wmod):

    def _L0_attn_ref(x, w_qkv, b_qkv, w_proj, b_proj):
        import jax, jax.numpy as jnp
        import numpy as np
        D_MODEL = 128
        N_HEADS = 16
        HEAD_DIM = D_MODEL // N_HEADS
        B, T, C = x.shape
        H, Dh = (N_HEADS, HEAD_DIM)
        qkv = x @ w_qkv + b_qkv
        qkv = qkv.reshape(B, T, 3, H, Dh)
        q = qkv[:, :, 0].transpose(0, 2, 1, 3)
        k = qkv[:, :, 1].transpose(0, 2, 1, 3)
        v = qkv[:, :, 2].transpose(0, 2, 1, 3)
        att = jnp.einsum('bhqd,bhkd->bhqk', q, k) / jnp.sqrt(jnp.float32(Dh))
        causal = jnp.tril(jnp.ones((T, T), dtype=bool))
        att = jnp.where(causal[None, None], att, -jnp.inf)
        att = jax.nn.softmax(att, axis=-1)
        y = jnp.einsum('bhqk,bhkd->bhqd', att, v)
        y = y.transpose(0, 2, 1, 3).reshape(B, T, C)
        return y @ w_proj + b_proj

    def _L0_ffn_ref(x, W1, b1, W2, b2, Wg, bg):
        import jax, jax.numpy as jnp
        import numpy as np
        B, S, D, H, E, K = (4, 128, 128, 256, 8, 2)
        b, s, d = x.shape
        xt = x.reshape(-1, d)
        gate_logits = xt @ Wg.T + bg
        w, idx = jax.lax.top_k(gate_logits, K)
        w = jax.nn.softmax(w, axis=1)
        h = jax.nn.relu(jnp.einsum('td,ehd->eth', xt, W1) + b1[:, None, :])
        y = jnp.einsum('eth,eoh->eto', h, W2) + b2[:, None, :]
        comb = (jax.nn.one_hot(idx, E, dtype=xt.dtype) * w[..., None]).sum(axis=1)
        out = jnp.einsum('eto,te->to', y, comb)
        return out.reshape(b, s, d)

    def _L1_attn_ref(hidden_states, Wq, Wk, Wv, Wg, Wo, conv_q, conv_k, conv_v, Wgk, Wb, b_b, A_log, dt_bias, g_norm_weight):
        import jax, jax.numpy as jnp
        import numpy as np
        import math
        B, L, HID = (2, 512, 128)
        NH, DK, DV = (12, 64, 128)
        KD, VD, CS = (NH * DK, NH * DV, 4)
        SCALE = DK ** (-0.5)

        def _causal_depthwise_conv(x, w):
            c, k = w.shape
            xt = jnp.transpose(x, (0, 2, 1))
            out = jax.lax.conv_general_dilated(xt, w[:, None, :], window_strides=(1,), padding=[(k - 1, 0)], feature_group_count=c, dimension_numbers=('NCH', 'OIH', 'NCH'))
            return jnp.transpose(out, (0, 2, 1))

        def _l2norm(x, eps=1e-06):
            return x * jax.lax.rsqrt(jnp.sum(x * x, axis=-1, keepdims=True) + eps)

        def _gated_delta_net(hidden_states, Wq, Wk, Wv, Wg, Wo, conv_q, conv_k, conv_v, Wgk, Wb, b_b, A_log, dt_bias, g_norm_weight):
            b, l, _ = hidden_states.shape
            q = jax.nn.silu(_causal_depthwise_conv(hidden_states @ Wq, conv_q))
            k = jax.nn.silu(_causal_depthwise_conv(hidden_states @ Wk, conv_k))
            v = jax.nn.silu(_causal_depthwise_conv(hidden_states @ Wv, conv_v))
            gk = -jnp.exp(A_log) * jax.nn.softplus(hidden_states @ Wgk + dt_bias)
            beta = jax.nn.sigmoid(hidden_states @ Wb + b_b)
            q = jnp.transpose(q.reshape(b, l, NH, DK), (0, 2, 1, 3))
            k = jnp.transpose(k.reshape(b, l, NH, DK), (0, 2, 1, 3))
            v = jnp.transpose(v.reshape(b, l, NH, DV), (0, 2, 1, 3))
            q = _l2norm(q) * SCALE
            k = _l2norm(k)
            qs = jnp.moveaxis(q, 2, 0)
            ks_ = jnp.moveaxis(k, 2, 0)
            vs = jnp.moveaxis(v, 2, 0)
            bs = jnp.moveaxis(beta, 1, 0)
            gs = jnp.moveaxis(gk, 1, 0)

            def step(S, inp):
                qt, kt, vt, bt, gt = inp
                S = S * jnp.exp(gt)[..., None, None]
                kv = jnp.einsum('bhk,bhkv->bhv', kt, S)
                delta = (vt - kv) * bt[..., None]
                S = S + jnp.einsum('bhk,bhv->bhkv', kt, delta)
                ot = jnp.einsum('bhk,bhkv->bhv', qt, S)
                return (S, ot)
            S0 = jnp.zeros((b, NH, DK, DV), hidden_states.dtype)
            _, os_ = jax.lax.scan(step, S0, (qs, ks_, vs, bs, gs))
            o = jnp.moveaxis(os_, 0, 1)
            g = (hidden_states @ Wg).reshape(b, l, NH, DV)
            var = jnp.mean(o * o, axis=-1, keepdims=True)
            o = o * jax.lax.rsqrt(var + 1e-05) * g_norm_weight
            o = o * g * jax.nn.sigmoid(g)
            return o.reshape(b, l, VD) @ Wo
        return _gated_delta_net(hidden_states, Wq, Wk, Wv, Wg, Wo, conv_q, conv_k, conv_v, Wgk, Wb, b_b, A_log, dt_bias, g_norm_weight)

    def _L1_ffn_ref(x, router_w, w1, b1, w2, b2):
        import jax, jax.numpy as jnp
        import numpy as np
        NUM_EXPERTS = 8
        TOP_K = 2
        B, S, H = x.shape
        xt = x.reshape(-1, H)
        router_logits = jnp.matmul(xt, router_w)
        router_probs = jax.nn.softmax(router_logits, axis=-1)
        top_k_probs, top_k_indices = jax.lax.top_k(router_probs, TOP_K)
        top_k_probs = top_k_probs / jnp.sum(top_k_probs, axis=-1, keepdims=True)
        one_hot = jax.nn.one_hot(top_k_indices, NUM_EXPERTS, dtype=xt.dtype)
        combine = jnp.einsum('tk,tke->te', top_k_probs, one_hot)
        expert_out = jnp.matmul(jax.nn.gelu(jnp.matmul(xt, w1) + b1), w2) + b2
        out = expert_out * jnp.sum(combine, axis=-1, keepdims=True)
        return out.reshape(B, S, H)
    x = L0_attn_x
    mod = (_silu(L0_c) @ L0_wmod).reshape(L0_c.shape[0], 6, 1, -1)
    sa, ca, ga, sb, cb, gb = (mod[:, 0], mod[:, 1], mod[:, 2], mod[:, 3], mod[:, 4], mod[:, 5])
    ga = (2 * (ga >= 0) - 1) * jnp.maximum(jnp.abs(ga), 0.25)
    gb = (2 * (gb >= 0) - 1) * jnp.maximum(jnp.abs(gb), 0.25)
    h = _layernorm(x, axis=-1) * (1 + ca) + sa
    x = x + ga * _L0_attn_ref(h, L0_attn_w_qkv, L0_attn_b_qkv, L0_attn_w_proj, L0_attn_b_proj)
    h = _layernorm(x, axis=-1) * (1 + cb) + sb
    x = x + gb * _L0_ffn_ref(h, L0_ffn_W1, L0_ffn_b1, L0_ffn_W2, L0_ffn_b2, L0_ffn_Wg, L0_ffn_bg)
    mod = (_silu(L1_c) @ L1_wmod).reshape(L1_c.shape[0], 6, 1, -1)
    sa, ca, ga, sb, cb, gb = (mod[:, 0], mod[:, 1], mod[:, 2], mod[:, 3], mod[:, 4], mod[:, 5])
    ga = (2 * (ga >= 0) - 1) * jnp.maximum(jnp.abs(ga), 0.25)
    gb = (2 * (gb >= 0) - 1) * jnp.maximum(jnp.abs(gb), 0.25)
    h = _layernorm(x, axis=-1) * (1 + ca) + sa
    x = x + ga * _L1_attn_ref(h, L1_attn_Wq, L1_attn_Wk, L1_attn_Wv, L1_attn_Wg, L1_attn_Wo, L1_attn_conv_q, L1_attn_conv_k, L1_attn_conv_v, L1_attn_Wgk, L1_attn_Wb, L1_attn_b_b, L1_attn_A_log, L1_attn_dt_bias, L1_attn_g_norm_weight)
    h = _layernorm(x, axis=-1) * (1 + cb) + sb
    x = x + gb * _L1_ffn_ref(h, L1_ffn_router_w, L1_ffn_w1, L1_ffn_b1, L1_ffn_w2, L1_ffn_b2)
    return x

_drawn_inputs = setup_inputs


def setup_inputs(seed=0):
    import zlib

    import numpy as np

    out = dict(_drawn_inputs(seed))
    spreads = {'L0_attn_b_qkv': (0.0, 0.297),
     'L0_attn_b_proj': (0.0, 0.304),
     'L0_ffn_b1': (0.0, 0.8),
     'L0_ffn_b2': (0.0, 0.445),
     'L0_ffn_bg': (0.0, 0.69),
     'L1_attn_g_norm_weight': (1.0, 0.567),
     'L1_ffn_b1': (0.0, 0.8),
     'L1_ffn_b2': (0.0, 0.304)}
    factors = {'L0_ffn_W1': 7.022,
     'L0_ffn_W2': 5.349,
     'L0_ffn_Wg': 3.248,
     'L1_attn_b_b': 31.201,
     'L1_ffn_router_w': 64.0,
     'L1_ffn_w1': 4.278,
     'L1_ffn_w2': 3.919}
    for name, (base, spread) in spreads.items():
        noise = np.random.default_rng([zlib.crc32(name.encode()), seed]).standard_normal(out[name].shape)
        drawn = base * np.exp(spread * noise) if base else spread * noise
        out[name] = jnp.asarray(drawn.astype(out[name].dtype))
    for name, factor in factors.items():
        out[name] = (out[name] * factor).astype(out[name].dtype)
    return out
```

```python
from contextlib import ExitStack

import concourse.bass as bass
from concourse import mybir

F32 = mybir.dt.float32
BF16 = mybir.dt.bfloat16
U32 = mybir.dt.uint32
ALU = mybir.AluOpType
ACT = mybir.ActivationFunctionType
AX = mybir.AxisListType

P = 128
MASKED = -1.0e30
EXP_LN = "natural_log_exp_and_others"

IN_ROW = {
    "x_in": 16, "w_in": 32, "wc_in": 48, "gates_in": 16, "v_pads": 1, "xin_free": 1, "x_done": 1, "out_sent": 16,
    "ln_var": 4, "ln_rstd": 4, "ln_xn": 4, "ln_ps": 4, "h_ready": 4, "dve_step": 243, "act_step": 13, "pool_step": 0,
    "qk_ps": 2, "qk_f": 2, "qk_parts": 2, "v_ps": 1, "v_ready": 1, "parts_out": 32, "stacks_in": 304, "s_ps": 64,
    "s_max": 64, "m_parts": 2, "m_ps": 2, "m_sb": 2, "m_out": 32, "m_in_0": 16, "m_in_1": 16, "st_ps": 48,
    "p_ready": 48, "pv_ps": 16, "y_sb": 4, "yt_ps": 4, "y_norm": 4, "y2_ps": 1, "y2_sb": 1, "proj_ps": 1, "lg_ps": 1,
    "top_d": 1, "top_e": 1, "comb_ready": 1, "ct_ps": 1, "ct_sb": 1, "b2_ps": 1, "hid_ps": 16, "hid_sb": 16,
    "moe_ps": 8, "moe_acc": 8, "gb_ps": 1, "gb_z": 1, "gb_e": 1, "gk_ready": 1, "z_ps": 24, "tap0": 24, "taps": 24,
    "qkv_t": 24, "vt_ps": 12, "v_tok": 12, "gm_ready": 4, "small_ps": 4, "kt_ps": 8, "qt_ps": 8, "dec_ready": 4,
    "k_sq": 8, "q_sq": 8, "ss_ready": 4, "rn_ready": 4, "khat_ready": 4, "kd_ready": 4, "lower_ps": 16, "l_ps": 12,
    "dt_ready": 12, "kh_ps": 8, "kh_ready": 8, "g_ps": 12, "gd_ready": 12, "qk2_ps": 12, "pt_ready": 12,
    "bm_ready": 12, "b_out": 512, "b_in": 64, "t_ready": 4, "t_out": 128, "t_in": 1024, "lv_ps": 96, "lv_16": 36,
    "lv_sb": 60, "ks_ps": 12, "r_ready": 12, "qs_ps": 12, "qse_ready": 12, "yd_ps": 12, "dl_ready": 12, "pd_ps": 12,
    "o_ready": 12, "su_ps": 6, "sd_ready": 3, "s_ready": 7, "gt_ps": 12, "gate_ready": 12, "osq_ready": 4,
    "ot_ready": 4, "of_ready": 4, "on_ready": 4, "og_ready": 4, "og_ps": 12, "ogt_ready": 12, "wo_ps": 4,
    "wo_done": 4, "rt_ps": 1, "rt_d": 1, "rt_e": 1, "rt_ready": 1, "f_ps": 4, "f_sb": 4, "f2_ps": 1,
}


def at(b, signal, k):
    return b * IN_ROW[signal.name] + k


def wide(ap, shape):
    return ap.unsqueeze(len(ap.shape)).to_broadcast(shape)


def adaln_two_layers(nc, L0_attn_x, L0_attn_w_qkv, L0_attn_b_qkv, L0_attn_w_proj, L0_attn_b_proj, L0_ffn_W1, L0_ffn_b1,
                     L0_ffn_W2, L0_ffn_b2, L0_ffn_Wg, L0_ffn_bg, L0_c, L0_wmod, L1_attn_Wq, L1_attn_Wk, L1_attn_Wv,
                     L1_attn_Wg, L1_attn_Wo, L1_attn_conv_q, L1_attn_conv_k, L1_attn_conv_v, L1_attn_Wgk, L1_attn_Wb,
                     L1_attn_b_b, L1_attn_A_log, L1_attn_dt_bias, L1_attn_g_norm_weight, L1_ffn_router_w, L1_ffn_w1,
                     L1_ffn_b1, L1_ffn_w2, L1_ffn_b2, L1_c, L1_wmod, out):
    NB, T, D = L0_attn_x.shape
    NT = T // P
    HA, DA = 16, 8
    SA = DA ** -0.5
    PARTS = 3
    KS = PARTS * PARTS * DA
    NE, HID = L0_ffn_W1.shape[:2]
    HT = HID // P
    HD, DK, DV = 12, 64, 128
    NP = HD // 2
    NG, GH = 3, 4
    HS = [slice(0, 8, 2), slice(1, 8, 2), slice(8, 12)]
    BEFORE = [2, 2, 3]
    NQK, NCV = 2 * NP, 2 * NP + HD
    FT = L1_ffn_w1.shape[1] // P
    BS = 16
    NBK = P // BS

    with ExitStack() as ctx:
        def sb(name, shape, dt=F32):
            return ctx.enter_context(nc.sbuf_tensor(name, shape, dt))

        def dram(name, shape, dt=F32):
            return nc.dram_tensor(name, shape, dt).ap()

        PS = [ctx.enter_context(nc.psum_tensor(f"bank{i}", [P, 512], F32)) for i in range(8)]

        def sig(name):
            return ctx.enter_context(nc.semaphore(name))

        ident = sb("ident", [P, P])
        ident_bf = sb("ident_bf", [P, P], BF16)
        ones = sb("ones", [P, P])
        later = sb("later", [P, P])
        upto = sb("upto", [P, P])
        mask16 = sb("mask16", [P, P])
        mask_q = sb("mask_q", [P, P], BF16)
        mask_k = sb("mask_k", [P, GH, P], BF16)
        eye16 = sb("eye16", [NBK * HD, BS * BS])
        iota8 = sb("iota8", [P, NE])
        v_pad = sb("v_pad", [P, 32 - DA])
        eps5 = sb("eps5", [P, 1])
        eps6 = sb("eps6", [P, 1])
        wqkv = sb("wqkv", [P, 3 * D])
        wproj = sb("wproj", [P, D])
        wo = sb("wo", [P, HD, D])
        wgate = sb("wgate", [P, HD * DV])
        w1 = sb("w1", [P, FT * P])
        w2 = sb("w2", [P, FT, D])
        wgb = sb("wgb", [P, 2 * HD])
        router0 = sb("router0", [P, NE])
        router1 = sb("router1", [P, NE])
        conv = sb("conv", [P, NCV, 4])
        bqk = sb("bqk", [P, 2])
        bv = sb("bv", [P, D])
        dt_bias = sb("dt_bias", [P, HD])
        neg_a = sb("neg_a", [P, HD])
        beta_bias = sb("beta_bias", [P, HD])
        gnorm = sb("gnorm", [P, 1])
        b1e = sb("b1e", [P, NE * HT])
        b2e = sb("b2e", [NE, D])
        b1f = sb("b1f", [P, FT])
        rows1 = sb("rows1", [1, 2 * D + NE])
        bproj, b2f, bgate = rows1[0:1, 0:D], rows1[0:1, D:2 * D], rows1[0:1, 2 * D:2 * D + NE]
        mod_t = sb("mod_t", [P, 8, NB])
        mod_b = sb("mod_b", [P, 8])
        xin = sb("xin", [P, NT, D])
        xs = sb("xs", [P, NT, D])
        xn = sb("xn", [P, NT, D])
        h_t = sb("h_t", [P, T])
        gates = sb("gates", [P, 4, D])
        st = sb("st", [P, NT, 6])
        mv = sb("mv", [P, 3, NT])
        rstd = sb("rstd", [P, NT])
        small = sb("small", [P, 512])

        vq = sb("vq", [P, NQK * T + NT * HD * DV])
        qk_t = vq[:, 0:NQK * T].rearrange("p (n t) -> p n t", t=T)
        v_all = vq[:, NQK * T:].rearrange("p (c h v) -> p c h v", c=NT, h=HD)
        half = HA * T // 2
        q_stack = vq[:, 0:half].bitcast(BF16).rearrange("p (h t) -> p h t", h=HA)
        k_stack = vq[:, half:2 * half].bitcast(BF16).rearrange("p (h t) -> p h t", h=HA)
        v32 = vq[:, 2 * half:2 * half + NT * HA * 32].rearrange("p (c h d) -> p c h d", c=NT, h=HA)
        o = 2 * half + NT * HA * 32
        y32 = vq[:, o:o + 4 * T].rearrange("p (g t) -> p g t", g=4)

        HW = HD * P
        arena = sb("arena", [P, 14 * HW])
        used = [0]

        def carve(n):
            used[0] += n
            return arena[:, used[0] - n:used[0]]

        def heads(ap, w=P):
            return ap.rearrange("p (h w) -> p h w", w=w)

        kd_a, kht_a, pt_a = carve(HW), carve(HW), carve(2 * HW)
        dec_a, bm_a, ub_a, t_a, x_a, rb_a, qse_a, dl_a, ob_a = [carve(HW) for _ in range(9)]
        khat_a, sd_a = carve(HW // 2), carve(HW // 2)
        kd = kd_a.rearrange("p (i h d) -> p i h d", i=2, h=HD)
        kh_t = kht_a.rearrange("p (i n t) -> p i n t", i=2, n=NP)
        pt = pt_a.rearrange("p (i h w) -> p i h w", i=2, h=HD)
        dt, bm, ub, tw, xw = heads(dec_a), heads(bm_a), heads(ub_a), heads(t_a), heads(x_a)
        gm = ub
        rb, qse, dl, ob = heads(rb_a), heads(qse_a), heads(dl_a), heads(ob_a)
        osq, ogt, og = rb, qse, dl
        khat = khat_a
        sdec = sd_a.rearrange("p (n v) -> p n v", n=NP)
        ktok = sd_a
        ksq, qsq = dl_a[:, 0:HW // 2], dl_a[:, HW // 2:HW]
        state = sb("state", [P, NP, DV])
        t16 = sb("t16", [P, HD, P])
        x16 = sb("x16", [P, HD, P])
        u32 = sb("u32", [P, HD, P])
        u64 = sb("u64", [P, HD, DK])
        gate = tw
        bm2 = sb("bm2", [P, HD, P])
        bms = [bm, bm2]
        blk = sb("blk", [NBK * HD, BS * BS])
        blk_t = sb("blk_t", [NBK * HD, BS * BS])
        blk_x = sb("blk_x", [NBK * HD, BS * BS])
        blk_tmp = small
        gk = sb("gk", [P, NT, HD])
        beta = sb("beta", [P, NT, HD])
        dec = sb("dec", [P, NT, 2, HD])
        neg_dec = sb("neg_dec", [P, NT, HD])
        dec_end = sb("dec_end", [P, NT, NP])
        ssq = sb("ssq", [P, NT, 2 * HD])
        rn = sb("rn", [P, NT, 2 * HD])
        fac = sb("fac", [P, 3, HD])
        acc = arena[:, 8 * HW:8 * HW + 4 * T].rearrange("p (i t) -> p i t", i=4)
        v_t = arena[:, 8 * HW + 4 * T:8 * HW + 8 * T].rearrange("p (i t) -> p i t", i=4)
        wconv = arena[:, 6 * HW:8 * HW]
        assert NCV * P <= 2 * HW
        w1t = arena[:, 8 * HW:8 * HW + NE * HT * P].rearrange("p (n m) -> p n m", m=P)
        w2t = arena[:, 8 * HW + NE * HT * P:8 * HW + 2 * NE * HT * P].rearrange("p (n m) -> p n m", m=P)
        o = 8 * HW + 2 * NE * HT * P
        hid = arena[:, o:o + 2 * HT * T].rearrange("p (i j t) -> p i j t", i=2, j=HT)
        o += 2 * HT * T
        moe = arena[:, o:o + T].rearrange("p (c d) -> p c d", c=NT)
        o += T
        p_t = arena[:, 0:2 * 10 * P].rearrange("p (i w) -> p i w", i=2)
        qkf = arena[:, 2560:2560 + 2 * T].rearrange("p (i t) -> p i t", i=2)
        rest = arena[:, 3584:3584 + T]
        qkp = arena[:, 4096:4096 + PARTS * T].bitcast(BF16).rearrange("p (i n t) -> p i n t", i=2, n=PARTS)
        y_tok = arena[:, 5632:5632 + T].rearrange("p (c d) -> p c d", c=NT)
        y_t = arena[:, 6144:6144 + T]
        wide_t = arena[:, 6656:6656 + T].rearrange("p (c d) -> p c d", c=NT)
        hid1 = arena[:, 0:FT * T].rearrange("p (j t) -> p j t", j=FT)
        mx = sb("mx", [P, HA, NT])
        mrest = sb("mrest", [P, HA // 2 * NT])
        mparts = sb("mparts", [P, PARTS, HA // 2 * NT], BF16)
        m_t = sb("m_t", [PARTS * HA // 2 * NT, P], BF16)
        rec = sb("rec", [P, HA])
        lnv = sb("lnv", [P, NT])
        comb = sb("comb", [P, NT, NE])
        comb_t = arena[0:NE, o:o + T]
        idx = sb("idx", [P, NT, 8], U32)

        qk_bounce = dram("qk_bounce", [2, HA, DA, PARTS, T], BF16)
        m_bounce = dram("m_bounce", [2, PARTS, HA // 2 * T], BF16)
        b_bounce = dram("b_bounce", [NBK, HD, BS, BS])
        t_bounce = dram("t_bounce", [2, NBK, HD, BS, BS])
        w1_bounce = dram("w1_bounce", [P, NE * HT * P])
        w2_bounce = dram("w2_bounce", [P, NE * HT * P])
        gate_rows = dram("gate_rows", [NB, 4 * D])
        one_rows = dram("one_rows", [PARTS, HA * T], BF16)

        consts_in, masks_made, zeros_made, silu_c, prologue_ps, prologue_sb, rows_out, weights_out = [
            ctx.enter_context(nc.semaphore(n)) for n in
            ("consts_in", "masks_made", "zeros_made", "silu_c", "prologue_ps", "prologue_sb", "rows_out", "weights_out")]
        pool_pro, dve_pro, act_pro = [ctx.enter_context(nc.semaphore(n)) for n in ("pool_pro", "dve_pro", "act_pro")]

        x_in, w_in, wc_in, gates_in = sig("x_in"), sig("w_in"), sig("wc_in"), sig("gates_in")
        v_pads = sig("v_pads")
        xin_free, x_done, out_sent = sig("xin_free"), sig("x_done"), sig("out_sent")
        ln_var, ln_rstd, ln_xn, ln_ps, h_ready = [sig(n) for n in ("ln_var", "ln_rstd", "ln_xn", "ln_ps", "h_ready")]
        dve_step, act_step = sig("dve_step"), sig("act_step")
        qk_ps, qk_f, qk_parts, v_ps, v_ready, parts_out, stacks_in = [sig(n) for n in (
            "qk_ps", "qk_f", "qk_parts", "v_ps", "v_ready", "parts_out", "stacks_in")]
        s_ps, s_max, m_parts, m_ps, m_sb, m_out = [sig(n) for n in (
            "s_ps", "s_max", "m_parts", "m_ps", "m_sb", "m_out")]
        m_in = [sig("m_in_0"), sig("m_in_1")]
        st_ps, p_ready, pv_ps, y_sb, yt_ps, y_norm, y2_ps, y2_sb, proj_ps = [sig(n) for n in (
            "st_ps", "p_ready", "pv_ps", "y_sb", "yt_ps", "y_norm", "y2_ps", "y2_sb", "proj_ps")]
        lg_ps, top_d, top_e, comb_ready, ct_ps, ct_sb, b2_ps, hid_ps, hid_sb, moe_ps, moe_acc = [sig(n) for n in (
            "lg_ps", "top_d", "top_e", "comb_ready", "ct_ps", "ct_sb", "b2_ps", "hid_ps", "hid_sb", "moe_ps", "moe_acc")]
        gb_ps, gb_z, gb_e, gk_ready = [sig(n) for n in ("gb_ps", "gb_z", "gb_e", "gk_ready")]
        z_ps, tap0, taps, qkv_t, vt_ps, v_tok = [sig(n) for n in ("z_ps", "tap0", "taps", "qkv_t", "vt_ps", "v_tok")]
        gm_ready, small_ps, kt_ps, qt_ps, dec_ready, k_sq, q_sq, ss_ready, rn_ready, khat_ready, kd_ready = [
            sig(n) for n in ("gm_ready", "small_ps", "kt_ps", "qt_ps", "dec_ready", "k_sq", "q_sq", "ss_ready",
                             "rn_ready", "khat_ready", "kd_ready")]
        lower_ps = sig("lower_ps")
        l_ps, dt_ready, kh_ps, kh_ready, g_ps, gd_ready, qk2_ps, pt_ready, bm_ready = [sig(n) for n in (
            "l_ps", "dt_ready", "kh_ps", "kh_ready", "g_ps", "gd_ready", "qk2_ps", "pt_ready", "bm_ready")]
        b_out, b_in, t_ready, t_out, t_in = [sig(n) for n in ("b_out", "b_in", "t_ready", "t_out", "t_in")]
        lv_ps, lv_16, lv_sb = [sig(n) for n in ("lv_ps", "lv_16", "lv_sb")]
        ks_ps, r_ready, qs_ps, qse_ready, yd_ps, dl_ready, pd_ps, o_ready, su_ps, sd_ready, s_ready = [sig(n) for n in (
            "ks_ps", "r_ready", "qs_ps", "qse_ready", "yd_ps", "dl_ready", "pd_ps", "o_ready", "su_ps", "sd_ready", "s_ready")]
        gt_ps, gate_ready, osq_ready, ot_ready, of_ready, on_ready, og_ready, og_ps, ogt_ready, wo_ps, wo_done = [
            sig(n) for n in ("gt_ps", "gate_ready", "osq_ready", "ot_ready", "of_ready", "on_ready", "og_ready", "og_ps",
                             "ogt_ready", "wo_ps", "wo_done")]
        rt_ps, rt_d, rt_e, rt_ready, f_ps, f_sb, f2_ps = [sig(n) for n in (
            "rt_ps", "rt_d", "rt_e", "rt_ready", "f_ps", "f_sb", "f2_ps")]

        ln_bank = PS[0]
        qk_banks, v_bank = PS[1:3], PS[3]
        yt_banks, y2_bank, proj_bank = PS[0:4], PS[4], PS[5]
        max_banks = [PS[7], PS[6]]

        def score_bank(n):
            return PS[n % 6 if n < 32 else n % 3]

        def score_t_bank(h, i):
            return PS[3 + i if h < 8 or h % 2 else i]

        def y_bank(g):
            return PS[6 + g % 2]

        logit_bank, comb_bank, b2_bank = PS[1], PS[0], PS[1]

        def hid_bank(n):
            return PS[2 + n % 4]

        def moe_bank(e):
            return PS[6 + e % 2]

        gb_bank = PS[1]

        def z_bank(n):
            return PS[2 + n % 4]

        def vt_bank(i):
            return PS[6 + i % 2]

        dec_bank, k_banks, q_banks, l_banks = PS[5], PS[6:8], PS[0:2], PS[2:5]
        low_banks, high_banks, ks_banks = PS[0:3], PS[3:6], PS[5:8]
        gate_banks, og_banks, wo_bank = PS[2:5], [PS[6], PS[7], PS[0]], PS[1]

        def level_bank(s, g):
            return PS[s % 2 * 3 + g]

        def f_bank(j):
            return PS[2 + j]

        f2_bank = PS[6]

        stages = [("conv", 0), ("norm", 0), ("conv", 1), ("gram", 0), ("conv", 2), ("subst", 0), ("conv", 3), ("norm", 1), ("gram", 1)]
        for c in range(NT):
            stages.append(("levels", c))
            if c:
                stages += [("rms", c - 1), ("gate", c - 1)]
            if c + 1 < NT:
                stages.append(("subst", c + 1))
            if c + 2 < NT:
                stages.append(("norm", c + 2))
            if c:
                stages += [("scale", c - 1), ("project", c - 1)]
            stages.append(("scan", c))
            if c + 2 < NT:
                stages.append(("gram", c + 2))
        stages += [("rms", NT - 1), ("gate", NT - 1), ("scale", NT - 1), ("project", NT - 1)]
        conv_tiles = [range(0, NQK + 2), range(NQK + 2, NQK + 6), range(NQK + 6, NQK + 10), range(NQK + 10, NCV)]
        V_LAG = 3

        const_loads = [
            (wqkv[:, :], L0_attn_w_qkv), (wproj[:, :], L0_attn_w_proj),
            (wo[:, :, :], L1_attn_Wo.rearrange("(h v) n -> v h n", h=HD)), (wgate[:, :], L1_attn_Wg),
            (w1[:, :], L1_ffn_w1), (w2[:, :, :], L1_ffn_w2.rearrange("(j p) n -> p j n", p=P)),
            (wgb[:, 0:HD], L1_attn_Wgk), (wgb[:, HD:2 * HD], L1_attn_Wb),
            (router0[:, :], L0_ffn_Wg.rearrange("e d -> d e")), (router1[:, :], L1_ffn_router_w),
            (conv[:, 0:NP, :], L1_attn_conv_q.rearrange("(n p) k -> p n k", p=P)),
            (conv[:, NP:NQK, :], L1_attn_conv_k.rearrange("(n p) k -> p n k", p=P)),
            (conv[:, NQK:NCV, :], L1_attn_conv_v.rearrange("(n p) k -> p n k", p=P)),
            (bqk[:, :], L0_attn_b_qkv[0:2 * D].rearrange("(s m) -> m s", s=2)),
            (bv[:, :], L0_attn_b_qkv[2 * D:3 * D].partition_broadcast(P)),
            (dt_bias[:, :], L1_attn_dt_bias.partition_broadcast(P)),
            (neg_a[:, :], L1_attn_A_log.partition_broadcast(P)),
            (beta_bias[:, :], L1_attn_b_b.partition_broadcast(P)),
            (gnorm[:, :], L1_attn_g_norm_weight.rearrange("(v a) -> v a", a=1)),
            (b1e[:, :].rearrange("p (e j) -> p e j", j=HT), L0_ffn_b1.rearrange("e (j p) -> p e j", p=P)),
            (b2e[:, :], L0_ffn_b2), (b1f[:, :], L1_ffn_b1.rearrange("(j p) -> p j", p=P)),
            (bproj, L0_attn_b_proj.rearrange("(a n) -> a n", a=1)), (b2f, L1_ffn_b2.rearrange("(a n) -> a n", a=1)),
            (bgate, L0_ffn_bg.rearrange("(a n) -> a n", a=1)),
        ]
        c_t = small[:, 0:2 * NB].rearrange("p (l b) -> p l b", l=2)
        w1raw = arena[:, 0:NE * HT * P].rearrange("p (n m) -> p n m", m=P)
        w2raw = arena[:, NE * HT * P:2 * NE * HT * P].rearrange("p (n m) -> p n m", m=P)
        wmod = arena[:, 2 * NE * HT * P:2 * NE * HT * P + 12 * D].rearrange("p (l j d) -> p l j d", l=2, j=6)
        g_rows = vq[0:NB, 0:4 * D]
        g_tmp = vq[0:NB, 4 * D:8 * D]
        const_loads += [
            (c_t[:, 0, :], L0_c.rearrange("b d -> d b")), (c_t[:, 1, :], L1_c.rearrange("b d -> d b")),
            (wmod[:, 0], L0_wmod.rearrange("p (j d) -> p j d", j=6)), (wmod[:, 1], L1_wmod.rearrange("p (j d) -> p j d", j=6)),
            (w1raw.rearrange("p (e j) d -> p e j d", j=HT), L0_ffn_W1.rearrange("e (j p) d -> p e j d", p=P)),
            (w2raw.rearrange("p (e j) m -> p e j m", j=HT), L0_ffn_W2.rearrange("e o (j m) -> o e j m", m=P)),
        ]
        CONSTS = 16 * len(const_loads)
        NW = NE * HT

        ctx.enter_context(nc.allow_non_contiguous_dma("small constants, and blocks that change partitions"))
        block = ctx.enter_context(nc.Block())

        @block.tensor
        def _(pe):
            mm, tr = nc.tensor.matmul, nc.tensor.transpose

            pe.wait_ge(consts_in, CONSTS)
            pe.wait_ge(silu_c, 1)
            pe.wait_ge(masks_made, 1)
            for i, (l, j) in enumerate([(l, j) for l in range(2) for j in (0, 1, 3, 4)]):
                mm(PS[0][:, i * NB:(i + 1) * NB], wmod[:, l, j, :], c_t[:, l, :], start=True, stop=True)
            for l in range(2):
                last = mm(PS[1][0:NB, l * 2 * D:(l + 1) * 2 * D].rearrange("b (j d) -> b j d", j=2), c_t[:, l, :],
                          wmod[:, l, 2::3, :], start=True, stop=True)
            last.then_inc(prologue_ps, 1)
            for i in range(2 * NW):
                n = i // 4
                if i % 4 == 0 and n >= 6:
                    pe.wait_ge(prologue_sb, n - 6 + 2)
                raw = w1raw if i < NW else w2raw
                last = tr(PS[2 + n % 6][:, i % 4 * P:(i % 4 + 1) * P], raw[:, i % NW, :], ident[:, :])
                if i % 4 == 3:
                    last.then_inc(prologue_ps, 1)
            pe.wait_ge(prologue_sb, 1 + 2 * NW // 4)

            with pe.Fori(0, NB) as b:
                lowers = [0]

                def lower():
                    lowers[0] += 1
                    return at(b, lower_ps, lowers[0])

                def layer_norm(k):
                    pe.wait_ge(ln_xn, at(b, ln_xn, k + 1))
                    ps = ln_bank
                    for t in range(NT):
                        last = tr(ps[:, t * P:(t + 1) * P], xn[:, t, :], ident[:, :])
                    last.then_inc(ln_ps, 1)
                    pe.wait_ge(h_ready, at(b, h_ready, k + 1))

                layer_norm(0)
                for i in range(2):
                    mm(qk_banks[i][:, :], wqkv[:, i * D:(i + 1) * D], h_t[:, :], start=True, stop=True).then_inc(qk_ps, 1)
                ps = v_bank
                for t in range(NT):
                    last = mm(ps[:, t * D:(t + 1) * D], h_t[:, t * P:(t + 1) * P], wqkv[:, 2 * D:3 * D], start=True, stop=True)
                last.then_inc(v_ps, 1)
                pe.wait_ge(stacks_in, at(b, stacks_in, 16 * (2 * PARTS * PARTS + 1)))
                pe.wait_ge(v_ready, at(b, v_ready, 1))

                def scores(h):
                    for t in range(NT):
                        n = h * NT + t
                        ps, e = score_bank(n), (t + 1) * P
                        if n >= 32:
                            pe.wait_ge(s_max, at(b, s_max, n - 2))
                        elif n >= 6:
                            pe.wait_ge(s_max, at(b, s_max, n - 5))
                        mm(ps[:, 0:e], q_stack[0:KS, h, t * P:e], k_stack[0:KS, h, 0:e], start=True, stop=False)
                        mm(ps[:, t * P:e], ident_bf[:, :], mask_q[:, :], start=False, stop=True).then_inc(s_ps, 1)

                def move_maxima(hh):
                    pe.wait_ge(m_parts, at(b, m_parts, hh + 1))
                    if hh:
                        pe.wait_ge(y_sb, at(b, y_sb, 1))
                    ps = max_banks[hh]
                    tr(ps[0:96, 0:P // 2].bitcast(BF16), mparts[:, :, :].rearrange("p n m -> p (n m)"), ident_bf[:, :]).then_inc(m_ps, 1)

                def scores_t(h):
                    if h % 8 == 0:
                        pe.wait_ge(m_in[h // 8], at(b, m_in[h // 8], 16))
                    lots = [[0], [1], [2, 3]]
                    for i, lot in enumerate(lots):
                        ps, c0 = score_t_bank(h, i), 0
                        if h >= 9:
                            pe.wait_ge(p_ready, at(b, p_ready, 3 * (h - 2) + i + 1))
                        elif 1 <= h < 8:
                            pe.wait_ge(p_ready, at(b, p_ready, 3 * (h - 1) + i + 1))
                        for j in lot:
                            n = T - j * P
                            mm(ps[:, c0:c0 + n], k_stack[0:KS + PARTS, h, j * P:(j + 1) * P], q_stack[0:KS + PARTS, h, j * P:T],
                               start=True, stop=False)
                            last = mm(ps[:, c0:c0 + P], ident_bf[:, :], mask_k[:, 0, :], start=False, stop=True)
                            c0 += n
                        last.then_inc(st_ps, 1)

                def weigh(h):
                    g, r = h // 4, 32 * (h % 4)
                    if h % 4 == 0 and g >= 2:
                        pe.wait_ge(y_sb, at(b, y_sb, g - 1))
                    pe.wait_ge(p_ready, at(b, p_ready, 3 * h + 3))
                    c0 = 0
                    for j in range(NT):
                        n = T - j * P
                        last = mm(y_bank(g)[r:r + 32, j * P:T], v32[:, j, h, :], p_t[:, h % 2, c0:c0 + n],
                                  start=(j == 0), stop=(j == NT - 1))
                        c0 += n
                    last.then_inc(pv_ps, 1)

                for h in range(8):
                    scores(h)
                move_maxima(0)
                for h in range(8, HA):
                    scores(h)
                    scores_t(h - 8)
                    if h > 8:
                        weigh(h - 9)
                move_maxima(1)
                for h in range(8, HA):
                    scores_t(h)
                    weigh(h - 1)
                weigh(HA - 1)
                pe.wait_ge(y_sb, at(b, y_sb, 4))
                for t in range(NT):
                    ps = yt_banks[t]
                    for g in range(4):
                        last = tr(ps[:, g * P:(g + 1) * P], y32[:, g, t * P:(t + 1) * P], ident[:, :])
                    last.then_inc(yt_ps, 1)
                ps = y2_bank
                for t in range(NT):
                    pe.wait_ge(y_norm, at(b, y_norm, t + 1))
                    last = tr(ps[:, t * P:(t + 1) * P], y_tok[:, t, :], ident[:, :])
                last.then_inc(y2_ps, 1)
                pe.wait_ge(y2_sb, at(b, y2_sb, 1))
                ps = proj_bank
                for t in range(NT):
                    mm(ps[:, t * D:(t + 1) * D], y_t[:, t * P:(t + 1) * P], wproj[:, :], start=True, stop=False)
                    last = mm(ps[:, t * D:(t + 1) * D], ones[0:1, :], bproj, start=False, stop=True)
                last.then_inc(proj_ps, 1)

                layer_norm(1)
                ps = logit_bank
                for t in range(NT):
                    mm(ps[:, t * NE:(t + 1) * NE], h_t[:, t * P:(t + 1) * P], router0[:, :], start=True, stop=False)
                    last = mm(ps[:, t * NE:(t + 1) * NE], ones[0:1, :], bgate, start=False, stop=True)
                last.then_inc(lg_ps, 1)
                pe.wait_ge(w_in, at(b, w_in, 32))

                def expert_in(e):
                    for j in range(HT):
                        n = e * HT + j
                        ps = hid_bank(n)
                        if n >= 4:
                            pe.wait_ge(hid_sb, at(b, hid_sb, n - 3))
                        mm(ps[:, :], w1t[:, n, :], h_t[:, :], start=True, stop=True).then_inc(hid_ps, 1)

                def expert_out(e):
                    pe.wait_ge(hid_sb, at(b, hid_sb, HT * (e + 1)))
                    ps = moe_bank(e)
                    if e >= 2:
                        pe.wait_ge(moe_acc, at(b, moe_acc, e - 1))
                    for t in range(NT):
                        for j in range(HT):
                            last = mm(ps[:, t * D:(t + 1) * D], hid[:, e % 2, j, t * P:(t + 1) * P], w2t[:, e * HT + j, :],
                                      start=(j == 0), stop=(j == HT - 1))
                    last.then_inc(moe_ps, 1)

                expert_in(0)
                expert_in(1)
                pe.wait_ge(comb_ready, at(b, comb_ready, 1))
                ps = comb_bank
                for t in range(NT):
                    last = tr(ps[0:NE, t * P:(t + 1) * P], comb[:, t, :], ident[:, :])
                last.then_inc(ct_ps, 1)
                expert_out(0)
                pe.wait_ge(ct_sb, at(b, ct_sb, 1))
                ps = b2_bank
                for t in range(NT):
                    last = mm(ps[:, t * D:(t + 1) * D], comb_t[0:NE, t * P:(t + 1) * P], b2e[:, :], start=True, stop=True)
                last.then_inc(b2_ps, 1)
                for e in range(1, NE):
                    if e + 1 < NE:
                        expert_in(e + 1)
                    expert_out(e)

                layer_norm(2)
                ps = gb_bank
                for t in range(NT):
                    last = mm(ps[:, t * 2 * HD:(t + 1) * 2 * HD], h_t[:, t * P:(t + 1) * P], wgb[:, :], start=True, stop=True)
                last.then_inc(gb_ps, 1)

                def to_tokens(n):
                    i = n - NQK
                    pe.wait_ge(qkv_t, at(b, qkv_t, n + 1))
                    ps = vt_bank(i)
                    if i >= 2:
                        pe.wait_ge(v_tok, at(b, v_tok, i - 1))
                    for t in range(NT):
                        last = tr(ps[:, t * P:(t + 1) * P], v_t[:, n % 4, t * P:(t + 1) * P], ident[:, :])
                    last.then_inc(vt_ps, 1)

                pe.wait_ge(wc_in, at(b, wc_in, 48))
                def convolve(i):
                    if i == 1:
                        pe.wait_ge(dec_ready, at(b, dec_ready, 1))
                        pe.wait_ge(dt_ready, at(b, dt_ready, NG))
                        pe.wait_ge(k_sq, at(b, k_sq, 2))
                    elif i == 2:
                        pe.wait_ge(gd_ready, at(b, gd_ready, NG))
                        pe.wait_ge(pt_ready, at(b, pt_ready, NG))
                    for n in conv_tiles[i]:
                        ps = z_bank(n)
                        if n >= 4:
                            pe.wait_ge(taps, at(b, taps, n - 3))
                        mm(ps[:, :], wconv[:, n * P:(n + 1) * P], h_t[:, :], start=True, stop=True).then_inc(z_ps, 1)
                        if n >= NQK + V_LAG:
                            to_tokens(n - V_LAG)
                    if n == NCV - 1:
                        for n in range(NCV - V_LAG, NCV):
                            to_tokens(n)

                def norm(c):
                    sl = slice(c * P, (c + 1) * P)
                    if c < 2:
                        if c == 0:
                            pe.wait_ge(qkv_t, at(b, qkv_t, NQK))
                        pe.wait_ge(taps, at(b, taps, conv_tiles[0].stop if c == 0 else NCV))
                        if c == 1:
                            pe.wait_ge(v_tok, at(b, v_tok, HD))
                    else:
                        pe.wait_ge(lv_sb, at(b, lv_sb, 5 * NG * (c - 1)))
                    ps = dec_bank
                    mm(ps[:, 0:HD], upto[:, :], gk[:, c, :], start=True, stop=True)
                    mm(ps[:, HD:2 * HD], later[:, :], gk[:, c, :], start=True, stop=True)
                    mm(ps[:, 2 * HD:3 * HD], ones[:, :], gk[:, c, :], start=True, stop=True).then_inc(small_ps, 1)
                    for x, first, done in (("k", NP, kt_ps), ("q", 0, qt_ps)):
                        for i, lot in enumerate((range(0, 4), range(4, NP))):
                            ps = (k_banks if x == "k" else q_banks)[i]
                            for j in lot:
                                last = tr(ps[:, j % 4 * P:(j % 4 + 1) * P], qk_t[:, first + j, sl], ident[:, :])
                            last.then_inc(done, 1)
                    pe.wait_ge(gm_ready, at(b, gm_ready, c + 1))
                    for g in range(NG):
                        if c >= 3:
                            pe.wait_ge(gate_ready, at(b, gate_ready, NG * (c - 3) + g + 1))
                        ps = l_banks[g]
                        mm(ps[:, :], later[:, :], gm[:, GH * g:GH * (g + 1), :].rearrange("p h w -> p (h w)"), start=True, stop=False)
                        mm(ps[:, :], ident_bf[:, :], mask_k[:, :, :].rearrange("p h w -> p (h w)"), start=False, stop=True).then_inc(l_ps, 1)

                def key_rows(g):
                    order = [0, 2, 1, 3] if g == 2 else range(GH)
                    return [(j, h, slice(DK * (h % 2), DK * (h % 2) + DK)) for j in order for h in [range(HD)[HS[g]][j]]]

                def gram(c):
                    sl = slice(c * P, (c + 1) * P)
                    pe.wait_ge(khat_ready, at(b, khat_ready, c + 1))
                    if c == 0:
                        pe.wait_ge(v_tok, at(b, v_tok, conv_tiles[1].stop - V_LAG - NQK))
                    elif c >= 2:
                        pe.wait_ge(s_ready, at(b, s_ready, 2 * c - 1))
                    for i, lot in enumerate((range(0, 4), range(4, NP))):
                        ps = k_banks[i]
                        for j in lot:
                            last = tr(ps[:, j % 4 * P:(j % 4 + 1) * P], khat[:, j * P:(j + 1) * P], ident[:, :])
                        last.then_inc(kh_ps, 1)
                    pe.wait_ge(kh_ready, at(b, kh_ready, 2 * c + 2))
                    if c == 0:
                        pe.wait_ge(q_sq, at(b, q_sq, 2))
                        pe.wait_ge(taps, at(b, taps, conv_tiles[1].stop))
                    elif c == 1:
                        pe.wait_ge(dec_ready, at(b, dec_ready, 2))
                        pe.wait_ge(dt_ready, at(b, dt_ready, 2 * NG))
                    else:
                        pe.wait_ge(o_ready, at(b, o_ready, NG * (c - 1)))
                    for name, done, banks in (("g", g_ps, low_banks), ("qk2", qk2_ps, high_banks)):
                        for g in range(NG):
                            ps = banks[g]
                            for j, h, rows in key_rows(g):
                                rhs = kh_t[rows, c % 2, h // 2, :] if name == "g" else qk_t[rows, h // 2, sl]
                                last = mm(ps[:, j * P:(j + 1) * P], kh_t[rows, c % 2, h // 2, :], rhs, start=True, stop=True)
                                if h == 10:
                                    last.then_inc(lower_ps, 1)
                                    pe.wait_ge(lower_ps, lower())
                            last.then_inc(done, 1)

                def levels(c):
                    n16, nsb = 3 * NG * c, 5 * NG * c
                    pe.wait_ge(t_in, at(b, t_in, 16 * 16 * (c + 1)))
                    pe.wait_ge(bm_ready, at(b, bm_ready, NG * (c + 1)))
                    if c + 1 < NT:
                        pe.wait_ge(gd_ready, at(b, gd_ready, NG * (c + 2)))
                        pe.wait_ge(pt_ready, at(b, pt_ready, NG * (c + 2)))
                    else:
                        pe.wait_ge(o_ready, at(b, o_ready, NG * c))
                    for s in range(8):
                        for g in range(NG):
                            if s == 1:
                                pe.wait_ge(lv_16, at(b, lv_16, n16 + g + 1))
                            elif s == 3:
                                pe.wait_ge(lv_16, at(b, lv_16, n16 + 2 * NG + g + 1))
                            elif s == 4:
                                pe.wait_ge(lv_sb, at(b, lv_sb, nsb + g + 1))
                            elif s == 6:
                                pe.wait_ge(lv_sb, at(b, lv_sb, nsb + NG + g + 1))
                            elif s == 7:
                                pe.wait_ge(lv_sb, at(b, lv_sb, nsb + 3 * NG + g + 1))
                            ps = level_bank(s, g)
                            for j in range(GH):
                                h = GH * g + j
                                at_j, at_d = slice(j * P, (j + 1) * P), slice(j * DK, (j + 1) * DK)
                                if s == 0:
                                    last = mm(ps[:, at_j], bms[c % 2][:, h, :], t16[:, h, :], start=True, stop=True)
                                elif s == 1:
                                    last = mm(ps[:, at_j], ub[:, h, :], x16[:, h, :], start=True, stop=True)
                                elif s == 2:
                                    last = mm(ps[:, at_j], x16[:, h, :], ub[:, h, :], start=True, stop=True)
                                elif s == 3:
                                    last = mm(ps[:, at_j], bms[c % 2][:, h, :], tw[:, h, :], start=True, stop=True)
                                elif s == 4:
                                    last = mm(ps[:, at_j], xw[:, h, :], u32[:, h, :], start=True, stop=True)
                                elif s == 5:
                                    last = mm(ps[:, at_j], u32[:, h, :], xw[:, h, :], start=True, stop=True)
                                elif s == 6:
                                    last = mm(ps[:, at_d], bms[c % 2][0:DK, h, :], tw[0:DK, h, 0:DK], start=True, stop=True)
                                else:
                                    last = mm(ps[0:DK, at_d], u64[:, h, :], xw[:, h, DK:P], start=True, stop=True)
                            last.then_inc(lv_ps, 1)

                def gate_proj(c):
                    for g in range(NG):
                        if c + 1 == NT:
                            if g == 0:
                                pe.wait_ge(o_ready, at(b, o_ready, NG * NT))
                        elif g:
                            pe.wait_ge(lv_sb, at(b, lv_sb, 5 * NG * (c + 1) + 4 * NG + g))
                        ps = gate_banks[g]
                        mm(ps[:, :], h_t[:, c * P:(c + 1) * P], wgate[:, g * 512:(g + 1) * 512], start=True, stop=True).then_inc(gt_ps, 1)

                def scan(c):
                    sl = slice(c * P, (c + 1) * P)
                    pe.wait_ge(s_ready, at(b, s_ready, 2 * c + 1))
                    if c + 2 < NT:
                        pe.wait_ge(dec_ready, at(b, dec_ready, c + 3))
                        pe.wait_ge(q_sq, at(b, q_sq, 2 * (c + 3)))
                        pe.wait_ge(dt_ready, at(b, dt_ready, NG * (c + 3)))
                    else:
                        pe.wait_ge(lv_sb, at(b, lv_sb, 5 * NG * (c + 1)))
                        pe.wait_ge(gate_ready, at(b, gate_ready, NG * c))
                    if c:
                        pe.wait_ge(wo_done, at(b, wo_done, c))
                    for name, done, banks in (("ks", ks_ps, ks_banks), ("qs", qs_ps, low_banks)):
                        for g in range(NG):
                            ps = banks[g]
                            for j, h, rows in key_rows(g):
                                lhs = kh_t[rows, c % 2, h // 2, :] if name == "ks" else qk_t[rows, h // 2, sl]
                                last = mm(ps[:, j * P:(j + 1) * P], lhs, state[rows, h // 2, :], start=True, stop=True)
                                if h == 10:
                                    last.then_inc(lower_ps, 1)
                                    pe.wait_ge(lower_ps, lower())
                            last.then_inc(done, 1)
                    for g in range(NG):
                        if g == 0 and c + 2 < NT:
                            pe.wait_ge(lv_sb, at(b, lv_sb, 5 * NG * (c + 1)))
                        pe.wait_ge(r_ready, at(b, r_ready, NG * c + g + 1))
                        ps = high_banks[g]
                        for j, h, rows in key_rows(g):
                            last = mm(ps[:, j * P:(j + 1) * P], xw[:, h, :], rb[:, h, :], start=True, stop=True)
                        last.then_inc(yd_ps, 1)
                    if c + 1 < NT:
                        pe.wait_ge(kd_ready, at(b, kd_ready, c + 1))
                        for i, lot in enumerate((range(0, 4), range(4, NP))):
                            pe.wait_ge(dl_ready, at(b, dl_ready, NG * c + (2 if i == 0 else 3)))
                            ps = k_banks[i]
                            for n in lot:
                                for s in range(2):
                                    last = mm(ps[DK * s:DK * (s + 1), n % 4 * DV:(n % 4 + 1) * DV], kd[:, c % 2, 2 * n + s, :],
                                              dl[:, 2 * n + s, :], start=True, stop=True)
                            last.then_inc(su_ps, 1)
                    for g in range(NG):
                        if c + 1 == NT:
                            pe.wait_ge(dl_ready, at(b, dl_ready, NG * c + g + 1))
                        pe.wait_ge(qse_ready, at(b, qse_ready, NG * c + g + 1))
                        ps = low_banks[g]
                        for j, h, rows in key_rows(g):
                            last = mm(ps[:, j * P:(j + 1) * P], pt[:, c % 2, h, :], dl[:, h, :], start=True, stop=True)
                        last.then_inc(pd_ps, 1)

                def project(c):
                    pe.wait_ge(og_ready, at(b, og_ready, c + 1))
                    for g in range(NG):
                        if g == 0 and c + 3 < NT:
                            pe.wait_ge(q_sq, at(b, q_sq, 2 * (c + 4)))
                        elif g == 0 and c + 2 == NT:
                            pe.wait_ge(s_ready, at(b, s_ready, 2 * c + 3))
                        ps = og_banks[g]
                        for j in range(GH):
                            last = tr(ps[:, j * P:(j + 1) * P], og[:, GH * g + j, :], ident[:, :])
                        last.then_inc(og_ps, 1)
                    ps = wo_bank
                    pe.wait_ge(ogt_ready, at(b, ogt_ready, NG * (c + 1)))
                    for h in range(HD):
                        last = mm(ps[:, 0:D], ogt[:, h, :], wo[:, h, :], start=(h == 0), stop=(h == HD - 1))
                    last.then_inc(wo_ps, 1)

                walk = {"conv": convolve, "norm": norm, "gram": gram, "levels": levels, "project": project, "gate": gate_proj, "scan": scan}
                for name, c in stages:
                    if name in walk:
                        walk[name](c)

                layer_norm(3)
                ps = logit_bank
                for t in range(NT):
                    last = mm(ps[:, t * NE:(t + 1) * NE], h_t[:, t * P:(t + 1) * P], router1[:, :], start=True, stop=True)
                last.then_inc(rt_ps, 1)
                for j in range(FT):
                    mm(f_bank(j)[:, :], w1[:, j * P:(j + 1) * P], h_t[:, :], start=True, stop=True).then_inc(f_ps, 1)
                pe.wait_ge(f_sb, at(b, f_sb, FT))
                ps = f2_bank
                for t in range(NT):
                    for j in range(FT):
                        mm(ps[:, t * D:(t + 1) * D], hid1[:, j, t * P:(t + 1) * P], w2[:, j, :], start=(j == 0), stop=False)
                    last = mm(ps[:, t * D:(t + 1) * D], ones[0:1, :], b2f, start=False, stop=True)
                last.then_inc(f2_ps, 1)

        @block.vector
        def _(dve):
            V = nc.vector
            pro = [0]

            def then(ins):
                pro[0] += 1
                ins.then_inc(dve_pro, 1)
                dve.wait_ge(dve_pro, pro[0])

            dve.wait_ge(prologue_ps, 1)
            mod4 = mod_t[:, :, :].rearrange("p (n k) b -> p n k b", k=2)
            ps4 = PS[0][:, 0:8 * NB].rearrange("p (n k b) -> p n k b", k=2, b=NB)
            V.tensor_copy(mod4[:, :, 0, :], ps4[:, :, 0, :])
            V.tensor_scalar(mod4[:, :, 1, :], ps4[:, :, 1, :], 1.0, None, ALU.add)
            then(V.tensor_copy(g_tmp, PS[1][0:NB, :]))
            then(V.scalar_tensor_tensor(g_rows, g_tmp, -1.0, g_tmp, ALU.mult, ALU.max))
            then(V.tensor_scalar(g_rows, g_rows, 0.25, None, ALU.max))
            then(V.tensor_scalar(g_tmp, g_tmp, 0.0, 2.0, ALU.is_ge, ALU.mult))
            V.scalar_tensor_tensor(g_rows, g_tmp, -1.0, g_rows, ALU.add, ALU.mult).then_inc(prologue_sb, 1)
            for n in range(2 * NW // 4):
                dve.wait_ge(prologue_ps, n + 2)
                dst = w1t if n < NW // 4 else w2t
                V.tensor_copy(dst[:, n % (NW // 4) * 4:n % (NW // 4) * 4 + 4, :],
                              PS[2 + n % 6][:, :].rearrange("p (n m) -> p n m", m=P)).then_inc(prologue_sb, 1)
            dve.wait_ge(consts_in, CONSTS)
            dve.wait_ge(act_pro, 1)
            V.tensor_scalar(neg_a[:, :], neg_a[:, :], -1.0, None, ALU.mult)
            then(V.tensor_scalar(wo[:, :, :], wo[:, :, :], gnorm[:, 0:1], None, ALU.mult))
            V.memset(t16[:, :, :], 0.0)
            V.memset(x16[:, :, :], 0.0)
            V.memset(u64[0:DK, :, :], 0.0)
            V.memset(u32[:, :, :], 0.0).then_inc(xin_free, 1)
            V.memset(k_stack[0:PARTS, :, :], 1.0).then_inc(prologue_sb, 1)
            V.memset(mrest[:, :], 0.0).then_inc(x_done, 1)

            with dve.Fori(0, NB) as b:

                steps = [0]

                def step():
                    steps[0] += 1
                    return at(b, dve_step, steps[0])

                def layer_norm(k, src):
                    if k == 0:
                        dve.wait_ge(x_in, at(b, x_in, 16))
                        V.tensor_copy(mod_b[:, :], mod_t[:, :, bass.ds(b, 1)].rearrange("p n a -> p (n a)")).then_inc(dve_step, 1)
                        dve.wait_ge(dve_step, step())
                    for t in range(NT):
                        last = V.bn_stats(st[:, t, :], src[:, t, :])
                    last.then_inc(dve_step, 1)
                    dve.wait_ge(dve_step, step())
                    V.tensor_tensor(mv[:, 0, :], st[:, :, 1], st[:, :, 4], ALU.add)
                    V.tensor_tensor(mv[:, 2, :], st[:, :, 2], st[:, :, 5], ALU.add)
                    V.tensor_tensor(mv[:, 1, :], st[:, :, 1], st[:, :, 4], ALU.subtract).then_inc(dve_step, 1)
                    dve.wait_ge(dve_step, step())
                    V.tensor_scalar(mv[:, 0, :], mv[:, 0, :], 0.5, None, ALU.mult)
                    V.scalar_tensor_tensor(mv[:, 1, :], mv[:, 1, :], D / 4.0, mv[:, 1, :], ALU.mult, ALU.mult).then_inc(dve_step, 1)
                    dve.wait_ge(dve_step, step())
                    V.tensor_tensor(mv[:, 1, :], mv[:, 1, :], mv[:, 2, :], ALU.add).then_inc(ln_var, 1)
                    dve.wait_ge(ln_rstd, at(b, ln_rstd, k + 1))
                    for t in range(NT):
                        last = V.tensor_scalar(xn[:, t, :], src[:, t, :], mv[:, 0, t:t + 1], rstd[:, t:t + 1], ALU.subtract, ALU.mult)
                    last.then_inc(ln_xn, 1)
                    dve.wait_ge(ln_ps, at(b, ln_ps, k + 1))
                    V.tensor_scalar(h_t[:, :], ln_bank[:, :], mod_b[:, 2 * k + 1:2 * k + 2], mod_b[:, 2 * k:2 * k + 1],
                                       ALU.mult, ALU.add).then_inc(h_ready, 1)

                def gate_row(i):
                    return gates[:, i, :].unsqueeze(1).to_broadcast([P, NT, D])

                def tiles(ps):
                    return ps[:, :].rearrange("p (c d) -> p c d", c=NT)

                layer_norm(0, xin)
                for i in range(2):
                    dve.wait_ge(qk_f, at(b, qk_f, i + 1))
                    f = qkf[:, i, :]
                    V.tensor_copy(qkp[:, i, 0, :], f).then_inc(dve_step, 1)
                    dve.wait_ge(dve_step, step())
                    V.tensor_tensor(rest, f, qkp[:, i, 0, :], ALU.subtract).then_inc(dve_step, 1)
                    dve.wait_ge(dve_step, step())
                    V.tensor_copy(qkp[:, i, 1, :], rest).then_inc(dve_step, 1)
                    dve.wait_ge(dve_step, step())
                    V.tensor_tensor(qkp[:, i, 2, :], rest, qkp[:, i, 1, :], ALU.subtract).then_inc(qk_parts, 1)
                    dve.wait_ge(qk_parts, at(b, qk_parts, i + 1))
                dve.wait_ge(v_ps, at(b, v_ps, 1))
                dve.wait_ge(v_pads, at(b, v_pads, 1))
                V.tensor_tensor(v32[:, :, :, 0:DA], v_bank[:, :].rearrange("p (c h d) -> p c h d", c=NT, h=HA),
                                   bv[:, :].rearrange("p (h d) -> p h d", h=HA).unsqueeze(1).to_broadcast([P, NT, HA, DA]), ALU.add).then_inc(v_ready, 1)
                for hh in range(2):
                    for h in range(8 * hh, 8 * hh + 8):
                        for t in range(NT):
                            n = h * NT + t
                            dve.wait_ge(s_ps, at(b, s_ps, n + 1))
                            last = V.reduce_max(mx[:, h, t:t + 1], score_bank(n)[:, 0:(t + 1) * P], AX.X)
                            last.then_inc(s_max, 1)
                    m = mx[:, 8 * hh:8 * hh + 8, :].rearrange("p h c -> p (h c)")
                    dve.wait_ge(s_max, at(b, s_max, 32 * (hh + 1)))
                    if hh:
                        dve.wait_ge(m_ps, at(b, m_ps, 1))
                    V.tensor_scalar(mparts[:, 0, :], m, -1.0, None, ALU.mult).then_inc(dve_step, 1)
                    dve.wait_ge(dve_step, step())
                    V.scalar_tensor_tensor(mrest[:, :], m, -1.0, mparts[:, 0, :], ALU.mult, ALU.subtract).then_inc(dve_step, 1)
                    dve.wait_ge(dve_step, step())
                    V.tensor_copy(mparts[:, 1, :], mrest[:, :]).then_inc(dve_step, 1)
                    dve.wait_ge(dve_step, step())
                    V.tensor_tensor(mparts[:, 2, :], mrest[:, :], mparts[:, 1, :], ALU.subtract).then_inc(m_parts, 1)
                for t in range(NT):
                    dve.wait_ge(yt_ps, at(b, yt_ps, t + 1))
                    ps = yt_banks[t][:, :].rearrange("p (h d) -> p h d", d=32)
                    V.reciprocal(rec[:, :], ps[:, :, DA]).then_inc(dve_step, 1)
                    dve.wait_ge(dve_step, step())
                    V.tensor_tensor(y_tok[:, t, :].rearrange("p (h d) -> p h d", d=DA), ps[:, :, 0:DA],
                                       wide(rec[:, :], [P, HA, DA]), ALU.mult).then_inc(y_norm, 1)
                    dve.wait_ge(y_norm, at(b, y_norm, t + 1))
                dve.wait_ge(proj_ps, at(b, proj_ps, 1))
                dve.wait_ge(gates_in, at(b, gates_in, 16))
                dve.wait_ge(out_sent, at(b, out_sent, 16))
                V.tensor_tensor(wide_t, tiles(proj_bank), gate_row(0), ALU.mult).then_inc(dve_step, 1)
                dve.wait_ge(dve_step, step())
                V.tensor_tensor(xs[:, :, :], xin[:, :, :], wide_t, ALU.add).then_inc(xin_free, 1)
                dve.wait_ge(xin_free, at(b, xin_free, 2))

                layer_norm(1, xs)
                logits = small[:, 0:NT * NE].rearrange("p (c e) -> p c e", c=NT)
                top = small[:, 32:64].rearrange("p (c e) -> p c e", c=NT)
                pos = small[:, 64:96].rearrange("p (c e) -> p c e", c=NT)
                diff, wt, com2 = small[:, 96:100], small[:, 100:108].rearrange("p (i c) -> p i c", i=2), small[:, 128:160].rearrange("p (c e) -> p c e", c=NT)
                dve.wait_ge(lg_ps, at(b, lg_ps, 1))
                raw = logit_bank[:, 0:NT * NE].rearrange("p (c e) -> p c e", c=NT)
                V.tensor_copy(logits, raw)
                for t in range(NT):
                    last = V.max(top[:, t, :], raw[:, t, :])
                last.then_inc(dve_step, 1)
                dve.wait_ge(dve_step, step())
                V.tensor_tensor(diff, top[:, :, 1], top[:, :, 0], ALU.subtract).then_inc(top_d, 1)
                for t in range(NT):
                    last = V.max_index(idx[:, t, :], top[:, t, :], logits[:, t, :])
                last.then_inc(dve_step, 1)
                dve.wait_ge(dve_step, step())
                V.tensor_copy(pos, idx[:, :, :])
                dve.wait_ge(top_e, at(b, top_e, 1))
                ex = small[:, 108:112]
                V.tensor_scalar(diff, ex, 1.0, None, ALU.add).then_inc(dve_step, 1)
                dve.wait_ge(dve_step, step())
                V.reciprocal(wt[:, 0, :], diff).then_inc(dve_step, 1)
                dve.wait_ge(dve_step, step())
                V.tensor_tensor(wt[:, 1, :], ex, wt[:, 0, :], ALU.mult).then_inc(dve_step, 1)
                dve.wait_ge(dve_step, step())
                for t in range(NT):
                    V.tensor_scalar(comb[:, t, :], iota8[:, :], pos[:, t, 0:1], wt[:, 0, t:t + 1], ALU.is_equal, ALU.mult)
                    last = V.tensor_scalar(com2[:, t, :], iota8[:, :], pos[:, t, 1:2], wt[:, 1, t:t + 1], ALU.is_equal, ALU.mult)
                last.then_inc(dve_step, 1)
                dve.wait_ge(dve_step, step())
                V.tensor_tensor(comb[:, :, :], comb[:, :, :], com2, ALU.add).then_inc(comb_ready, 1)
                dve.wait_ge(comb_ready, at(b, comb_ready, 1))
                dve.wait_ge(b2_ps, at(b, b2_ps, 1))
                V.tensor_copy(moe, tiles(b2_bank)).then_inc(dve_step, 1)
                dve.wait_ge(dve_step, step())
                for e in range(NE):
                    dve.wait_ge(moe_ps, at(b, moe_ps, e + 1))
                    if e:
                        dve.wait_ge(moe_acc, at(b, moe_acc, e))
                    for t in range(NT):
                        last = V.scalar_tensor_tensor(moe[:, t, :], moe_bank(e)[:, t * D:(t + 1) * D], comb[:, t, e:e + 1],
                                                      moe[:, t, :], ALU.mult, ALU.add)
                    last.then_inc(moe_acc, 1)
                dve.wait_ge(moe_acc, at(b, moe_acc, NE))
                V.tensor_tensor(moe, moe, gate_row(1), ALU.mult).then_inc(dve_step, 1)
                dve.wait_ge(dve_step, step())
                V.tensor_tensor(xs[:, :, :], xs[:, :, :], moe, ALU.add).then_inc(dve_step, 1)
                dve.wait_ge(dve_step, step())

                layer_norm(2, xs)
                V.memset(state[:, :, :], 0.0).then_inc(s_ready, 1)
                dve.wait_ge(gb_ps, at(b, gb_ps, 1))
                ps = gb_bank[:, 0:NT * 2 * HD].rearrange("p (c k h) -> p c k h", c=NT, k=2)

                def over_tiles(row):
                    return row[:, :].unsqueeze(1).to_broadcast([P, NT, HD])

                def scratch(i):
                    return small[:, 192 + i * 48:240 + i * 48].rearrange("p (c h) -> p c h", c=NT)
                z, az, zb, ln1 = scratch(0), scratch(1), scratch(2), scratch(3)
                V.tensor_tensor(zb, ps[:, :, 1, :], over_tiles(beta_bias), ALU.add)
                V.tensor_tensor(z, ps[:, :, 0, :], over_tiles(dt_bias), ALU.add).then_inc(dve_step, 1)
                dve.wait_ge(dve_step, step())
                V.scalar_tensor_tensor(az, z, -1.0, z, ALU.mult, ALU.min).then_inc(gb_z, 1)
                dve.wait_ge(gb_e, at(b, gb_e, 1))
                V.scalar_tensor_tensor(z, z, 0.0, ln1, ALU.max, ALU.add).then_inc(dve_step, 1)
                dve.wait_ge(dve_step, step())
                V.tensor_tensor(gk[:, :, :], z, over_tiles(neg_a), ALU.mult)
                V.tensor_scalar(zb, zb, 1.0, None, ALU.add).then_inc(dve_step, 1)
                dve.wait_ge(dve_step, step())
                V.reciprocal(beta[:, :, :], zb).then_inc(gk_ready, 1)
                def convolve(i):
                    for n in conv_tiles[i]:
                        dve.wait_ge(tap0, at(b, tap0, n + 1))
                        ps, a = z_bank(n), acc[:, n % 4, :]
                        for k in (1, 2, 3):
                            ins = V.scalar_tensor_tensor(a[:, k:T], ps[:, 0:T - k], conv[:, n, 3 - k:4 - k], a[:, k:T], ALU.mult, ALU.add)
                            if k < 3:
                                ins.then_inc(dve_step, 1)
                                dve.wait_ge(dve_step, step())
                        ins.then_inc(taps, 1)

                def norm(c):
                    dve.wait_ge(k_sq, at(b, k_sq, 2 * c + 2))
                    V.reduce_sum(ssq[:, c, HD:2 * HD], ksq.rearrange("p (h d) -> p h d", d=DK), AX.X)
                    dve.wait_ge(q_sq, at(b, q_sq, 2 * c + 2))
                    V.reduce_sum(ssq[:, c, 0:HD], qsq.rearrange("p (h d) -> p h d", d=DK), AX.X).then_inc(ss_ready, 1)
                    dve.wait_ge(dec_ready, at(b, dec_ready, c + 1))
                    V.tensor_scalar(neg_dec[:, c, :], dec[:, c, 0, :], -1.0, None, ALU.mult)
                    dve.wait_ge(rn_ready, at(b, rn_ready, c + 1))
                    if c:
                        dve.wait_ge(kd_ready, at(b, kd_ready, c))
                        dve.wait_ge(kh_ps, at(b, kh_ps, 2 * c))
                    V.tensor_tensor(khat.rearrange("p (h d) -> p h d", d=DK), ktok.rearrange("p (h d) -> p h d", d=DK),
                                       wide(rn[:, c, HD:2 * HD], [P, HD, DK]), ALU.mult).then_inc(khat_ready, 1)

                def gram(c):
                    for g, hs in enumerate(HS):
                        dve.wait_ge(g_ps, at(b, g_ps, NG * c + g + 1))
                        if g != 1:
                            dve.wait_ge(dt_ready, at(b, dt_ready, NG * c + BEFORE[g]))
                        if c >= 2 and g == 0:
                            dve.wait_ge(lv_ps, at(b, lv_ps, 24 * (c - 2) + 21))
                            dve.wait_ge(b_out, at(b, b_out, 16 * NBK * (c - 1)))
                        V.tensor_tensor(bms[c % 2][:, hs, :], low_banks[g][:, :].rearrange("p (h t) -> p h t", h=GH), dt[:, hs, :], ALU.mult).then_inc(gd_ready, 1)
                    for g, hs in enumerate(HS):
                        dve.wait_ge(qk2_ps, at(b, qk2_ps, NG * c + g + 1))
                        V.tensor_tensor(pt[:, c % 2, hs, :], high_banks[g][:, :].rearrange("p (h t) -> p h t", h=GH), dt[:, hs, :], ALU.mult).then_inc(pt_ready, 1)

                def subst(c):
                    dve.wait_ge(b_in, at(b, b_in, 16 * (c + 1)))
                    if c:
                        dve.wait_ge(t_out, at(b, t_out, 32 * c))
                    V.tensor_copy(blk_t[:, :], eye16[:, :]).then_inc(dve_step, 1)
                    dve.wait_ge(dve_step, step())
                    cols = blk_t[:, :].rearrange("p (k c) -> p c k", c=BS)
                    a = blk[:, :].rearrange("p (k i) -> p i k", i=BS)
                    for i in range(1, BS):
                        tmp = blk_tmp[0:NBK * HD, 0:i * i].rearrange("p (c k) -> p c k", k=i)
                        V.tensor_tensor(tmp, cols[:, 0:i, 0:i], a[:, i, 0:i].unsqueeze(1).to_broadcast([NBK * HD, i, i]), ALU.mult).then_inc(dve_step, 1)
                        dve.wait_ge(dve_step, step())
                        V.tensor_reduce(blk_t[:, i * BS:i * BS + i], tmp, AX.X, ALU.add, negate=True).then_inc(dve_step, 1)
                        dve.wait_ge(dve_step, step())
                    V.tensor_copy(blk_x[:, :].rearrange("p (c k) -> p c k", k=BS), cols).then_inc(t_ready, 1)

                def levels(c):
                    n16 = 3 * NG * c
                    dve.wait_ge(t_in, at(b, t_in, 16 * 16 * (c + 1)))
                    for s in range(3):
                        for g in range(NG):
                            hs = slice(GH * g, GH * (g + 1))
                            dve.wait_ge(lv_ps, at(b, lv_ps, 24 * c + NG * s + g + 1))
                            ps = level_bank(s, g)[:, :].rearrange("p (h t) -> p h t", h=GH)
                            if s == 0:
                                if g == 0 and c + 1 < NT:
                                    dve.wait_ge(l_ps, at(b, l_ps, NG * (c + 2)))
                                ins = V.tensor_tensor(ub[:, hs, :], ps, mask16[:, :].unsqueeze(1).to_broadcast([P, GH, P]), ALU.mult)
                            elif s == 1:
                                if c and g == 0:
                                    dve.wait_ge(yd_ps, at(b, yd_ps, NG * c))
                                ins = V.tensor_tensor(xw[:, hs, :], x16[:, hs, :], ps, ALU.subtract)
                            else:
                                if c >= 2 and g == 0:
                                    dve.wait_ge(og_ready, at(b, og_ready, c - 1))
                                ins = V.tensor_tensor(tw[:, hs, :], t16[:, hs, :], ps, ALU.subtract)
                            ins.then_inc(lv_16, 1)

                def scan(c):
                    for g in range(NG):
                        dve.wait_ge(ks_ps, at(b, ks_ps, NG * c + g + 1))
                        ps = ks_banks[g]
                        for j, h in enumerate(range(HD)[HS[g]]):
                            ins = V.scalar_tensor_tensor(rb[:, h, :], ps[:, j * P:(j + 1) * P], neg_dec[:, c, h:h + 1], v_all[:, c, h, :], ALU.mult, ALU.add)
                        ins.then_inc(r_ready, 1)
                    if c + 1 < NT:
                        dve.wait_ge(sd_ready, at(b, sd_ready, c + 1))
                        for i in range(2):
                            dve.wait_ge(su_ps, at(b, su_ps, 2 * c + i + 1))
                            if i == 0:
                                dve.wait_ge(qs_ps, at(b, qs_ps, NG * (c + 1)))
                            ns = slice(4 * i, min(4 * i + 4, NP))
                            n = ns.stop - ns.start
                            V.tensor_tensor(state[:, ns, :], k_banks[i][:, 0:n * DV].rearrange("p (n v) -> p n v", n=n), sdec[:, ns, :], ALU.add).then_inc(s_ready, 1)
                    for g, hs in enumerate(HS):
                        dve.wait_ge(pd_ps, at(b, pd_ps, NG * c + g + 1))
                        dve.wait_ge(qse_ready, at(b, qse_ready, NG * c + g + 1))
                        V.tensor_tensor(ob[:, hs, :], low_banks[g][:, :].rearrange("p (h t) -> p h t", h=GH), qse[:, hs, :], ALU.add).then_inc(o_ready, 1)

                def rms(c):
                    dve.wait_ge(osq_ready, at(b, osq_ready, c + 1))
                    V.reduce_sum(fac[:, 0, :], osq, AX.X).then_inc(dve_step, 1)
                    dve.wait_ge(dve_step, step())
                    V.tensor_scalar(fac[:, 1, :], rn[:, c, 0:HD], DK ** -0.5, None, ALU.mult).then_inc(dve_step, 1)
                    dve.wait_ge(dve_step, step())
                    V.tensor_tensor(fac[:, 2, :], fac[:, 1, :], fac[:, 1, :], ALU.mult).then_inc(dve_step, 1)
                    dve.wait_ge(dve_step, step())
                    V.tensor_tensor(fac[:, 0, :], fac[:, 0, :], fac[:, 2, :], ALU.mult).then_inc(ot_ready, 1)

                def scale(c):
                    dve.wait_ge(of_ready, at(b, of_ready, c + 1))
                    V.tensor_tensor(fac[:, 1, :], fac[:, 1, :], fac[:, 2, :], ALU.mult).then_inc(dve_step, 1)
                    dve.wait_ge(dve_step, step())
                    V.tensor_tensor(ob, ob, wide(fac[:, 1, :], [P, HD, DV]), ALU.mult).then_inc(on_ready, 1)

                def project(c):
                    dve.wait_ge(wo_ps, at(b, wo_ps, c + 1))
                    V.tensor_tensor(wide_x(c), wo_bank[:, 0:D], gates[:, 2, :], ALU.mult).then_inc(dve_step, 1)
                    dve.wait_ge(dve_step, step())
                    V.tensor_tensor(xs[:, c, :], xs[:, c, :], wide_x(c), ALU.add).then_inc(wo_done, 1)

                def wide_x(c):
                    return xn[:, c, :]

                walk = {"conv": convolve, "norm": norm, "gram": gram, "subst": subst, "levels": levels, "scan": scan, "rms": rms, "scale": scale,
                        "project": project}
                for name, c in stages:
                    if name in walk:
                        walk[name](c)
                dve.wait_ge(wo_done, at(b, wo_done, NT))

                layer_norm(3, xs)
                top = small[:, 32:64].rearrange("p (c e) -> p c e", c=NT)
                ex = small[:, 64:96].rearrange("p (c e) -> p c e", c=NT)
                tot, r1 = small[:, 96:100], small[:, 100:104]
                p2 = small[:, 104:112].rearrange("p (c i) -> p c i", c=NT)
                dve.wait_ge(rt_ps, at(b, rt_ps, 1))
                logits = logit_bank[:, 0:NT * NE].rearrange("p (c e) -> p c e", c=NT)
                V.reduce_max(tot, logits, AX.X).then_inc(dve_step, 1)
                dve.wait_ge(dve_step, step())
                V.tensor_tensor(ex, logits, wide(tot, [P, NT, NE]), ALU.subtract).then_inc(rt_d, 1)
                dve.wait_ge(rt_e, at(b, rt_e, 1))
                V.reduce_sum(tot, ex, AX.X)
                for t in range(NT):
                    last = V.max(top[:, t, :], ex[:, t, :])
                last.then_inc(dve_step, 1)
                dve.wait_ge(dve_step, step())
                V.reciprocal(r1, tot).then_inc(dve_step, 1)
                dve.wait_ge(dve_step, step())
                V.tensor_tensor(p2, top[:, :, 0:2], wide(r1, [P, NT, 2]), ALU.mult).then_inc(dve_step, 1)
                dve.wait_ge(dve_step, step())
                V.tensor_tensor(tot, p2[:, :, 0], p2[:, :, 1], ALU.add).then_inc(dve_step, 1)
                dve.wait_ge(dve_step, step())
                V.reciprocal(r1, tot).then_inc(dve_step, 1)
                dve.wait_ge(dve_step, step())
                V.tensor_tensor(p2, p2, wide(r1, [P, NT, 2]), ALU.mult).then_inc(dve_step, 1)
                dve.wait_ge(dve_step, step())
                V.tensor_tensor(tot, p2[:, :, 0], p2[:, :, 1], ALU.add).then_inc(rt_ready, 1)
                dve.wait_ge(rt_ready, at(b, rt_ready, 1))
                dve.wait_ge(f2_ps, at(b, f2_ps, 1))
                V.tensor_tensor(xn[:, :, :], tiles(f2_bank), wide(tot, [P, NT, D]), ALU.mult).then_inc(dve_step, 1)
                dve.wait_ge(dve_step, step())
                V.tensor_tensor(xn[:, :, :], xn[:, :, :], gate_row(3), ALU.mult).then_inc(dve_step, 1)
                dve.wait_ge(dve_step, step())
                V.tensor_tensor(xs[:, :, :], xs[:, :, :], xn[:, :, :], ALU.add).then_inc(x_done, 1)

        @block.scalar
        def _(act):
            A = nc.scalar
            act.wait_ge(consts_in, CONSTS)
            A.activation(c_t, c_t, ACT.Silu).then_inc(silu_c, 1)
            A.activation(neg_a[:, :], neg_a[:, :], ACT.Exp).then_inc(act_pro, 1)
            act.wait_ge(masks_made, 1)

            with act.Fori(0, NB) as b:
                nc.scalar.preload_act_table_set(EXP_LN)

                steps = [0]

                def step():
                    steps[0] += 1
                    return at(b, act_step, steps[0])

                def layer_norm(k):
                    act.wait_ge(ln_var, at(b, ln_var, k + 1))
                    A.activation(lnv[:, :], mv[:, 1, :], ACT.Ln, scale=1.0 / D, bias=eps5[:, 0:1]).then_inc(act_step, 1)
                    act.wait_ge(act_step, step())
                    A.activation(rstd[:, :], lnv[:, :], ACT.Exp, scale=-0.5).then_inc(ln_rstd, 1)

                layer_norm(0)
                for i in range(2):
                    act.wait_ge(qk_ps, at(b, qk_ps, i + 1))
                    A.activation(qkf[:, i, :], qk_banks[i][:, :], ACT.Identity, bias=bqk[:, i:i + 1]).then_inc(qk_f, 1)

                def copy_maxima(hh):
                    act.wait_ge(m_ps, at(b, m_ps, hh + 1))
                    if hh:
                        act.wait_ge(m_out, at(b, m_out, 16))
                    A.copy(m_t[:, :], max_banks[hh][0:96, 0:P // 2].bitcast(BF16)).then_inc(m_sb, 1)

                def copy_y(g):
                    act.wait_ge(pv_ps, at(b, pv_ps, 4 * g + 4))
                    A.copy(y32[:, g, :], y_bank(g)[:, :]).then_inc(y_sb, 1)

                copy_maxima(0)
                for h in range(HA):
                    if h == 8:
                        copy_maxima(1)
                    if h >= 2 and h % 4 != 1:
                        act.wait_ge(pv_ps, at(b, pv_ps, h - 1))
                    c0 = 0
                    for i, n in enumerate((T, T - P, T - 2 * P + P)):
                        act.wait_ge(st_ps, at(b, st_ps, 3 * h + i + 1))
                        A.activation(p_t[:, h % 2, c0:c0 + n], score_t_bank(h, i)[:, 0:n], ACT.Exp, scale=SA).then_inc(p_ready, 1)
                        c0 += n
                    if h % 4 == 0 and h:
                        copy_y(h // 4 - 1)
                copy_y(3)
                act.wait_ge(y2_ps, at(b, y2_ps, 1))
                A.copy(y_t, y2_bank[:, :]).then_inc(y2_sb, 1)

                layer_norm(1)
                act.wait_ge(top_d, at(b, top_d, 1))
                A.activation(small[:, 108:112], small[:, 96:100], ACT.Exp).then_inc(top_e, 1)
                for n in range(NE * HT):
                    if n == 2 * HT:
                        act.wait_ge(ct_ps, at(b, ct_ps, 1))
                        A.copy(comb_t[:, :], comb_bank[0:NE, :]).then_inc(ct_sb, 1)
                    act.wait_ge(hid_ps, at(b, hid_ps, n + 1))
                    if n >= 2 * HT and n % HT == 0:
                        act.wait_ge(moe_ps, at(b, moe_ps, n // HT - 1))
                    A.activation(hid[:, n // HT % 2, n % HT, :], hid_bank(n)[:, :], ACT.Relu, bias=b1e[:, n:n + 1]).then_inc(hid_sb, 1)

                layer_norm(2)
                az, zb, ln1 = [small[:, 192 + i * 48:240 + i * 48] for i in (1, 2, 3)]
                act.wait_ge(gb_z, at(b, gb_z, 1))
                A.activation(zb, zb, ACT.Exp, scale=-1.0)
                A.activation(az, az, ACT.Exp).then_inc(act_step, 1)
                act.wait_ge(act_step, step())
                A.activation(ln1, az, ACT.Ln, bias=ones[:, 0:1]).then_inc(gb_e, 1)

                def first_tap(n):
                    act.wait_ge(z_ps, at(b, z_ps, n + 1))
                    if n >= 4:
                        act.wait_ge(qkv_t, at(b, qkv_t, n - 3))
                    A.activation(acc[:, n % 4, :], z_bank(n)[:, :], ACT.Identity, scale=conv[:, n, 3:4]).then_inc(tap0, 1)

                def silu(n):
                    act.wait_ge(taps, at(b, taps, n + 1))
                    dst = qk_t[:, n, :] if n < NQK else v_t[:, n % 4, :]
                    A.activation(dst, acc[:, n % 4, :], ACT.Silu).then_inc(qkv_t, 1)

                def copy_v(i):
                    act.wait_ge(vt_ps, at(b, vt_ps, i + 1))
                    A.copy(v_all[:, :, i, :], vt_bank(i)[:, :].rearrange("p (c v) -> p c v", c=NT)).then_inc(v_tok, 1)

                nc.scalar.preload_act_table_set("silu_and_others")

                def convolve(i):
                    tiles = conv_tiles[i]
                    if i:
                        nc.scalar.preload_act_table_set("silu_and_others")
                    for n in tiles[0:2]:
                        first_tap(n)
                    for n in tiles:
                        if n + 2 in tiles:
                            first_tap(n + 2)
                        silu(n)
                        if n >= NQK + V_LAG:
                            copy_v(n - NQK - V_LAG)
                    if n == NCV - 1:
                        for v in range(HD - V_LAG, HD):
                            copy_v(v)
                    nc.scalar.preload_act_table_set(EXP_LN)

                def norm(c):
                    act.wait_ge(small_ps, at(b, small_ps, c + 1))
                    ps = dec_bank
                    A.activation(dec[:, c, :, :].rearrange("p k h -> p (k h)"), ps[:, 0:2 * HD], ACT.Exp)
                    A.activation(dec_end[0:DK, c, :], ps[0:DK, 2 * HD:3 * HD:2], ACT.Exp)
                    A.activation(dec_end[DK:P, c, :], ps[DK:P, 2 * HD + 1:3 * HD:2], ACT.Exp).then_inc(dec_ready, 1)
                    if c:
                        act.wait_ge(khat_ready, at(b, khat_ready, c))
                    if c >= 3:
                        act.wait_ge(s_ready, at(b, s_ready, 1 + 2 * (c - 2)))
                    for i, n in enumerate((512, 256)):
                        act.wait_ge(kt_ps, at(b, kt_ps, 2 * c + i + 1))
                        ps = k_banks[i]
                        A.copy(ktok[:, 512 * i:512 * i + n], ps[:, 0:n])
                        A.activation(ksq[:, 512 * i:512 * i + n], ps[:, 0:n], ACT.Square).then_inc(k_sq, 1)
                    for i, n in enumerate((512, 256)):
                        act.wait_ge(qt_ps, at(b, qt_ps, 2 * c + i + 1))
                        A.activation(qsq[:, 512 * i:512 * i + n], q_banks[i][:, 0:n], ACT.Square).then_inc(q_sq, 1)
                    for g in range(NG):
                        act.wait_ge(l_ps, at(b, l_ps, NG * c + g + 1))
                        if c and g == 0:
                            act.wait_ge(pt_ready, at(b, pt_ready, NG * c))
                        A.activation(dt[:, GH * g:GH * (g + 1), :].rearrange("p h t -> p (h t)"), l_banks[g][:, :], ACT.Exp).then_inc(dt_ready, 1)
                    act.wait_ge(ss_ready, at(b, ss_ready, c + 1))
                    A.activation(ssq[:, c, :], ssq[:, c, :], ACT.Ln, bias=eps6[:, 0:1]).then_inc(act_step, 1)
                    act.wait_ge(act_step, step())
                    A.activation(rn[:, c, :], ssq[:, c, :], ACT.Exp, scale=-0.5).then_inc(rn_ready, 1)

                def gram(c):
                    for i, n in enumerate((4, 2)):
                        act.wait_ge(kh_ps, at(b, kh_ps, 2 * c + i + 1))
                        if c >= 2 and i == 0:
                            act.wait_ge(ks_ps, at(b, ks_ps, NG * (c - 1)))
                        A.copy(kh_t[:, c % 2, 4 * i:4 * i + n, :], k_banks[i][:, 0:n * P].rearrange("p (n t) -> p n t", n=n)).then_inc(kh_ready, 1)

                def levels(c):
                    lower = [(slice(32, 64), slice(0, 32)), (slice(96, P), slice(64, 96))]
                    for s in range(3, 8):
                        for g in range(NG):
                            hs = slice(GH * g, GH * (g + 1))
                            act.wait_ge(lv_ps, at(b, lv_ps, 24 * c + NG * s + g + 1))
                            ps = level_bank(s, g)
                            full = ps[:, :].rearrange("p (h t) -> p h t", h=GH)
                            part = ps[:, 0:GH * DK].rearrange("p (h t) -> p h t", h=GH)
                            if s == 3:
                                for r, q in lower:
                                    ins = A.copy(u32[r, hs, q], full[r, :, q])
                            elif s == 4:
                                for r, q in lower:
                                    ins = A.mul(tw[r, hs, q], full[r, :, q], -1.0)
                            elif s == 5:
                                for r, q in lower:
                                    ins = A.mul(xw[q, hs, r], full[q, :, r], -1.0)
                            elif s == 6:
                                ins = A.copy(u64[DK:P, hs, :], part[DK:P])
                            else:
                                ins = A.mul(xw[0:DK, hs, DK:P], part[0:DK], -1.0)
                            ins.then_inc(lv_sb, 1)

                def gate_silu(c):
                    nc.scalar.preload_act_table_set("silu_and_others")
                    for g in range(NG):
                        act.wait_ge(gt_ps, at(b, gt_ps, NG * c + g + 1))
                        A.activation(gate[:, GH * g:GH * (g + 1), :].rearrange("p h v -> p (h v)"), gate_banks[g][:, :], ACT.Silu).then_inc(gate_ready, 1)
                    nc.scalar.preload_act_table_set(EXP_LN)

                def scan(c):
                    if c:
                        act.wait_ge(wo_ps, at(b, wo_ps, c))
                    for g in range(NG):
                        act.wait_ge(qs_ps, at(b, qs_ps, NG * c + g + 1))
                        ps = low_banks[g]
                        for j, h in enumerate(range(HD)[HS[g]]):
                            ins = A.mul(qse[:, h, :], ps[:, j * P:(j + 1) * P], dec[:, c, 0, h:h + 1])
                        ins.then_inc(qse_ready, 1)
                    for g in range(NG):
                        act.wait_ge(yd_ps, at(b, yd_ps, NG * c + g + 1))
                        ps = high_banks[g]
                        for j, h in enumerate(range(HD)[HS[g]]):
                            ins = A.mul(dl[:, h, :], ps[:, j * P:(j + 1) * P], beta[:, c, h:h + 1])
                        ins.then_inc(dl_ready, 1)

                def rms(c):
                    act.wait_ge(ot_ready, at(b, ot_ready, c + 1))
                    A.activation(fac[:, 0, :], fac[:, 0, :], ACT.Ln, scale=1.0 / DV, bias=eps5[:, 0:1]).then_inc(act_step, 1)
                    act.wait_ge(act_step, step())
                    A.activation(fac[:, 2, :], fac[:, 0, :], ACT.Exp, scale=-0.5).then_inc(of_ready, 1)

                def project(c):
                    act.wait_ge(o_ready, at(b, o_ready, NG * (c + 1)))
                    for g in range(NG):
                        act.wait_ge(og_ps, at(b, og_ps, NG * c + g + 1))
                        A.copy(ogt[:, GH * g:GH * (g + 1), :], og_banks[g][:, :].rearrange("p (h t) -> p h t", h=GH)).then_inc(ogt_ready, 1)

                walk = {"conv": convolve, "norm": norm, "gram": gram, "levels": levels, "gate": gate_silu, "scan": scan, "rms": rms, "project": project}
                for name, c in stages:
                    if name in walk:
                        walk[name](c)

                layer_norm(3)
                act.wait_ge(rt_d, at(b, rt_d, 1))
                A.activation(small[:, 64:96], small[:, 64:96], ACT.Exp).then_inc(rt_e, 1)
                for j in range(FT):
                    act.wait_ge(f_ps, at(b, f_ps, j + 1))
                    A.activation(hid1[:, j, :], f_bank(j)[:, :], ACT.Gelu_apprx_tanh, bias=b1f[:, j:j + 1]).then_inc(f_sb, 1)
                act.wait_ge(x_done, at(b, x_done, 2))
                act.dma_start(out[bass.ds(b, 1), :, :].rearrange("a (c p) d -> p (a c) d", p=P), xs[:, :, :]).then_inc(out_sent, 16)
            act.wait_ge(out_sent, 16 * (NB + 1))

        @block.gpsimd
        def _(pool):
            G = nc.gpsimd
            pro = [0]

            def then(ins):
                pro[0] += 1
                ins.then_inc(pool_pro, 1)
                pool.wait_ge(pool_pro, pro[0])

            def keep(ap, pattern, base, step, fill, op=ALU.is_ge):
                return G.affine_select(out=ap, in_=ap, compare_op=op, fill=fill, base=base, pattern=pattern, channel_multiplier=step)

            m16 = mask16[:, :].rearrange("p (q k i) -> p q k i", q=4, k=2)
            G.memset(ident[:, :], 0.0)
            G.memset(ident_bf[:, :], 0.0)
            G.memset(ones[:, :], 1.0)
            G.memset(v_pad[:, 1:32 - DA], 0.0)
            G.memset(v_pad[:, 0:1], 1.0)
            G.memset(later[:, :], 1.0)
            G.memset(upto[:, :], 1.0)
            G.memset(mask_q[:, :], 0.0)
            G.memset(mask_k[:, :, :], 0.0)
            G.memset(m16[:, :, 0, :], 1.0)
            G.memset(m16[:, :, 1, :], 0.0)
            G.memset(eye16[:, :], 0.0)
            G.memset(eps5[:, :], 1e-5)
            then(G.memset(eps6[:, :], 1e-6))
            G.memset(eye16[:, 0:BS * BS:BS + 1], 1.0)
            keep(ident[:, :], [[-1, P]], 0, 1, 1.0, ALU.not_equal)
            keep(ident_bf[:, :], [[-1, P]], 0, 1, 1.0, ALU.not_equal)
            keep(later[:, :], [[-1, P]], -1, 1, 0.0)
            keep(upto[:, :], [[1, P]], 0, -1, 0.0)
            keep(mask_q[:, :], [[-1, P]], 0, 1, MASKED)
            keep(mask_k[:, :, :], [[0, GH], [1, P]], 0, -1, MASKED)
            then(keep(mask16[:, :].rearrange("p (q i) -> p q i", q=4), [[-32, 4], [0, 32]], -16, 1, 0.0))
            G.iota(iota8[:, :], pattern=[[1, NE]], base=0, channel_multiplier=0, allow_small_or_imprecise_dtypes=True)
            keep(mask16[:, :].rearrange("p (q i) -> p q i", q=4), [[32, 4], [0, 32]], 31, -1, 0.0).then_inc(masks_made, 1)

            with pool.Fori(0, NB) as b:

                pool.wait_ge(x_done, at(b, x_done, 1))
                pad = v_pad[:, :].unsqueeze(1).unsqueeze(1).to_broadcast([P, NT, HA, 32 - DA])
                G.tensor_tensor(v32[:, :, :, DA:32], pad, pad, ALU.mult).then_inc(v_pads, 1)

                def norm(c):
                    if c == 0:
                        pool.wait_ge(z_ps, at(b, z_ps, NQK))
                        pool.wait_ge(gk_ready, at(b, gk_ready, 1))
                    else:
                        pool.wait_ge(l_ps, at(b, l_ps, NG * c))
                    if c >= 2:
                        pool.wait_ge(lv_ps, at(b, lv_ps, 24 * (c - 2) + 3 * NG))
                    G.tensor_tensor(gm[:, :, :], upto[:, :].unsqueeze(1).to_broadcast([P, HD, P]), wide(gk[:, c, :], [P, HD, P]), ALU.mult).then_inc(gm_ready, 1)

                def gram(c):
                    for g, hs in enumerate(HS):
                        pool.wait_ge(gd_ready, at(b, gd_ready, NG * c + g + 1))
                        G.tensor_tensor(bms[c % 2][:, hs, :], bms[c % 2][:, hs, :], wide(beta[:, c, hs], [P, GH, P]), ALU.mult).then_inc(bm_ready, 1)
                    pool.wait_ge(khat_ready, at(b, khat_ready, c + 1))
                    pool.wait_ge(dec_ready, at(b, dec_ready, c + 1))
                    if c >= 2:
                        pool.wait_ge(su_ps, at(b, su_ps, 2 * (c - 1)))
                    G.tensor_tensor(kd[:, c % 2, :, :], khat.rearrange("p (h d) -> p h d", d=DK), wide(dec[:, c, 1, :], [P, HD, DK]), ALU.mult).then_inc(kd_ready, 1)

                def scan(c):
                    if c + 1 < NT:
                        pool.wait_ge(s_ready, at(b, s_ready, 2 * c + 1))
                        pool.wait_ge(khat_ready, at(b, khat_ready, min(c + 3, NT)))
                        G.tensor_tensor(sdec, state[:, :, :], wide(dec_end[:, c, :], [P, NP, DV]), ALU.mult).then_inc(sd_ready, 1)

                def rms(c):
                    pool.wait_ge(yd_ps, at(b, yd_ps, NG * (c + 1)))
                    pool.wait_ge(o_ready, at(b, o_ready, NG * (c + 1)))
                    G.tensor_tensor(osq, ob, ob, ALU.mult).then_inc(osq_ready, 1)

                def scale(c):
                    pool.wait_ge(on_ready, at(b, on_ready, c + 1))
                    pool.wait_ge(gate_ready, at(b, gate_ready, NG * (c + 1)))
                    G.tensor_tensor(og, ob, gate[:, :, :], ALU.mult).then_inc(og_ready, 1)

                walk = {"norm": norm, "gram": gram, "scan": scan, "rms": rms, "scale": scale}
                for name, c in stages:
                    if name in walk:
                        walk[name](c)

        @block.sync
        def _(sp):
            for dst, src in const_loads:
                sp.dma_start(dst, src).then_inc(consts_in, 16)
            sp.wait_ge(prologue_sb, 1)
            sp.dma_start(gate_rows, g_rows).then_inc(rows_out, 16)
            sp.wait_ge(prologue_sb, 2 + 2 * NW // 4)
            sp.dma_start(one_rows, k_stack[0:PARTS, :, :].rearrange("p h t -> p (h t)")).then_inc(out_sent, 16)
            sp.dma_start(w1_bounce, w1t.rearrange("p n m -> p (n m)")).then_inc(weights_out, 16)
            sp.dma_start(w2_bounce, w2t.rearrange("p n m -> p (n m)")).then_inc(weights_out, 16)
            sp.wait_ge(rows_out, 16)
            sp.wait_ge(out_sent, 16)
            sp.wait_ge(weights_out, 32)
            sp.wait_ge(silu_c, 1)

            with sp.Fori(0, NB) as b:
                sp.wait_ge(xin_free, at(b, xin_free, 1))
                sp.dma_start(xin[:, :, :], L0_attn_x[bass.ds(b, 1), :, :].rearrange("a (c p) d -> p (a c) d", p=P)).then_inc(x_in, 16)
                sp.wait_ge(x_done, at(b, x_done, 1))
                sp.dma_start(gates[:, :, :].rearrange("p i d -> p (i d)"),
                                gate_rows[bass.ds(b, 1), :].rearrange("a n -> (a n)").partition_broadcast(P)).then_inc(gates_in, 16)
                sp.dma_start(w1t.rearrange("p n m -> p (n m)"), w1_bounce).then_inc(w_in, 16)
                sp.dma_start(w2t.rearrange("p n m -> p (n m)"), w2_bounce).then_inc(w_in, 16)
                nq, nv = HD * DK, HD * DV
                sp.dma_start(wconv[:, 0:nq], L1_attn_Wq).then_inc(wc_in, 16)
                sp.dma_start(wconv[:, nq:2 * nq], L1_attn_Wk).then_inc(wc_in, 16)
                sp.dma_start(wconv[:, 2 * nq:2 * nq + nv], L1_attn_Wv).then_inc(wc_in, 16)
                sp.dma_start(k_stack[KS:KS + PARTS, :, :].rearrange("p h t -> p (h t)"), one_rows).then_inc(stacks_in, 16)
                for i in range(2):
                    sp.wait_ge(qk_parts, at(b, qk_parts, i + 1))
                    sp.dma_start(qk_bounce[i].rearrange("h d n t -> (h d) n t"), qkp[:, i, :, :]).then_inc(parts_out, 16)
                sp.wait_ge(parts_out, at(b, parts_out, 32))
                for i, stack in enumerate((q_stack, k_stack)):
                    for s in range(PARTS * PARTS):
                        part = s // PARTS if i == 0 else s % PARTS
                        sp.dma_start(stack[DA * s:DA * (s + 1), :, :], qk_bounce[i, :, :, part, :].rearrange("h d t -> d h t")).then_inc(stacks_in, 16)
                for hh in range(2):
                    sp.wait_ge(m_sb, at(b, m_sb, hh + 1))
                    sp.dma_start(m_bounce[hh].rearrange("p (a t) -> (p a) t", t=P), m_t[:, :]).then_inc(m_out, 16)
                    sp.wait_ge(m_out, at(b, m_out, 16 * (hh + 1)))
                    sp.dma_start(q_stack[KS:KS + PARTS, 8 * hh:8 * hh + 8, :], m_bounce[hh].rearrange("p (h t) -> p h t", t=T)).then_inc(m_in[hh], 16)
                for c in range(NT):
                    sp.wait_ge(bm_ready, at(b, bm_ready, NG * (c + 1)))
                    for q in range(NBK):
                        r = slice(BS * q, BS * (q + 1))
                        sp.dma_start(b_bounce[q].rearrange("h j i -> j h i"), bms[c % 2][r, :, r]).then_inc(b_out, 16)
                    sp.wait_ge(b_out, at(b, b_out, 16 * NBK * (c + 1)))
                    sp.dma_start(blk[:, :], b_bounce.rearrange("q h j i -> (q h) (j i)")).then_inc(b_in, 16)
                    sp.wait_ge(t_ready, at(b, t_ready, c + 1))
                    sp.dma_start(t_bounce[0].rearrange("q h i k -> (q h) (i k)"), blk_t[:, :]).then_inc(t_out, 16)
                    sp.dma_start(t_bounce[1].rearrange("q h i k -> (q h) (i k)"), blk_x[:, :]).then_inc(t_out, 16)
                    sp.wait_ge(t_out, at(b, t_out, 32 * (c + 1)))
                    for q in range(NBK):
                        r = slice(BS * q, BS * (q + 1))
                        sp.dma_start(t16[r, :, r], t_bounce[0, q].rearrange("h i k -> i h k")).then_inc(t_in, 16)
                        sp.dma_start(x16[r, :, r], t_bounce[1, q].rearrange("h i k -> i h k")).then_inc(t_in, 16)



_INS = ['L0_attn_x', 'L0_attn_w_qkv', 'L0_attn_b_qkv', 'L0_attn_w_proj', 'L0_attn_b_proj', 'L0_ffn_W1', 'L0_ffn_b1', 'L0_ffn_W2',
        'L0_ffn_b2', 'L0_ffn_Wg', 'L0_ffn_bg', 'L0_c', 'L0_wmod', 'L1_attn_Wq', 'L1_attn_Wk', 'L1_attn_Wv', 'L1_attn_Wg',
        'L1_attn_Wo', 'L1_attn_conv_q', 'L1_attn_conv_k', 'L1_attn_conv_v', 'L1_attn_Wgk', 'L1_attn_Wb', 'L1_attn_b_b',
        'L1_attn_A_log', 'L1_attn_dt_bias', 'L1_attn_g_norm_weight', 'L1_ffn_router_w', 'L1_ffn_w1', 'L1_ffn_b1', 'L1_ffn_w2',
        'L1_ffn_b2', 'L1_c', 'L1_wmod']
_OUT = ((8, 512, 128), 'float32')


def kernel(**inputs):
    import numpy as _np
    import concourse.bacc as _bacc
    from concourse import mybir as _mybir
    from concourse.bass_utils import run_bass_kernel_spmd as _run

    nc = _bacc.Bacc("TRN2", target_bir_lowering=False, num_devices=1)
    arrays, args = {}, []
    for name in _INS:
        a = _np.ascontiguousarray(inputs[name])
        arrays[f"in_{name}_dram"] = a
        args.append(nc.dram_tensor(f"in_{name}_dram", a.shape, _mybir.dt.from_np(a.dtype), kind="ExternalInput").ap())
    shape, dtype = _OUT
    args.append(nc.dram_tensor("out_dram", shape, _mybir.dt.from_np(_np.dtype(dtype)), kind="ExternalOutput").ap())
    adaln_two_layers(nc, *args)
    r = _run(nc, [arrays], core_ids=[0])
    return r.results[0]["out_dram"]
```

```python
from contextlib import ExitStack

import concourse.bass as bass
from concourse import mybir

F32 = mybir.dt.float32
BF16 = mybir.dt.bfloat16
U32 = mybir.dt.uint32
ALU = mybir.AluOpType
ACT = mybir.ActivationFunctionType
AX = mybir.AxisListType

P = 128
MASKED = -1.0e30
ENTER, LEAVE = (0, 3), 4
EXP_LN = "natural_log_exp_and_others"

IN_ROW = {
    "x_in": 16, "w_in": 32, "wc_in": 48, "gates_in": 16, "v_pads": 1, "xin_free": 1, "x_done": 1, "out_sent": 16,
    "ln_var": 4, "ln_rstd": 4, "ln_xn": 4, "ln_ps": 4, "h_ready": 4, "dve_step": 220, "act_step": 13, "pool_step": 0,
    "qk_ps": 2, "qk_f": 2, "qk_parts": 2, "v_ps": 1, "v_ready": 1, "parts_out": 32, "stacks_in": 304, "s_ps": 64,
    "s_max": 64, "m_parts": 2, "m_ps": 2, "m_sb": 2, "m_out": 32, "m_in_0": 16, "m_in_1": 16, "st_ps": 48,
    "p_ready": 48, "pv_ps": 16, "y_sb": 4, "yt_ps": 4, "y_norm": 4, "y2_ps": 1, "y2_sb": 1, "proj_ps": 1, "lg_ps": 1,
    "top_d": 1, "top_e": 1, "comb_ready": 1, "ct_ps": 1, "ct_sb": 1, "b2_ps": 1, "hid_ps": 16, "hid_sb": 16,
    "moe_ps": 8, "moe_acc": 8, "gb_ps": 1, "gb_z": 1, "gb_e": 1, "gk_ready": 1, "z_ps": 24, "tap0": 24, "taps": 24, "taps_added": 24,
    "qkv_t": 24, "vt_ps": 12, "v_tok": 12, "gm_ready": 4, "small_ps": 1, "kt_ps": 8, "qt_ps": 8, "dec_ready": 1,
    "k_sq": 8, "q_sq": 8, "ss_ready": 4, "rn_ready": 4, "khat_ready": 4, "kd_ready": 4, "lower_ps": 16, "l_ps": 12,
    "dt_ready": 12, "kh_ps": 8, "kh_ready": 8, "g_ps": 12, "gd_ready": 12, "qk2_ps": 12, "pt_ready": 12,
    "bm_ready": 12, "b_out": 512, "b_in": 64, "t_ready": 4, "t_out": 128, "t_in": 1024, "lv_ps": 96, "lv_16": 36,
    "lv_sb": 60, "ks_ps": 12, "r_ready": 12, "qs_ps": 12, "qse_ready": 12, "yd_ps": 12, "dl_ready": 12, "pd_ps": 12,
    "o_ready": 12, "su_ps": 6, "sd_ready": 3, "s_ready": 7, "gt_ps": 12, "gate_ready": 12, "osq_ready": 4,
    "ot_ready": 4, "of_ready": 4, "on_ready": 4, "og_ready": 4, "og_ps": 12, "ogt_ready": 12, "wo_ps": 4,
    "wo_done": 4, "rt_ps": 1, "rt_d": 1, "rt_e": 1, "rt_ready": 1, "f_ps": 4, "f_sb": 4, "f2_ps": 1,
}


def at(b, signal, k, ahead=0):
    return b * IN_ROW[signal.name] + ahead * IN_ROW[signal.name] + k


def wide(ap, shape):
    return ap.unsqueeze(len(ap.shape)).to_broadcast(shape)


def adaln_two_layers(nc, L0_attn_x, L0_attn_w_qkv, L0_attn_b_qkv, L0_attn_w_proj, L0_attn_b_proj, L0_ffn_W1, L0_ffn_b1,
                     L0_ffn_W2, L0_ffn_b2, L0_ffn_Wg, L0_ffn_bg, L0_c, L0_wmod, L1_attn_Wq, L1_attn_Wk, L1_attn_Wv,
                     L1_attn_Wg, L1_attn_Wo, L1_attn_conv_q, L1_attn_conv_k, L1_attn_conv_v, L1_attn_Wgk, L1_attn_Wb,
                     L1_attn_b_b, L1_attn_A_log, L1_attn_dt_bias, L1_attn_g_norm_weight, L1_ffn_router_w, L1_ffn_w1,
                     L1_ffn_b1, L1_ffn_w2, L1_ffn_b2, L1_c, L1_wmod, out):
    NB, T, D = L0_attn_x.shape
    NT = T // P
    HA, DA = 16, 8
    SA = DA ** -0.5
    PARTS = 3
    KS = PARTS * PARTS * DA
    NE, HID = L0_ffn_W1.shape[:2]
    HT = HID // P
    HD, DK, DV = 12, 64, 128
    NP = HD // 2
    NG, GH = 3, 4
    HS = [slice(0, 8, 2), slice(1, 8, 2), slice(8, 12)]
    BEFORE = [2, 2, 3]
    NQK, NCV = 2 * NP, 2 * NP + HD
    FT = L1_ffn_w1.shape[1] // P
    BS = 16
    NBK = P // BS

    with ExitStack() as ctx:
        def sb(name, shape, dt=F32):
            return ctx.enter_context(nc.sbuf_tensor(name, shape, dt))

        def dram(name, shape, dt=F32):
            return nc.dram_tensor(name, shape, dt).ap()

        PS = [ctx.enter_context(nc.psum_tensor(f"bank{i}", [P, 512], F32)) for i in range(8)]

        def sig(name):
            return ctx.enter_context(nc.semaphore(name))

        ident = sb("ident", [P, P])
        ident_bf = sb("ident_bf", [P, P], BF16)
        ones = sb("ones", [P, P])
        later = sb("later", [P, P])
        upto = sb("upto", [P, P])
        mask16 = sb("mask16", [P, P])
        mask_q = sb("mask_q", [P, P], BF16)
        mask_k = sb("mask_k", [P, GH, P], BF16)
        eye16 = sb("eye16", [NBK * HD, BS * BS])
        iota8 = sb("iota8", [P, NE])
        v_pad = sb("v_pad", [P, 32 - DA])
        eps5 = sb("eps5", [P, 1])
        eps6 = sb("eps6", [P, 1])
        wqkv = sb("wqkv", [P, 3 * D])
        wproj = sb("wproj", [P, D])
        wo = sb("wo", [P, HD, D])
        wgate = sb("wgate", [P, HD * DV])
        w1 = sb("w1", [P, FT * P])
        w2 = sb("w2", [P, FT, D])
        wgb = sb("wgb", [P, 2 * HD])
        router0 = sb("router0", [P, NE])
        router1 = sb("router1", [P, NE])
        conv = sb("conv", [P, NCV, 4])
        bqk = sb("bqk", [P, 2])
        bv = sb("bv", [P, D])
        dt_bias = sb("dt_bias", [P, HD])
        neg_a = sb("neg_a", [P, HD])
        beta_bias = sb("beta_bias", [P, HD])
        gnorm = sb("gnorm", [P, 1])
        b1e = sb("b1e", [P, NE * HT])
        b2e = sb("b2e", [NE, D])
        b1f = sb("b1f", [P, FT])
        rows1 = sb("rows1", [1, 2 * D + NE])
        bproj, b2f, bgate = rows1[0:1, 0:D], rows1[0:1, D:2 * D], rows1[0:1, 2 * D:2 * D + NE]
        mod_t = sb("mod_t", [P, 8, NB + 1])
        mod_b = sb("mod_b", [P, 8])
        mod_0 = sb("mod_0", [P, 2])
        xin = sb("xin", [P, NT, D])
        xs = sb("xs", [P, NT, D])
        xn = sb("xn", [P, NT, D])
        h_t = sb("h_t", [P, T])
        gates = sb("gates", [P, 4, D])
        st = sb("st", [P, NT, 6])
        mv = sb("mv", [P, 3, NT])
        rstd = sb("rstd", [P, NT])
        small = sb("small", [P, 512])

        vq = sb("vq", [P, NQK * T + NT * HD * DV])
        qk_t = vq[:, 0:NQK * T].rearrange("p (n t) -> p n t", t=T)
        v_all = vq[:, NQK * T:].rearrange("p (c h v) -> p c h v", c=NT, h=HD)
        half = HA * T // 2
        q_stack = vq[:, 0:half].bitcast(BF16).rearrange("p (h t) -> p h t", h=HA)
        k_stack = vq[:, half:2 * half].bitcast(BF16).rearrange("p (h t) -> p h t", h=HA)
        v32 = vq[:, 2 * half:2 * half + NT * HA * 32].rearrange("p (c h d) -> p c h d", c=NT, h=HA)
        o = 2 * half + NT * HA * 32
        y32 = vq[:, o:o + 4 * T].rearrange("p (g t) -> p g t", g=4)

        HW = HD * P
        arena = sb("arena", [P, 14 * HW])
        used = [0]

        def carve(n):
            used[0] += n
            return arena[:, used[0] - n:used[0]]

        def heads(ap, w=P):
            return ap.rearrange("p (h w) -> p h w", w=w)

        kd_a, kht_a, pt_a = carve(HW), carve(HW), carve(2 * HW)
        dec_a, bm_a, ub_a, t_a, x_a, rb_a, qse_a, dl_a, ob_a = [carve(HW) for _ in range(9)]
        khat_a, sd_a = carve(HW // 2), carve(HW // 2)
        kd = kd_a.rearrange("p (i h d) -> p i h d", i=2, h=HD)
        kh_t = kht_a.rearrange("p (i n t) -> p i n t", i=2, n=NP)
        pt = pt_a.rearrange("p (i h w) -> p i h w", i=2, h=HD)
        dt, bm, ub, tw, xw = heads(dec_a), heads(bm_a), heads(ub_a), heads(t_a), heads(x_a)
        h_0 = bm_a[:, 0:T]
        gm = ub
        rb, qse, dl, ob = heads(rb_a), heads(qse_a), heads(dl_a), heads(ob_a)
        osq, ogt, og = rb, xw, tw
        khat = khat_a
        sdec = sd_a.rearrange("p (n v) -> p n v", n=NP)
        ktok = sd_a
        ksq, qsq = dl_a[:, 0:HW // 2], dl_a[:, HW // 2:HW]
        state = sb("state", [P, NP, DV])
        t16 = sb("t16", [P, HD, P])
        x16 = sb("x16", [P, HD, P])
        u32 = sb("u32", [P, HD, P])
        u64 = sb("u64", [P, HD, DK])
        gate = tw
        bm2 = sb("bm2", [P, HD, P])
        bms = [bm, bm2]
        blk = sb("blk", [NBK * HD, BS * BS])
        blk_t = sb("blk_t", [NBK * HD, BS * BS])
        blk_x = sb("blk_x", [NBK * HD, BS * BS])
        blk_tmp = small
        gk = sb("gk", [P, NT, HD])
        beta = sb("beta", [P, NT, HD])
        dec = sb("dec", [P, NT, 2, HD])
        neg_dec = sb("neg_dec", [P, NT, HD])
        dec_end = sb("dec_end", [P, NT, NP])
        ssq = sb("ssq", [P, NT, 2 * HD])
        rn = sb("rn", [P, NT, 2 * HD])
        fac = sb("fac", [P, 3, HD])
        acc = arena[:, 8 * HW:8 * HW + 4 * T].rearrange("p (i t) -> p i t", i=4)
        acc2 = ob_a.rearrange("p (i t) -> p i t", i=3)
        v_t = arena[:, 8 * HW + 4 * T:8 * HW + 8 * T].rearrange("p (i t) -> p i t", i=4)
        wconv = arena[:, 6 * HW:8 * HW]
        assert NCV * P <= 2 * HW
        w1t = arena[:, 8 * HW:8 * HW + NE * HT * P].rearrange("p (n m) -> p n m", m=P)
        w2t = arena[:, 8 * HW + NE * HT * P:8 * HW + 2 * NE * HT * P].rearrange("p (n m) -> p n m", m=P)
        o = 8 * HW + 2 * NE * HT * P
        hid = arena[:, o:o + 2 * HT * T].rearrange("p (i j t) -> p i j t", i=2, j=HT)
        o += 2 * HT * T
        moe = arena[:, o:o + T].rearrange("p (c d) -> p c d", c=NT)
        o += T
        p_t = arena[:, 0:2 * 10 * P].rearrange("p (i w) -> p i w", i=2)
        qkf = arena[:, 2560:2560 + 2 * T].rearrange("p (i t) -> p i t", i=2)
        rest = arena[:, 3584:3584 + T]
        qkp = arena[:, 4096:4096 + PARTS * T].bitcast(BF16).rearrange("p (i n t) -> p i n t", i=2, n=PARTS)
        y_tok = arena[:, 5632:5632 + T].rearrange("p (c d) -> p c d", c=NT)
        y_t = arena[:, 6144:6144 + T]
        wide_t = arena[:, 6656:6656 + T].rearrange("p (c d) -> p c d", c=NT)
        hid1 = arena[:, 0:FT * T].rearrange("p (j t) -> p j t", j=FT)
        mx = sb("mx", [P, HA, NT])
        mrest = sb("mrest", [P, HA // 2 * NT])
        mparts = sb("mparts", [P, PARTS, HA // 2 * NT], BF16)
        m_t = sb("m_t", [PARTS * HA // 2 * NT, P], BF16)
        rec = sb("rec", [P, HA])
        lnv = sb("lnv", [P, NT])
        comb = sb("comb", [P, NT, NE])
        comb_t = arena[0:NE, o:o + T]
        idx = sb("idx", [P, NT, 8], U32)

        qk_bounce = dram("qk_bounce", [2, HA, DA, PARTS, T], BF16)
        m_bounce = dram("m_bounce", [2, PARTS, HA // 2 * T], BF16)
        b_bounce = dram("b_bounce", [NBK, HD, BS, BS])
        t_bounce = dram("t_bounce", [2, NBK, HD, BS, BS])
        w1_bounce = dram("w1_bounce", [P, NE * HT * P])
        w2_bounce = dram("w2_bounce", [P, NE * HT * P])
        gate_rows = dram("gate_rows", [NB, 4 * D])
        one_rows = dram("one_rows", [PARTS, HA * T], BF16)

        consts_in, masks_made, zeros_made, silu_c, prologue_ps, prologue_sb, rows_out, weights_out = [
            ctx.enter_context(nc.semaphore(n)) for n in
            ("consts_in", "masks_made", "zeros_made", "silu_c", "prologue_ps", "prologue_sb", "rows_out", "weights_out")]
        pool_pro, dve_pro, act_pro = [ctx.enter_context(nc.semaphore(n)) for n in ("pool_pro", "dve_pro", "act_pro")]

        x_in, w_in, wc_in, gates_in = sig("x_in"), sig("w_in"), sig("wc_in"), sig("gates_in")
        v_pads = sig("v_pads")
        xin_free, x_done, out_sent = sig("xin_free"), sig("x_done"), sig("out_sent")
        ln_var, ln_rstd, ln_xn, ln_ps, h_ready = [sig(n) for n in ("ln_var", "ln_rstd", "ln_xn", "ln_ps", "h_ready")]
        dve_step, act_step = sig("dve_step"), sig("act_step")
        qk_ps, qk_f, qk_parts, v_ps, v_ready, parts_out, stacks_in = [sig(n) for n in (
            "qk_ps", "qk_f", "qk_parts", "v_ps", "v_ready", "parts_out", "stacks_in")]
        s_ps, s_max, m_parts, m_ps, m_sb, m_out = [sig(n) for n in (
            "s_ps", "s_max", "m_parts", "m_ps", "m_sb", "m_out")]
        m_in = [sig("m_in_0"), sig("m_in_1")]
        st_ps, p_ready, pv_ps, y_sb, yt_ps, y_norm, y2_ps, y2_sb, proj_ps = [sig(n) for n in (
            "st_ps", "p_ready", "pv_ps", "y_sb", "yt_ps", "y_norm", "y2_ps", "y2_sb", "proj_ps")]
        lg_ps, top_d, top_e, comb_ready, ct_ps, ct_sb, b2_ps, hid_ps, hid_sb, moe_ps, moe_acc = [sig(n) for n in (
            "lg_ps", "top_d", "top_e", "comb_ready", "ct_ps", "ct_sb", "b2_ps", "hid_ps", "hid_sb", "moe_ps", "moe_acc")]
        gb_ps, gb_z, gb_e, gk_ready = [sig(n) for n in ("gb_ps", "gb_z", "gb_e", "gk_ready")]
        z_ps, tap0, taps, taps_added, qkv_t, vt_ps, v_tok = [sig(n) for n in (
            "z_ps", "tap0", "taps", "taps_added", "qkv_t", "vt_ps", "v_tok")]
        gm_ready, small_ps, kt_ps, qt_ps, dec_ready, k_sq, q_sq, ss_ready, rn_ready, khat_ready, kd_ready = [
            sig(n) for n in ("gm_ready", "small_ps", "kt_ps", "qt_ps", "dec_ready", "k_sq", "q_sq", "ss_ready",
                             "rn_ready", "khat_ready", "kd_ready")]
        lower_ps = sig("lower_ps")
        l_ps, dt_ready, kh_ps, kh_ready, g_ps, gd_ready, qk2_ps, pt_ready, bm_ready = [sig(n) for n in (
            "l_ps", "dt_ready", "kh_ps", "kh_ready", "g_ps", "gd_ready", "qk2_ps", "pt_ready", "bm_ready")]
        b_out, b_in, t_ready, t_out, t_in = [sig(n) for n in ("b_out", "b_in", "t_ready", "t_out", "t_in")]
        lv_ps, lv_16, lv_sb = [sig(n) for n in ("lv_ps", "lv_16", "lv_sb")]
        ks_ps, r_ready, qs_ps, qse_ready, yd_ps, dl_ready, pd_ps, o_ready, su_ps, sd_ready, s_ready = [sig(n) for n in (
            "ks_ps", "r_ready", "qs_ps", "qse_ready", "yd_ps", "dl_ready", "pd_ps", "o_ready", "su_ps", "sd_ready", "s_ready")]
        gt_ps, gate_ready, osq_ready, ot_ready, of_ready, on_ready, og_ready, og_ps, ogt_ready, wo_ps, wo_done = [
            sig(n) for n in ("gt_ps", "gate_ready", "osq_ready", "ot_ready", "of_ready", "on_ready", "og_ready", "og_ps",
                             "ogt_ready", "wo_ps", "wo_done")]
        rt_ps, rt_d, rt_e, rt_ready, f_ps, f_sb, f2_ps = [sig(n) for n in (
            "rt_ps", "rt_d", "rt_e", "rt_ready", "f_ps", "f_sb", "f2_ps")]

        ln_bank = PS[0]
        qk_banks, v_bank = PS[6:8], PS[5]
        yt_banks, y2_bank, proj_bank = PS[0:4], PS[4], PS[5]
        max_banks = [PS[7], PS[6]]

        def score_bank(n):
            return PS[n % 6 if n < 32 else n % 3]

        def score_t_bank(h, i):
            return PS[3 + i if h < 8 or h % 2 else i]

        def y_bank(g):
            return PS[6 + g % 2]

        logit_bank, comb_bank, b2_bank = PS[1], PS[0], PS[1]

        def hid_bank(n):
            return PS[2 + n % 4]

        def moe_bank(e):
            return PS[6 + e % 2]

        gb_bank = PS[1]

        def z_bank(n):
            return PS[2 + n % 3]

        def vt_bank(i):
            return PS[6 + i % 2]

        dec_bank, few_banks = PS[5], [PS[0], PS[1], PS[5]]

        def k_banks(c):
            return few_banks if c == 1 else PS[6:8]

        def q_banks(c):
            return PS[0:2]

        def l_banks(c):
            return few_banks if c < 2 else PS[2:5]

        def g_banks(c):
            return few_banks if c < 2 else PS[0:3]

        def qk2_banks(c):
            return few_banks if c < 2 else PS[3:6]

        low_banks, high_banks, ks_banks, su_banks = PS[0:3], PS[3:6], PS[5:8], PS[6:8]
        gate_banks, og_banks, wo_bank = PS[2:5], PS[5:8], PS[3]

        def level_bank(s, g):
            return PS[s % 2 * 3 + g]

        def f_bank(j):
            return PS[2 + j]

        f2_bank = PS[6]

        stages = []
        for c in range(NT):
            stages.append(("levels", c))
            if c == 0:
                stages.append(("values", 1))
            if c + 1 == NT:
                stages += [("enter_stats", 1), ("rms", c - 1), ("enter_norm", 1), ("gate", c - 1)]
            elif c:
                stages += [("rms", c - 1), ("gate", c - 1)]
            if c + 1 < NT:
                stages.append(("subst", c + 1))
            if c:
                stages.append(("scale", c - 1))
            if c + 1 == NT:
                stages.append(("enter_h", 1))
            if c + 2 < NT:
                stages.append(("norm", c + 2))
            stages.append(("scan", c))
            if c:
                stages.append(("project", c - 1))
            if c + 2 < NT:
                stages.append(("gram", c + 2))
        stages += [("enter_qkv", 1), ("rms", NT - 1), ("enter_k", 1), ("gate", NT - 1), ("scale", NT - 1), ("project", NT - 1)]
        Z_LEAD = 3
        TOK_LAG, V_LAG = 6, 3
        LAST_V = NCV - 4
        stops = [NQK + 1, NQK + 5, NQK + 9, NCV]
        tap_stops = [NQK + 4, NQK + 8, NCV]
        add_stops = [NQK + 1, NQK + 4, NCV]

        def lots(stops):
            return [range(a, z) for a, z in zip([0] + stops, stops)]

        pe_act_stages = [("conv", 0), ("norm", 0), ("gram", 0), ("conv", 1), ("norm", 1), ("conv", 2), ("values", 0),
                         ("gram", 1), ("conv", 3)] + stages
        dve_stages = [("conv", 0), ("norm", 0), ("gram", 0), ("conv", 1), ("subst", 0), ("norm", 1), ("conv", 2), ("gram", 1)] + stages
        pool_stages = [("conv", 0), ("norm", 0), ("conv", 1), ("gram", 0), ("norm", 1), ("conv", 2), ("gram", 1)]
        for name, c in stages:
            at_scale = len(pool_stages) - (pool_stages[-1][0] == "scale")
            pool_stages.insert(at_scale if name == "norm" else len(pool_stages), (name, c))

        const_loads = [
            (wqkv[:, :], L0_attn_w_qkv), (wproj[:, :], L0_attn_w_proj),
            (wo[:, :, :], L1_attn_Wo.rearrange("(h v) n -> v h n", h=HD)), (wgate[:, :], L1_attn_Wg),
            (w1[:, :], L1_ffn_w1), (w2[:, :, :], L1_ffn_w2.rearrange("(j p) n -> p j n", p=P)),
            (wgb[:, 0:HD], L1_attn_Wgk), (wgb[:, HD:2 * HD], L1_attn_Wb),
            (router0[:, :], L0_ffn_Wg.rearrange("e d -> d e")), (router1[:, :], L1_ffn_router_w),
            (conv[:, 0:NP, :], L1_attn_conv_q.rearrange("(n p) k -> p n k", p=P)),
            (conv[:, NP:NQK, :], L1_attn_conv_k.rearrange("(n p) k -> p n k", p=P)),
            (conv[:, NQK:NCV, :], L1_attn_conv_v.rearrange("(n p) k -> p n k", p=P)),
            (bqk[:, :], L0_attn_b_qkv[0:2 * D].rearrange("(s m) -> m s", s=2)),
            (bv[:, :], L0_attn_b_qkv[2 * D:3 * D].partition_broadcast(P)),
            (dt_bias[:, :], L1_attn_dt_bias.partition_broadcast(P)),
            (neg_a[:, :], L1_attn_A_log.partition_broadcast(P)),
            (beta_bias[:, :], L1_attn_b_b.partition_broadcast(P)),
            (gnorm[:, :], L1_attn_g_norm_weight.rearrange("(v a) -> v a", a=1)),
            (b1e[:, :].rearrange("p (e j) -> p e j", j=HT), L0_ffn_b1.rearrange("e (j p) -> p e j", p=P)),
            (b2e[:, :], L0_ffn_b2), (b1f[:, :], L1_ffn_b1.rearrange("(j p) -> p j", p=P)),
            (bproj, L0_attn_b_proj.rearrange("(a n) -> a n", a=1)), (b2f, L1_ffn_b2.rearrange("(a n) -> a n", a=1)),
            (bgate, L0_ffn_bg.rearrange("(a n) -> a n", a=1)),
        ]
        c_t = small[:, 0:2 * NB].rearrange("p (l b) -> p l b", l=2)
        w1raw = arena[:, 0:NE * HT * P].rearrange("p (n m) -> p n m", m=P)
        w2raw = arena[:, NE * HT * P:2 * NE * HT * P].rearrange("p (n m) -> p n m", m=P)
        wmod = arena[:, 2 * NE * HT * P:2 * NE * HT * P + 12 * D].rearrange("p (l j d) -> p l j d", l=2, j=6)
        g_rows = vq[0:NB, 0:4 * D]
        g_tmp = vq[0:NB, 4 * D:8 * D]
        const_loads += [
            (c_t[:, 0, :], L0_c.rearrange("b d -> d b")), (c_t[:, 1, :], L1_c.rearrange("b d -> d b")),
            (wmod[:, 0], L0_wmod.rearrange("p (j d) -> p j d", j=6)), (wmod[:, 1], L1_wmod.rearrange("p (j d) -> p j d", j=6)),
            (w1raw.rearrange("p (e j) d -> p e j d", j=HT), L0_ffn_W1.rearrange("e (j p) d -> p e j d", p=P)),
            (w2raw.rearrange("p (e j) m -> p e j m", j=HT), L0_ffn_W2.rearrange("e o (j m) -> o e j m", m=P)),
        ]
        CONSTS = 16 * len(const_loads)
        NW = NE * HT

        ctx.enter_context(nc.allow_non_contiguous_dma("small constants, and blocks that change partitions"))
        block = ctx.enter_context(nc.Block())

        @block.tensor
        def _(pe):
            mm, tr = nc.tensor.matmul, nc.tensor.transpose

            pe.wait_ge(consts_in, CONSTS)
            pe.wait_ge(silu_c, 1)
            pe.wait_ge(masks_made, 1)
            for i, (l, j) in enumerate([(l, j) for l in range(2) for j in (0, 1, 3, 4)]):
                mm(PS[0][:, i * NB:(i + 1) * NB], wmod[:, l, j, :], c_t[:, l, :], start=True, stop=True)
            for l in range(2):
                last = mm(PS[1][0:NB, l * 2 * D:(l + 1) * 2 * D].rearrange("b (j d) -> b j d", j=2), c_t[:, l, :],
                          wmod[:, l, 2::3, :], start=True, stop=True)
            last.then_inc(prologue_ps, 1)
            for i in range(2 * NW):
                n = i // 4
                if i % 4 == 0 and n >= 6:
                    pe.wait_ge(prologue_sb, n - 6 + 2)
                raw = w1raw if i < NW else w2raw
                last = tr(PS[2 + n % 6][:, i % 4 * P:(i % 4 + 1) * P], raw[:, i % NW, :], ident[:, :])
                if i % 4 == 3:
                    last.then_inc(prologue_ps, 1)
            pe.wait_ge(prologue_sb, 1 + 2 * NW // 4)

            def transpose_norm(b, k):
                pe.wait_ge(ln_xn, at(b, ln_xn, k + 1))
                for t in range(NT):
                    last = tr(ln_bank[:, t * P:(t + 1) * P], xn[:, t, :], ident[:, :])
                last.then_inc(ln_ps, 1)

            def enter_norm(b, ahead):
                transpose_norm(b, ENTER[ahead])

            def enter_qkv(b, ahead):
                pe.wait_ge(h_ready, at(b, h_ready, ENTER[ahead] + 1))
                for i in range(2):
                    mm(qk_banks[i][:, :], wqkv[:, i * D:(i + 1) * D], h_0, start=True, stop=True).then_inc(qk_ps, 1)
                for t in range(NT):
                    last = mm(v_bank[:, t * D:(t + 1) * D], h_0[:, t * P:(t + 1) * P], wqkv[:, 2 * D:3 * D], start=True, stop=True)
                last.then_inc(v_ps, 1)

            enter_norm(0, 0)
            enter_qkv(0, 0)

            with pe.Fori(0, NB) as b:
                lowers = [0]

                def layer_norm(k):
                    transpose_norm(b, k)
                    pe.wait_ge(h_ready, at(b, h_ready, k + 1))

                def lower():
                    lowers[0] += 1
                    return at(b, lower_ps, lowers[0])

                pe.wait_ge(stacks_in, at(b, stacks_in, 16 * (2 * PARTS * PARTS + 1)))
                pe.wait_ge(v_ready, at(b, v_ready, 1))
                pe.wait_ge(v_pads, at(b, v_pads, 1))

                def scores(h):
                    for t in range(NT):
                        n = h * NT + t
                        ps, e = score_bank(n), (t + 1) * P
                        if n >= 32:
                            pe.wait_ge(s_max, at(b, s_max, n - 2))
                        elif n >= 6:
                            pe.wait_ge(s_max, at(b, s_max, n - 5))
                        mm(ps[:, 0:e], q_stack[0:KS, h, t * P:e], k_stack[0:KS, h, 0:e], start=True, stop=False)
                        mm(ps[:, t * P:e], ident_bf[:, :], mask_q[:, :], start=False, stop=True).then_inc(s_ps, 1)

                def move_maxima(hh):
                    pe.wait_ge(m_parts, at(b, m_parts, hh + 1))
                    if hh == 0:
                        pe.wait_ge(x_done, at(b, x_done, 1))
                    if hh:
                        pe.wait_ge(y_sb, at(b, y_sb, 1))
                    ps = max_banks[hh]
                    tr(ps[0:96, 0:P // 2].bitcast(BF16), mparts[:, :, :].rearrange("p n m -> p (n m)"), ident_bf[:, :]).then_inc(m_ps, 1)

                def scores_t(h):
                    if h % 8 == 0:
                        pe.wait_ge(m_in[h // 8], at(b, m_in[h // 8], 16))
                    lots = [[0], [1], [2, 3]]
                    for i, lot in enumerate(lots):
                        ps, c0 = score_t_bank(h, i), 0
                        if h >= 9:
                            pe.wait_ge(p_ready, at(b, p_ready, 3 * (h - 2) + i + 1))
                        elif 1 <= h < 8:
                            pe.wait_ge(p_ready, at(b, p_ready, 3 * (h - 1) + i + 1))
                        for j in lot:
                            n = T - j * P
                            mm(ps[:, c0:c0 + n], k_stack[0:KS + PARTS, h, j * P:(j + 1) * P], q_stack[0:KS + PARTS, h, j * P:T],
                               start=True, stop=False)
                            last = mm(ps[:, c0:c0 + P], ident_bf[:, :], mask_k[:, 0, :], start=False, stop=True)
                            c0 += n
                        last.then_inc(st_ps, 1)

                def weigh(h):
                    g, r = h // 4, 32 * (h % 4)
                    if h % 4 == 0 and g >= 2:
                        pe.wait_ge(y_sb, at(b, y_sb, g - 1))
                    pe.wait_ge(p_ready, at(b, p_ready, 3 * h + 3))
                    c0 = 0
                    for j in range(NT):
                        n = T - j * P
                        last = mm(y_bank(g)[r:r + 32, j * P:T], v32[:, j, h, :], p_t[:, h % 2, c0:c0 + n],
                                  start=(j == 0), stop=(j == NT - 1))
                        c0 += n
                    last.then_inc(pv_ps, 1)

                for h in range(10):
                    scores(h)
                move_maxima(0)
                scores(10)
                for h in range(11, HA):
                    scores(h)
                    scores_t(h - 11)
                    if h > 11:
                        weigh(h - 12)
                move_maxima(1)
                for h in range(HA - 11, HA):
                    scores_t(h)
                    weigh(h - 1)
                weigh(HA - 1)
                pe.wait_ge(y_sb, at(b, y_sb, 4))
                for t in range(NT):
                    ps = yt_banks[t]
                    for g in range(4):
                        last = tr(ps[:, g * P:(g + 1) * P], y32[:, g, t * P:(t + 1) * P], ident[:, :])
                    last.then_inc(yt_ps, 1)
                ps = y2_bank
                for t in range(NT):
                    pe.wait_ge(y_norm, at(b, y_norm, t + 1))
                    last = tr(ps[:, t * P:(t + 1) * P], y_tok[:, t, :], ident[:, :])
                last.then_inc(y2_ps, 1)
                pe.wait_ge(y2_sb, at(b, y2_sb, 1))
                ps = proj_bank
                for t in range(NT):
                    mm(ps[:, t * D:(t + 1) * D], y_t[:, t * P:(t + 1) * P], wproj[:, :], start=True, stop=False)
                    last = mm(ps[:, t * D:(t + 1) * D], ones[0:1, :], bproj, start=False, stop=True)
                last.then_inc(proj_ps, 1)

                layer_norm(1)
                ps = logit_bank
                for t in range(NT):
                    mm(ps[:, t * NE:(t + 1) * NE], h_t[:, t * P:(t + 1) * P], router0[:, :], start=True, stop=False)
                    last = mm(ps[:, t * NE:(t + 1) * NE], ones[0:1, :], bgate, start=False, stop=True)
                last.then_inc(lg_ps, 1)
                pe.wait_ge(w_in, at(b, w_in, 32))

                def expert_in(e):
                    for j in range(HT):
                        n = e * HT + j
                        ps = hid_bank(n)
                        if n >= 4:
                            pe.wait_ge(hid_sb, at(b, hid_sb, n - 3))
                        mm(ps[:, :], w1t[:, n, :], h_t[:, :], start=True, stop=True).then_inc(hid_ps, 1)

                def expert_out(e):
                    pe.wait_ge(hid_sb, at(b, hid_sb, HT * (e + 1)))
                    ps = moe_bank(e)
                    if e >= 2:
                        pe.wait_ge(moe_acc, at(b, moe_acc, e - 1))
                    for t in range(NT):
                        for j in range(HT):
                            last = mm(ps[:, t * D:(t + 1) * D], hid[:, e % 2, j, t * P:(t + 1) * P], w2t[:, e * HT + j, :],
                                      start=(j == 0), stop=(j == HT - 1))
                    last.then_inc(moe_ps, 1)

                expert_in(0)
                expert_in(1)
                pe.wait_ge(comb_ready, at(b, comb_ready, 1))
                ps = comb_bank
                for t in range(NT):
                    last = tr(ps[0:NE, t * P:(t + 1) * P], comb[:, t, :], ident[:, :])
                last.then_inc(ct_ps, 1)
                expert_out(0)
                pe.wait_ge(ct_sb, at(b, ct_sb, 1))
                ps = b2_bank
                for t in range(NT):
                    last = mm(ps[:, t * D:(t + 1) * D], comb_t[0:NE, t * P:(t + 1) * P], b2e[:, :], start=True, stop=True)
                last.then_inc(b2_ps, 1)
                for e in range(1, NE):
                    if e + 1 < NE:
                        expert_in(e + 1)
                    expert_out(e)

                layer_norm(2)
                ps = gb_bank
                for t in range(NT):
                    last = mm(ps[:, t * 2 * HD:(t + 1) * 2 * HD], h_t[:, t * P:(t + 1) * P], wgb[:, :], start=True, stop=True)
                last.then_inc(gb_ps, 1)

                def to_tokens(n):
                    i = n - NQK
                    pe.wait_ge(qkv_t, at(b, qkv_t, n + 1))
                    ps = vt_bank(i)
                    if i == 0:
                        pe.wait_ge(kh_ready, at(b, kh_ready, 2))
                    elif i >= 2:
                        pe.wait_ge(v_tok, at(b, v_tok, i - 1))
                    for t in range(NT):
                        last = tr(ps[:, t * P:(t + 1) * P], v_t[:, n % 4, t * P:(t + 1) * P], ident[:, :])
                    last.then_inc(vt_ps, 1)

                def decays():
                    pe.wait_ge(gk_ready, at(b, gk_ready, 1))
                    steps_of = gk[:, :, :].rearrange("p c h -> p (c h)")
                    for k, mask in enumerate((upto, later, ones)):
                        last = mm(dec_bank[:, k * NT * HD:(k + 1) * NT * HD], mask[:, :], steps_of, start=True, stop=True)
                    last.then_inc(small_ps, 1)

                pe.wait_ge(wc_in, at(b, wc_in, 48))
                def convolve(i):
                    tiles = lots(stops)[i]
                    for n in range(tiles.start + (Z_LEAD if i else 0), min(tiles.stop + Z_LEAD, NCV)):
                        if n == Z_LEAD:
                            decays()
                        if n >= NQK + TOK_LAG:
                            to_tokens(n - TOK_LAG)
                        ps = z_bank(n)
                        if n >= 3:
                            pe.wait_ge(taps, at(b, taps, n - 2))
                        mm(ps[:, :], wconv[:, n * P:(n + 1) * P], h_t[:, :], start=True, stop=True).then_inc(z_ps, 1)

                def values(i):
                    for n in range(LAST_V, NCV) if i else range(NCV - TOK_LAG, LAST_V):
                        to_tokens(n)

                def norm(c):
                    sl = slice(c * P, (c + 1) * P)
                    if c == 0:
                        pe.wait_ge(qkv_t, at(b, qkv_t, NQK))
                    elif c == 1:
                        pe.wait_ge(pt_ready, at(b, pt_ready, NG))
                    else:
                        pe.wait_ge(lv_sb, at(b, lv_sb, 5 * NG * (c - 1)))
                    if c == 2:
                        pe.wait_ge(v_tok, at(b, v_tok, HD))
                    for x, first, done in (("k", NP, kt_ps), ("q", 0, qt_ps)):
                        for i, lot in enumerate((range(0, 4), range(4, NP))):
                            if c == 1 and x == "q":
                                pe.wait_ge(k_sq, at(b, k_sq, 2 * c + i + 1))
                            ps = (k_banks if x == "k" else q_banks)(c)[i]
                            for j in lot:
                                last = tr(ps[:, j % 4 * P:(j % 4 + 1) * P], qk_t[:, first + j, sl], ident[:, :])
                            last.then_inc(done, 1)
                    pe.wait_ge(gm_ready, at(b, gm_ready, c + 1))
                    for g in range(NG):
                        if c < 2 and g == 0:
                            pe.wait_ge(q_sq, at(b, q_sq, 2 * (c + 1)))
                            pe.wait_ge(dec_ready, at(b, dec_ready, 1))
                        elif c >= 3:
                            pe.wait_ge(gate_ready, at(b, gate_ready, NG * (c - 3) + g + 1))
                        ps = l_banks(c)[g]
                        mm(ps[:, :], later[:, :], gm[:, GH * g:GH * (g + 1), :].rearrange("p h w -> p (h w)"), start=True, stop=False)
                        mm(ps[:, :], ident_bf[:, :], mask_k[:, :, :].rearrange("p h w -> p (h w)"), start=False, stop=True).then_inc(l_ps, 1)

                def key_rows(g):
                    order = [0, 2, 1, 3] if g == 2 else range(GH)
                    return [(j, h, slice(DK * (h % 2), DK * (h % 2) + DK)) for j in order for h in [range(HD)[HS[g]][j]]]

                def gram(c):
                    sl = slice(c * P, (c + 1) * P)
                    pe.wait_ge(khat_ready, at(b, khat_ready, c + 1))
                    if c == 1:
                        pe.wait_ge(dt_ready, at(b, dt_ready, NG * (c + 1)))
                    elif c > 2:
                        pe.wait_ge(ogt_ready, at(b, ogt_ready, NG * (c - 2)))
                    elif c == 2:
                        pe.wait_ge(s_ready, at(b, s_ready, 3))
                    for i, lot in enumerate((range(0, 4), range(4, NP))):
                        ps = k_banks(c)[i]
                        for j in lot:
                            last = tr(ps[:, j % 4 * P:(j % 4 + 1) * P], khat[:, j * P:(j + 1) * P], ident[:, :])
                        last.then_inc(kh_ps, 1)
                    pe.wait_ge(kh_ready, at(b, kh_ready, 2 * c + 2))
                    if c == 0:
                        pe.wait_ge(dt_ready, at(b, dt_ready, NG))
                    if c >= 2:
                        pe.wait_ge(o_ready, at(b, o_ready, NG * (c - 1)))
                    if c > 2:
                        pe.wait_ge(wo_done, at(b, wo_done, c - 2))
                    for name, done, banks in (("g", g_ps, g_banks(c)), ("qk2", qk2_ps, qk2_banks(c))):
                        for g in range(NG):
                            if c < 2 and name == "qk2":
                                pe.wait_ge(gd_ready, at(b, gd_ready, NG * c + g + 1))
                            ps = banks[g]
                            for j, h, rows in key_rows(g):
                                rhs = kh_t[rows, c % 2, h // 2, :] if name == "g" else qk_t[rows, h // 2, sl]
                                last = mm(ps[:, j * P:(j + 1) * P], kh_t[rows, c % 2, h // 2, :], rhs, start=True, stop=True)
                                if h == 10:
                                    last.then_inc(lower_ps, 1)
                                    pe.wait_ge(lower_ps, lower())
                            last.then_inc(done, 1)

                def levels(c):
                    n16, nsb = 3 * NG * c, 5 * NG * c
                    pe.wait_ge(t_in, at(b, t_in, 16 * 16 * (c + 1)))
                    pe.wait_ge(bm_ready, at(b, bm_ready, NG * (c + 1)))
                    if c == 0:
                        pe.wait_ge(taps, at(b, taps, NCV))
                    if c + 1 < NT:
                        pe.wait_ge(gd_ready, at(b, gd_ready, NG * (c + 2)))
                        pe.wait_ge(pt_ready, at(b, pt_ready, NG * (c + 2)))
                    else:
                        pe.wait_ge(o_ready, at(b, o_ready, NG * c))
                    for s in range(8):
                        for g in range(NG):
                            if s == 1 and g == 0 and c + 1 == NT:
                                pe.wait_ge(wo_done, at(b, wo_done, c - 1))
                            if s == 1:
                                pe.wait_ge(lv_16, at(b, lv_16, n16 + g + 1))
                            elif s == 3:
                                pe.wait_ge(lv_16, at(b, lv_16, n16 + 2 * NG + g + 1))
                            elif s == 4:
                                pe.wait_ge(lv_sb, at(b, lv_sb, nsb + g + 1))
                            elif s == 6:
                                pe.wait_ge(lv_sb, at(b, lv_sb, nsb + NG + g + 1))
                            elif s == 7:
                                pe.wait_ge(lv_sb, at(b, lv_sb, nsb + 3 * NG + g + 1))
                            ps = level_bank(s, g)
                            for j in range(GH):
                                h = GH * g + j
                                at_j, at_d = slice(j * P, (j + 1) * P), slice(j * DK, (j + 1) * DK)
                                if s == 0:
                                    last = mm(ps[:, at_j], bms[c % 2][:, h, :], t16[:, h, :], start=True, stop=True)
                                elif s == 1:
                                    last = mm(ps[:, at_j], ub[:, h, :], x16[:, h, :], start=True, stop=True)
                                elif s == 2:
                                    last = mm(ps[:, at_j], x16[:, h, :], ub[:, h, :], start=True, stop=True)
                                elif s in (3, 4, 5) and (j or s == 5):
                                    for q in (0, 64) if s != 4 else (0,):
                                        up, low = slice(q, q + 32), slice(q + 32, q + 64)
                                        if s == 3:
                                            out_at, lhs, rhs = ps[low, j * P + q:j * P + q + 32], bms[c % 2][up, h, low], tw[up, h, up]
                                        elif s == 4:
                                            out_at, lhs, rhs = ps[low, j * P + q:j * P + q + 32], xw[low, h, low], u32[low, h, up]
                                        else:
                                            out_at, lhs, rhs = ps[up, j * P + q + 32:j * P + q + 64], u32[low, h, up], xw[low, h, low]
                                        last = mm(out_at, lhs, rhs, start=True, stop=True)
                                elif s == 3:
                                    last = mm(ps[:, at_j], bms[c % 2][:, h, :], tw[:, h, :], start=True, stop=True)
                                elif s == 4:
                                    last = mm(ps[:, at_j], xw[:, h, :], u32[:, h, :], start=True, stop=True)
                                elif s == 6:
                                    last = mm(ps[:, at_d], bms[c % 2][0:DK, h, :], tw[0:DK, h, 0:DK], start=True, stop=True)
                                else:
                                    last = mm(ps[0:DK, at_d], u64[:, h, :], xw[:, h, DK:P], start=True, stop=True)
                            last.then_inc(lv_ps, 1)

                def gate_proj(c):
                    for g in range(NG):
                        if c + 1 == NT:
                            if g == 0:
                                pe.wait_ge(o_ready, at(b, o_ready, NG * NT))
                                pe.wait_ge(wo_done, at(b, wo_done, NT - 1))
                        elif g:
                            pe.wait_ge(lv_sb, at(b, lv_sb, 5 * NG * (c + 1) + 4 * NG + g))
                        ps = gate_banks[g]
                        mm(ps[:, :], h_t[:, c * P:(c + 1) * P], wgate[:, g * 512:(g + 1) * 512], start=True, stop=True).then_inc(gt_ps, 1)

                def scan(c):
                    sl = slice(c * P, (c + 1) * P)
                    pe.wait_ge(s_ready, at(b, s_ready, 2 * c + 1))
                    if c + 1 == NT:
                        pe.wait_ge(h_ready, at(b, h_ready, ENTER[1] + 1))
                    if c + 2 < NT:
                        pe.wait_ge(k_sq, at(b, k_sq, 2 * (c + 3)))
                    else:
                        pe.wait_ge(lv_sb, at(b, lv_sb, 5 * NG * (c + 1)))
                        pe.wait_ge(gate_ready, at(b, gate_ready, NG * c))
                    for name, done, banks in (("ks", ks_ps, ks_banks), ("qs", qs_ps, low_banks)):
                        if name == "qs" and c + 2 < NT:
                            pe.wait_ge(q_sq, at(b, q_sq, 2 * (c + 3)))
                            pe.wait_ge(dt_ready, at(b, dt_ready, NG * (c + 3)))
                        for g in range(NG):
                            ps = banks[g]
                            for j, h, rows in key_rows(g):
                                lhs = kh_t[rows, c % 2, h // 2, :] if name == "ks" else qk_t[rows, h // 2, sl]
                                last = mm(ps[:, j * P:(j + 1) * P], lhs, state[rows, h // 2, :], start=True, stop=True)
                                if h == 10:
                                    last.then_inc(lower_ps, 1)
                                    pe.wait_ge(lower_ps, lower())
                            last.then_inc(done, 1)
                    for g in range(NG):
                        if g == 0 and c + 2 < NT:
                            pe.wait_ge(lv_sb, at(b, lv_sb, 5 * NG * (c + 1)))
                        pe.wait_ge(r_ready, at(b, r_ready, NG * c + g + 1))
                        ps = high_banks[g]
                        for j, h, rows in key_rows(g):
                            last = mm(ps[:, j * P:(j + 1) * P], xw[:, h, :], rb[:, h, :], start=True, stop=True)
                        last.then_inc(yd_ps, 1)
                    if c + 1 < NT:
                        pe.wait_ge(kd_ready, at(b, kd_ready, c + 1))
                        for i, lot in enumerate((range(0, 4), range(4, NP))):
                            pe.wait_ge(dl_ready, at(b, dl_ready, NG * c + (2 if i == 0 else 3)))
                            ps = su_banks[i]
                            for n in lot:
                                for s in range(2):
                                    last = mm(ps[DK * s:DK * (s + 1), n % 4 * DV:(n % 4 + 1) * DV], kd[:, c % 2, 2 * n + s, :],
                                              dl[:, 2 * n + s, :], start=True, stop=True)
                            last.then_inc(su_ps, 1)
                    for g in range(NG):
                        if c + 1 == NT:
                            pe.wait_ge(dl_ready, at(b, dl_ready, NG * c + g + 1))
                        pe.wait_ge(qse_ready, at(b, qse_ready, NG * c + g + 1))
                        ps = low_banks[g]
                        for j, h, rows in key_rows(g):
                            last = mm(ps[:, j * P:(j + 1) * P], pt[:, c % 2, h, :], dl[:, h, :], start=True, stop=True)
                        last.then_inc(pd_ps, 1)

                def project(c):
                    pe.wait_ge(og_ready, at(b, og_ready, c + 1))
                    for g in range(NG):
                        if g == 0 and c + 2 < NT:
                            pe.wait_ge(s_ready, at(b, s_ready, 2 * c + 5))
                        elif g == 0 and c + 1 == NT:
                            pe.wait_ge(qk_f, at(b, qk_f, 2, 1))
                            pe.wait_ge(v_ready, at(b, v_ready, 1, 1))
                        ps = og_banks[g]
                        for j in range(GH):
                            last = tr(ps[:, j * P:(j + 1) * P], og[:, GH * g + j, :], ident[:, :])
                        last.then_inc(og_ps, 1)
                    ps = wo_bank
                    pe.wait_ge(ogt_ready, at(b, ogt_ready, NG * (c + 1)))
                    for h in range(HD):
                        last = mm(ps[:, 0:D], ogt[:, h, :], wo[:, h, :], start=(h == 0), stop=(h == HD - 1))
                    last.then_inc(wo_ps, 1)

                walk = {"conv": convolve, "values": values, "norm": norm, "gram": gram, "levels": levels, "project": project,
                        "gate": gate_proj, "scan": scan,
                        "enter_norm": lambda ahead: enter_norm(b, ahead), "enter_qkv": lambda ahead: enter_qkv(b, ahead)}
                for name, c in pe_act_stages:
                    if name in walk:
                        walk[name](c)

                layer_norm(LEAVE)
                ps = logit_bank
                for t in range(NT):
                    last = mm(ps[:, t * NE:(t + 1) * NE], h_t[:, t * P:(t + 1) * P], router1[:, :], start=True, stop=True)
                last.then_inc(rt_ps, 1)
                for j in range(FT):
                    mm(f_bank(j)[:, :], w1[:, j * P:(j + 1) * P], h_t[:, :], start=True, stop=True).then_inc(f_ps, 1)
                pe.wait_ge(f_sb, at(b, f_sb, FT))
                ps = f2_bank
                for t in range(NT):
                    for j in range(FT):
                        mm(ps[:, t * D:(t + 1) * D], hid1[:, j, t * P:(t + 1) * P], w2[:, j, :], start=(j == 0), stop=False)
                    last = mm(ps[:, t * D:(t + 1) * D], ones[0:1, :], b2f, start=False, stop=True)
                last.then_inc(f2_ps, 1)
                pe.wait_ge(rt_d, at(b, rt_d, 1))

        @block.vector
        def _(dve):
            V = nc.vector
            pro = [0]

            def then(ins):
                pro[0] += 1
                ins.then_inc(dve_pro, 1)
                dve.wait_ge(dve_pro, pro[0])

            dve.wait_ge(prologue_ps, 1)
            mod4 = mod_t[:, :, :].rearrange("p (n k) b -> p n k b", k=2)
            ps4 = PS[0][:, 0:8 * NB].rearrange("p (n k b) -> p n k b", k=2, b=NB)
            V.tensor_copy(mod4[:, :, 0, 0:NB], ps4[:, :, 0, :])
            then(V.tensor_scalar(mod4[:, :, 1, 0:NB], ps4[:, :, 1, :], 1.0, None, ALU.add))
            V.tensor_copy(mod_t[:, :, NB:NB + 1], mod_t[:, :, 0:1])
            then(V.tensor_copy(g_tmp, PS[1][0:NB, :]))
            then(V.scalar_tensor_tensor(g_rows, g_tmp, -1.0, g_tmp, ALU.mult, ALU.max))
            then(V.tensor_scalar(g_rows, g_rows, 0.25, None, ALU.max))
            then(V.tensor_scalar(g_tmp, g_tmp, 0.0, 2.0, ALU.is_ge, ALU.mult))
            V.scalar_tensor_tensor(g_rows, g_tmp, -1.0, g_rows, ALU.add, ALU.mult).then_inc(prologue_sb, 1)
            for n in range(2 * NW // 4):
                dve.wait_ge(prologue_ps, n + 2)
                dst = w1t if n < NW // 4 else w2t
                V.tensor_copy(dst[:, n % (NW // 4) * 4:n % (NW // 4) * 4 + 4, :],
                              PS[2 + n % 6][:, :].rearrange("p (n m) -> p n m", m=P)).then_inc(prologue_sb, 1)
            dve.wait_ge(consts_in, CONSTS)
            dve.wait_ge(act_pro, 1)
            V.tensor_scalar(neg_a[:, :], neg_a[:, :], -1.0, None, ALU.mult)
            then(V.tensor_scalar(wo[:, :, :], wo[:, :, :], gnorm[:, 0:1], None, ALU.mult))
            V.memset(t16[:, :, :], 0.0)
            V.memset(x16[:, :, :], 0.0)
            V.memset(u64[0:DK, :, :], 0.0)
            V.memset(u32[:, :, :], 0.0).then_inc(xin_free, 1)
            V.memset(k_stack[0:PARTS, :, :], 1.0).then_inc(prologue_sb, 1)
            V.memset(mrest[:, :], 0.0).then_inc(x_done, 1)

            row, steps = [0], [0]

            def step():
                steps[0] += 1
                return at(row[0], dve_step, steps[0])

            def statistics(b, k, src):
                for t in range(NT):
                    last = V.bn_stats(st[:, t, :], src[:, t, :])
                last.then_inc(dve_step, 1)
                dve.wait_ge(dve_step, step())
                V.tensor_tensor(mv[:, 0, :], st[:, :, 1], st[:, :, 4], ALU.add)
                V.tensor_tensor(mv[:, 2, :], st[:, :, 2], st[:, :, 5], ALU.add)
                V.tensor_tensor(mv[:, 1, :], st[:, :, 1], st[:, :, 4], ALU.subtract).then_inc(dve_step, 1)
                dve.wait_ge(dve_step, step())
                V.tensor_scalar(mv[:, 0, :], mv[:, 0, :], 0.5, None, ALU.mult)
                V.scalar_tensor_tensor(mv[:, 1, :], mv[:, 1, :], D / 4.0, mv[:, 1, :], ALU.mult, ALU.mult).then_inc(dve_step, 1)
                dve.wait_ge(dve_step, step())
                V.tensor_tensor(mv[:, 1, :], mv[:, 1, :], mv[:, 2, :], ALU.add).then_inc(ln_var, 1)

            def normalise(b, k, src):
                dve.wait_ge(ln_rstd, at(b, ln_rstd, k + 1))
                for t in range(NT):
                    last = V.tensor_scalar(xn[:, t, :], src[:, t, :], mv[:, 0, t:t + 1], rstd[:, t:t + 1], ALU.subtract, ALU.mult)
                last.then_inc(ln_xn, 1)

            def modulate(b, k, dst, mod):
                dve.wait_ge(ln_ps, at(b, ln_ps, k + 1))
                V.tensor_scalar(dst, ln_bank[:, :], mod[:, 1:2], mod[:, 0:1], ALU.mult, ALU.add).then_inc(h_ready, 1)

            def enter_stats(b, ahead):
                dve.wait_ge(x_in, at(b, x_in, 16, ahead))
                V.tensor_copy(mod_0[:, :], mod_t[:, 0:2, bass.ds(b + ahead, 1)].rearrange("p n a -> p (n a)")).then_inc(dve_step, 1)
                dve.wait_ge(dve_step, step())
                statistics(b, ENTER[ahead], xin)

            def enter_norm(b, ahead):
                normalise(b, ENTER[ahead], xin)

            def enter_h(b, ahead):
                modulate(b, ENTER[ahead], h_0, mod_0[:, :])

            def parts(b, ahead, i):
                dve.wait_ge(qk_f, at(b, qk_f, i + 1, ahead))
                f = qkf[:, i, :]
                V.tensor_copy(qkp[:, i, 0, :], f).then_inc(dve_step, 1)
                dve.wait_ge(dve_step, step())
                V.tensor_tensor(rest, f, qkp[:, i, 0, :], ALU.subtract).then_inc(dve_step, 1)
                dve.wait_ge(dve_step, step())
                V.tensor_copy(qkp[:, i, 1, :], rest).then_inc(dve_step, 1)
                dve.wait_ge(dve_step, step())
                V.tensor_tensor(qkp[:, i, 2, :], rest, qkp[:, i, 1, :], ALU.subtract).then_inc(qk_parts, 1)
                dve.wait_ge(qk_parts, at(b, qk_parts, i + 1, ahead))

            def enter_qkv(b, ahead):
                parts(b, ahead, 0)
                dve.wait_ge(v_ps, at(b, v_ps, 1, ahead))
                V.tensor_tensor(v32[:, :, :, 0:DA], v_bank[:, :].rearrange("p (c h d) -> p c h d", c=NT, h=HA),
                                bv[:, :].rearrange("p (h d) -> p h d", h=HA).unsqueeze(1).to_broadcast([P, NT, HA, DA]), ALU.add).then_inc(v_ready, 1)

            def enter_k(b, ahead):
                parts(b, ahead, 1)

            for stage in (enter_stats, enter_norm, enter_h, enter_qkv, enter_k):
                stage(0, 0)

            with dve.Fori(0, NB) as b:
                row[0] = b
                V.tensor_copy(mod_b[:, :], mod_t[:, :, bass.ds(b, 1)].rearrange("p n a -> p (n a)")).then_inc(dve_step, 1)
                dve.wait_ge(dve_step, step())

                def layer_norm(k, src):
                    statistics(b, k, src)
                    normalise(b, k, src)
                    modulate(b, k, h_t[:, :], mod_b[:, 2 * min(k, 3):2 * min(k, 3) + 2])

                def gate_row(i):
                    return gates[:, i, :].unsqueeze(1).to_broadcast([P, NT, D])

                def tiles(ps):
                    return ps[:, :].rearrange("p (c d) -> p c d", c=NT)

                for hh in range(2):
                    for h in range(8 * hh, 8 * hh + 8):
                        for t in range(NT):
                            n = h * NT + t
                            dve.wait_ge(s_ps, at(b, s_ps, n + 1))
                            last = V.reduce_max(mx[:, h, t:t + 1], score_bank(n)[:, 0:(t + 1) * P], AX.X)
                            last.then_inc(s_max, 1)
                    m = mx[:, 8 * hh:8 * hh + 8, :].rearrange("p h c -> p (h c)")
                    dve.wait_ge(s_max, at(b, s_max, 32 * (hh + 1)))
                    if hh:
                        dve.wait_ge(m_ps, at(b, m_ps, 1))
                    V.tensor_scalar(mparts[:, 0, :], m, -1.0, None, ALU.mult).then_inc(dve_step, 1)
                    dve.wait_ge(dve_step, step())
                    V.scalar_tensor_tensor(mrest[:, :], m, -1.0, mparts[:, 0, :], ALU.mult, ALU.subtract).then_inc(dve_step, 1)
                    dve.wait_ge(dve_step, step())
                    V.tensor_copy(mparts[:, 1, :], mrest[:, :]).then_inc(dve_step, 1)
                    dve.wait_ge(dve_step, step())
                    V.tensor_tensor(mparts[:, 2, :], mrest[:, :], mparts[:, 1, :], ALU.subtract).then_inc(m_parts, 1)
                for t in range(NT):
                    dve.wait_ge(yt_ps, at(b, yt_ps, t + 1))
                    ps = yt_banks[t][:, :].rearrange("p (h d) -> p h d", d=32)
                    V.reciprocal(rec[:, :], ps[:, :, DA]).then_inc(dve_step, 1)
                    dve.wait_ge(dve_step, step())
                    V.tensor_tensor(y_tok[:, t, :].rearrange("p (h d) -> p h d", d=DA), ps[:, :, 0:DA],
                                       wide(rec[:, :], [P, HA, DA]), ALU.mult).then_inc(y_norm, 1)
                    dve.wait_ge(y_norm, at(b, y_norm, t + 1))
                dve.wait_ge(proj_ps, at(b, proj_ps, 1))
                dve.wait_ge(gates_in, at(b, gates_in, 16))
                dve.wait_ge(out_sent, at(b, out_sent, 16))
                V.tensor_tensor(wide_t, tiles(proj_bank), gate_row(0), ALU.mult).then_inc(dve_step, 1)
                dve.wait_ge(dve_step, step())
                V.tensor_tensor(xs[:, :, :], xin[:, :, :], wide_t, ALU.add).then_inc(xin_free, 1)
                dve.wait_ge(xin_free, at(b, xin_free, 2))

                layer_norm(1, xs)
                logits = small[:, 0:NT * NE].rearrange("p (c e) -> p c e", c=NT)
                top = small[:, 32:64].rearrange("p (c e) -> p c e", c=NT)
                pos = small[:, 64:96].rearrange("p (c e) -> p c e", c=NT)
                diff, wt, com2 = small[:, 96:100], small[:, 100:108].rearrange("p (i c) -> p i c", i=2), small[:, 128:160].rearrange("p (c e) -> p c e", c=NT)
                dve.wait_ge(lg_ps, at(b, lg_ps, 1))
                raw = logit_bank[:, 0:NT * NE].rearrange("p (c e) -> p c e", c=NT)
                V.tensor_copy(logits, raw)
                for t in range(NT):
                    last = V.max(top[:, t, :], raw[:, t, :])
                last.then_inc(dve_step, 1)
                dve.wait_ge(dve_step, step())
                V.tensor_tensor(diff, top[:, :, 1], top[:, :, 0], ALU.subtract).then_inc(top_d, 1)
                for t in range(NT):
                    last = V.max_index(idx[:, t, :], top[:, t, :], logits[:, t, :])
                last.then_inc(dve_step, 1)
                dve.wait_ge(dve_step, step())
                V.tensor_copy(pos, idx[:, :, :])
                dve.wait_ge(top_e, at(b, top_e, 1))
                ex = small[:, 108:112]
                V.tensor_scalar(diff, ex, 1.0, None, ALU.add).then_inc(dve_step, 1)
                dve.wait_ge(dve_step, step())
                V.reciprocal(wt[:, 0, :], diff).then_inc(dve_step, 1)
                dve.wait_ge(dve_step, step())
                V.tensor_tensor(wt[:, 1, :], ex, wt[:, 0, :], ALU.mult).then_inc(dve_step, 1)
                dve.wait_ge(dve_step, step())
                for t in range(NT):
                    V.tensor_scalar(comb[:, t, :], iota8[:, :], pos[:, t, 0:1], wt[:, 0, t:t + 1], ALU.is_equal, ALU.mult)
                    last = V.tensor_scalar(com2[:, t, :], iota8[:, :], pos[:, t, 1:2], wt[:, 1, t:t + 1], ALU.is_equal, ALU.mult)
                last.then_inc(dve_step, 1)
                dve.wait_ge(dve_step, step())
                V.tensor_tensor(comb[:, :, :], comb[:, :, :], com2, ALU.add).then_inc(comb_ready, 1)
                dve.wait_ge(comb_ready, at(b, comb_ready, 1))
                dve.wait_ge(b2_ps, at(b, b2_ps, 1))
                V.tensor_copy(moe, tiles(b2_bank)).then_inc(dve_step, 1)
                dve.wait_ge(dve_step, step())
                for e in range(NE):
                    dve.wait_ge(moe_ps, at(b, moe_ps, e + 1))
                    if e:
                        dve.wait_ge(moe_acc, at(b, moe_acc, e))
                    for t in range(NT):
                        last = V.scalar_tensor_tensor(moe[:, t, :], moe_bank(e)[:, t * D:(t + 1) * D], comb[:, t, e:e + 1],
                                                      moe[:, t, :], ALU.mult, ALU.add)
                    last.then_inc(moe_acc, 1)
                dve.wait_ge(moe_acc, at(b, moe_acc, NE))
                V.tensor_tensor(moe, moe, gate_row(1), ALU.mult).then_inc(dve_step, 1)
                dve.wait_ge(dve_step, step())
                V.tensor_tensor(xs[:, :, :], xs[:, :, :], moe, ALU.add).then_inc(dve_step, 1)
                dve.wait_ge(dve_step, step())

                layer_norm(2, xs)
                V.memset(state[:, :, :], 0.0).then_inc(s_ready, 1)
                dve.wait_ge(gb_ps, at(b, gb_ps, 1))
                ps = gb_bank[:, 0:NT * 2 * HD].rearrange("p (c k h) -> p c k h", c=NT, k=2)

                def over_tiles(row):
                    return row[:, :].unsqueeze(1).to_broadcast([P, NT, HD])

                def scratch(i):
                    return small[:, 192 + i * 48:240 + i * 48].rearrange("p (c h) -> p c h", c=NT)
                z, az, zb, ln1 = scratch(0), scratch(1), scratch(2), scratch(3)
                V.tensor_tensor(zb, ps[:, :, 1, :], over_tiles(beta_bias), ALU.add)
                V.tensor_tensor(z, ps[:, :, 0, :], over_tiles(dt_bias), ALU.add).then_inc(dve_step, 1)
                dve.wait_ge(dve_step, step())
                V.scalar_tensor_tensor(az, z, -1.0, z, ALU.mult, ALU.min).then_inc(gb_z, 1)
                dve.wait_ge(gb_e, at(b, gb_e, 1))
                V.scalar_tensor_tensor(z, z, 0.0, ln1, ALU.max, ALU.add).then_inc(dve_step, 1)
                dve.wait_ge(dve_step, step())
                V.tensor_tensor(gk[:, :, :], z, over_tiles(neg_a), ALU.mult)
                V.tensor_scalar(zb, zb, 1.0, None, ALU.add).then_inc(dve_step, 1)
                dve.wait_ge(dve_step, step())
                V.reciprocal(beta[:, :, :], zb).then_inc(gk_ready, 1)
                def convolve(i):
                    for n in lots(tap_stops)[i]:
                        dve.wait_ge(tap0, at(b, tap0, n + 1))
                        ps, a = z_bank(n), acc[:, n % 4, :]
                        for k in (2, 3):
                            ins = V.scalar_tensor_tensor(a[:, k:T], ps[:, 0:T - k], conv[:, n, 3 - k:4 - k], a[:, k:T], ALU.mult, ALU.add)
                            if k < 3:
                                ins.then_inc(dve_step, 1)
                                dve.wait_ge(dve_step, step())
                        ins.then_inc(taps, 1)

                def norm(c):
                    dve.wait_ge(k_sq, at(b, k_sq, 2 * c + 2))
                    V.reduce_sum(ssq[:, c, HD:2 * HD], ksq.rearrange("p (h d) -> p h d", d=DK), AX.X)
                    dve.wait_ge(q_sq, at(b, q_sq, 2 * c + 2))
                    V.reduce_sum(ssq[:, c, 0:HD], qsq.rearrange("p (h d) -> p h d", d=DK), AX.X).then_inc(ss_ready, 1)
                    if c == 0:
                        dve.wait_ge(dec_ready, at(b, dec_ready, 1))
                        V.tensor_scalar(neg_dec[:, :, :], dec[:, :, 0, :], -1.0, None, ALU.mult)
                    dve.wait_ge(rn_ready, at(b, rn_ready, c + 1))
                    if c:
                        dve.wait_ge(kd_ready, at(b, kd_ready, c))
                        dve.wait_ge(kh_ps, at(b, kh_ps, 2 * c))
                    V.tensor_tensor(khat.rearrange("p (h d) -> p h d", d=DK), ktok.rearrange("p (h d) -> p h d", d=DK),
                                       wide(rn[:, c, HD:2 * HD], [P, HD, DK]), ALU.mult).then_inc(khat_ready, 1)

                def gram(c):
                    for g, hs in enumerate(HS):
                        dve.wait_ge(g_ps, at(b, g_ps, NG * c + g + 1))
                        if g != 1:
                            dve.wait_ge(dt_ready, at(b, dt_ready, NG * c + BEFORE[g]))
                        if c >= 2 and g == 0:
                            dve.wait_ge(lv_ps, at(b, lv_ps, 24 * (c - 2) + 21))
                            dve.wait_ge(b_out, at(b, b_out, 16 * NBK * (c - 1)))
                        V.tensor_tensor(bms[c % 2][:, hs, :], g_banks(c)[g][:, :].rearrange("p (h t) -> p h t", h=GH), dt[:, hs, :], ALU.mult).then_inc(gd_ready, 1)
                    for g, hs in enumerate(HS):
                        dve.wait_ge(qk2_ps, at(b, qk2_ps, NG * c + g + 1))
                        V.tensor_tensor(pt[:, c % 2, hs, :], qk2_banks(c)[g][:, :].rearrange("p (h t) -> p h t", h=GH), dt[:, hs, :], ALU.mult).then_inc(pt_ready, 1)

                def subst(c):
                    dve.wait_ge(b_in, at(b, b_in, 16 * (c + 1)))
                    if c:
                        dve.wait_ge(t_out, at(b, t_out, 32 * c))
                    V.tensor_copy(blk_t[:, :], eye16[:, :]).then_inc(dve_step, 1)
                    dve.wait_ge(dve_step, step())
                    cols = blk_t[:, :].rearrange("p (k c) -> p c k", c=BS)
                    a = blk[:, :].rearrange("p (k i) -> p i k", i=BS)
                    for i in range(1, BS):
                        tmp = blk_tmp[0:NBK * HD, 0:i * i].rearrange("p (c k) -> p c k", k=i)
                        V.tensor_tensor(tmp, cols[:, 0:i, 0:i], a[:, i, 0:i].unsqueeze(1).to_broadcast([NBK * HD, i, i]), ALU.mult).then_inc(dve_step, 1)
                        dve.wait_ge(dve_step, step())
                        V.tensor_reduce(blk_t[:, i * BS:i * BS + i], tmp, AX.X, ALU.add, negate=True).then_inc(dve_step, 1)
                        dve.wait_ge(dve_step, step())
                    V.tensor_copy(blk_x[:, :].rearrange("p (c k) -> p c k", k=BS), cols).then_inc(t_ready, 1)

                def levels(c):
                    n16 = 3 * NG * c
                    dve.wait_ge(t_in, at(b, t_in, 16 * 16 * (c + 1)))
                    for s in range(3):
                        for g in range(NG):
                            hs = slice(GH * g, GH * (g + 1))
                            dve.wait_ge(lv_ps, at(b, lv_ps, 24 * c + NG * s + g + 1))
                            ps = level_bank(s, g)[:, :].rearrange("p (h t) -> p h t", h=GH)
                            if s == 0:
                                if g == 0 and c + 1 < NT:
                                    dve.wait_ge(l_ps, at(b, l_ps, NG * (c + 2)))
                                ins = V.tensor_tensor(ub[:, hs, :], ps, mask16[:, :].unsqueeze(1).to_broadcast([P, GH, P]), ALU.mult)
                            elif s == 1:
                                if c == 0 and g == 0:
                                    dve.wait_ge(qkv_t, at(b, qkv_t, NCV))
                                if c and g == 0:
                                    dve.wait_ge(yd_ps, at(b, yd_ps, NG * c))
                                if c >= 2 and g == 0:
                                    dve.wait_ge(wo_ps, at(b, wo_ps, c - 1))
                                ins = V.tensor_tensor(xw[:, hs, :], x16[:, hs, :], ps, ALU.subtract)
                            else:
                                ins = V.tensor_tensor(tw[:, hs, :], t16[:, hs, :], ps, ALU.subtract)
                            ins.then_inc(lv_16, 1)

                def scan(c):
                    for g in range(NG):
                        dve.wait_ge(ks_ps, at(b, ks_ps, NG * c + g + 1))
                        ps = ks_banks[g]
                        for j, h in enumerate(range(HD)[HS[g]]):
                            ins = V.scalar_tensor_tensor(rb[:, h, :], ps[:, j * P:(j + 1) * P], neg_dec[:, c, h:h + 1], v_all[:, c, h, :], ALU.mult, ALU.add)
                        ins.then_inc(r_ready, 1)
                    if c + 1 < NT:
                        dve.wait_ge(sd_ready, at(b, sd_ready, c + 1))
                        for i in range(2):
                            dve.wait_ge(su_ps, at(b, su_ps, 2 * c + i + 1))
                            if i == 0:
                                dve.wait_ge(qs_ps, at(b, qs_ps, NG * (c + 1)))
                            ns = slice(4 * i, min(4 * i + 4, NP))
                            n = ns.stop - ns.start
                            V.tensor_tensor(state[:, ns, :], su_banks[i][:, 0:n * DV].rearrange("p (n v) -> p n v", n=n), sdec[:, ns, :], ALU.add).then_inc(s_ready, 1)
                    for g, hs in enumerate(HS):
                        dve.wait_ge(pd_ps, at(b, pd_ps, NG * c + g + 1))
                        dve.wait_ge(qse_ready, at(b, qse_ready, NG * c + g + 1))
                        if c and g == 0:
                            dve.wait_ge(og_ready, at(b, og_ready, c))
                        V.tensor_tensor(ob[:, hs, :], low_banks[g][:, :].rearrange("p (h t) -> p h t", h=GH), qse[:, hs, :], ALU.add).then_inc(o_ready, 1)

                def rms(c):
                    dve.wait_ge(osq_ready, at(b, osq_ready, c + 1))
                    V.reduce_sum(fac[:, 0, :], osq, AX.X).then_inc(dve_step, 1)
                    dve.wait_ge(dve_step, step())
                    V.tensor_scalar(fac[:, 1, :], rn[:, c, 0:HD], DK ** -0.5, None, ALU.mult).then_inc(dve_step, 1)
                    dve.wait_ge(dve_step, step())
                    V.tensor_tensor(fac[:, 2, :], fac[:, 1, :], fac[:, 1, :], ALU.mult).then_inc(dve_step, 1)
                    dve.wait_ge(dve_step, step())
                    V.tensor_tensor(fac[:, 0, :], fac[:, 0, :], fac[:, 2, :], ALU.mult).then_inc(ot_ready, 1)

                def scale(c):
                    dve.wait_ge(of_ready, at(b, of_ready, c + 1))
                    V.tensor_tensor(fac[:, 1, :], fac[:, 1, :], fac[:, 2, :], ALU.mult).then_inc(dve_step, 1)
                    dve.wait_ge(dve_step, step())
                    V.tensor_tensor(ob, ob, wide(fac[:, 1, :], [P, HD, DV]), ALU.mult).then_inc(on_ready, 1)

                def project(c):
                    dve.wait_ge(wo_ps, at(b, wo_ps, c + 1))
                    V.tensor_tensor(wide_x(c), wo_bank[:, 0:D], gates[:, 2, :], ALU.mult).then_inc(dve_step, 1)
                    dve.wait_ge(dve_step, step())
                    V.tensor_tensor(xs[:, c, :], xs[:, c, :], wide_x(c), ALU.add).then_inc(wo_done, 1)

                def wide_x(c):
                    return xn[:, c, :]

                walk = {"conv": convolve, "norm": norm, "gram": gram, "subst": subst, "levels": levels, "scan": scan, "rms": rms, "scale": scale,
                        "project": project}
                for stage in (enter_stats, enter_norm, enter_h, enter_qkv, enter_k):
                    walk[stage.__name__] = lambda ahead, stage=stage: stage(b, ahead)
                for name, c in dve_stages:
                    if name in walk:
                        walk[name](c)
                dve.wait_ge(wo_done, at(b, wo_done, NT))

                layer_norm(LEAVE, xs)
                top = small[:, 32:64].rearrange("p (c e) -> p c e", c=NT)
                ex = small[:, 64:96].rearrange("p (c e) -> p c e", c=NT)
                tot, r1 = small[:, 96:100], small[:, 100:104]
                p2 = small[:, 104:112].rearrange("p (c i) -> p c i", c=NT)
                dve.wait_ge(rt_ps, at(b, rt_ps, 1))
                logits = logit_bank[:, 0:NT * NE].rearrange("p (c e) -> p c e", c=NT)
                V.reduce_max(tot, logits, AX.X).then_inc(dve_step, 1)
                dve.wait_ge(dve_step, step())
                V.tensor_tensor(ex, logits, wide(tot, [P, NT, NE]), ALU.subtract).then_inc(rt_d, 1)
                dve.wait_ge(rt_e, at(b, rt_e, 1))
                V.reduce_sum(tot, ex, AX.X)
                for t in range(NT):
                    last = V.max(top[:, t, :], ex[:, t, :])
                last.then_inc(dve_step, 1)
                dve.wait_ge(dve_step, step())
                V.reciprocal(r1, tot).then_inc(dve_step, 1)
                dve.wait_ge(dve_step, step())
                V.tensor_tensor(p2, top[:, :, 0:2], wide(r1, [P, NT, 2]), ALU.mult).then_inc(dve_step, 1)
                dve.wait_ge(dve_step, step())
                V.tensor_tensor(tot, p2[:, :, 0], p2[:, :, 1], ALU.add).then_inc(dve_step, 1)
                dve.wait_ge(dve_step, step())
                V.reciprocal(r1, tot).then_inc(dve_step, 1)
                dve.wait_ge(dve_step, step())
                V.tensor_tensor(p2, p2, wide(r1, [P, NT, 2]), ALU.mult).then_inc(dve_step, 1)
                dve.wait_ge(dve_step, step())
                V.tensor_tensor(tot, p2[:, :, 0], p2[:, :, 1], ALU.add).then_inc(rt_ready, 1)
                dve.wait_ge(rt_ready, at(b, rt_ready, 1))
                dve.wait_ge(f2_ps, at(b, f2_ps, 1))
                V.tensor_tensor(xn[:, :, :], tiles(f2_bank), wide(tot, [P, NT, D]), ALU.mult).then_inc(dve_step, 1)
                dve.wait_ge(dve_step, step())
                V.tensor_tensor(xn[:, :, :], xn[:, :, :], gate_row(3), ALU.mult).then_inc(dve_step, 1)
                dve.wait_ge(dve_step, step())
                V.tensor_tensor(xs[:, :, :], xs[:, :, :], xn[:, :, :], ALU.add).then_inc(x_done, 1)

        @block.scalar
        def _(act):
            A = nc.scalar
            act.wait_ge(consts_in, CONSTS)
            A.activation(c_t, c_t, ACT.Silu).then_inc(silu_c, 1)
            A.activation(neg_a[:, :], neg_a[:, :], ACT.Exp).then_inc(act_pro, 1)
            act.wait_ge(masks_made, 1)

            row, steps = [0], [0]

            def step():
                steps[0] += 1
                return at(row[0], act_step, steps[0])

            def deviation(b, k):
                act.wait_ge(ln_var, at(b, ln_var, k + 1))
                A.activation(lnv[:, :], mv[:, 1, :], ACT.Ln, scale=1.0 / D, bias=eps5[:, 0:1]).then_inc(act_step, 1)
                act.wait_ge(act_step, step())
                A.activation(rstd[:, :], lnv[:, :], ACT.Exp, scale=-0.5).then_inc(ln_rstd, 1)

            def enter_stats(b, ahead):
                deviation(b, ENTER[ahead])

            def enter_qkv(b, ahead):
                for i in range(2):
                    act.wait_ge(qk_ps, at(b, qk_ps, i + 1, ahead))
                    A.activation(qkf[:, i, :], qk_banks[i][:, :], ACT.Identity, bias=bqk[:, i:i + 1]).then_inc(qk_f, 1)

            nc.scalar.preload_act_table_set(EXP_LN)
            enter_stats(0, 0)
            enter_qkv(0, 0)

            with act.Fori(0, NB) as b:
                row[0] = b
                nc.scalar.preload_act_table_set(EXP_LN)

                def layer_norm(k):
                    deviation(b, k)

                def copy_maxima(hh):
                    act.wait_ge(m_ps, at(b, m_ps, hh + 1))
                    if hh:
                        act.wait_ge(m_out, at(b, m_out, 16))
                    A.copy(m_t[:, :], max_banks[hh][0:96, 0:P // 2].bitcast(BF16)).then_inc(m_sb, 1)

                def copy_y(g):
                    act.wait_ge(pv_ps, at(b, pv_ps, 4 * g + 4))
                    A.copy(y32[:, g, :], y_bank(g)[:, :]).then_inc(y_sb, 1)

                copy_maxima(0)
                for h in range(HA):
                    if h == 5:
                        copy_maxima(1)
                    if h >= 2 and h % 4 != 1:
                        act.wait_ge(pv_ps, at(b, pv_ps, h - 1))
                    c0 = 0
                    for i, n in enumerate((T, T - P, T - 2 * P + P)):
                        act.wait_ge(st_ps, at(b, st_ps, 3 * h + i + 1))
                        A.activation(p_t[:, h % 2, c0:c0 + n], score_t_bank(h, i)[:, 0:n], ACT.Exp, scale=SA).then_inc(p_ready, 1)
                        c0 += n
                    if h % 4 == 0 and h:
                        copy_y(h // 4 - 1)
                copy_y(3)
                act.wait_ge(y2_ps, at(b, y2_ps, 1))
                A.copy(y_t, y2_bank[:, :]).then_inc(y2_sb, 1)

                layer_norm(1)
                act.wait_ge(top_d, at(b, top_d, 1))
                A.activation(small[:, 108:112], small[:, 96:100], ACT.Exp).then_inc(top_e, 1)
                for n in range(NE * HT):
                    if n == 2 * HT:
                        act.wait_ge(ct_ps, at(b, ct_ps, 1))
                        A.copy(comb_t[:, :], comb_bank[0:NE, :]).then_inc(ct_sb, 1)
                    act.wait_ge(hid_ps, at(b, hid_ps, n + 1))
                    if n >= 2 * HT and n % HT == 0:
                        act.wait_ge(moe_ps, at(b, moe_ps, n // HT - 1))
                    A.activation(hid[:, n // HT % 2, n % HT, :], hid_bank(n)[:, :], ACT.Relu, bias=b1e[:, n:n + 1]).then_inc(hid_sb, 1)

                layer_norm(2)
                az, zb, ln1 = [small[:, 192 + i * 48:240 + i * 48] for i in (1, 2, 3)]
                act.wait_ge(gb_z, at(b, gb_z, 1))
                A.activation(zb, zb, ACT.Exp, scale=-1.0)
                A.activation(az, az, ACT.Exp).then_inc(act_step, 1)
                act.wait_ge(act_step, step())
                A.activation(ln1, az, ACT.Ln, bias=ones[:, 0:1]).then_inc(gb_e, 1)

                def first_tap(n):
                    act.wait_ge(z_ps, at(b, z_ps, n + 1))
                    if n >= 4:
                        act.wait_ge(qkv_t, at(b, qkv_t, n - 3))
                    A.activation(acc[:, n % 4, :], z_bank(n)[:, :], ACT.Identity, scale=conv[:, n, 3:4])
                    A.activation(acc2[:, n % 3, 0:T - 1], z_bank(n)[:, 0:T - 1], ACT.Identity, scale=conv[:, n, 2:3]).then_inc(tap0, 1)

                def silu(n):
                    act.wait_ge(taps_added, at(b, taps_added, n + 1))
                    if n >= NQK + 4:
                        act.wait_ge(vt_ps, at(b, vt_ps, n - NQK - 3))
                    dst = qk_t[:, n, :] if n < NQK else v_t[:, n % 4, :]
                    A.activation(dst, acc[:, n % 4, :], ACT.Silu).then_inc(qkv_t, 1)

                def copy_v(i):
                    act.wait_ge(vt_ps, at(b, vt_ps, i + 1))
                    A.copy(v_all[:, :, i, :], vt_bank(i)[:, :].rearrange("p (c v) -> p c v", c=NT)).then_inc(v_tok, 1)

                def decays():
                    act.wait_ge(small_ps, at(b, small_ps, 1))
                    sums = dec_bank[:, 0:3 * NT * HD].rearrange("p (k c h) -> p k c h", k=3, c=NT)
                    for k in range(2):
                        A.activation(dec[:, :, k, :], sums[:, k, :, :], ACT.Exp)
                    A.activation(dec_end[0:DK, :, :], sums[0:DK, 2, :, 0::2], ACT.Exp)
                    A.activation(dec_end[DK:P, :, :], sums[DK:P, 2, :, 1::2], ACT.Exp).then_inc(dec_ready, 1)

                def convolve(i):
                    if i == 0:
                        for n in range(Z_LEAD):
                            first_tap(n)
                        decays()
                    nc.scalar.preload_act_table_set("silu_and_others")
                    for n in lots(stops)[i]:
                        silu(n)
                        if n + Z_LEAD < NCV:
                            first_tap(n + Z_LEAD)
                        if NQK <= n - V_LAG < LAST_V:
                            copy_v(n - NQK - V_LAG)
                    nc.scalar.preload_act_table_set(EXP_LN)

                def values(i):
                    for n in range(LAST_V, NCV) if i else ():
                        copy_v(n - NQK)

                def norm(c):
                    if c:
                        act.wait_ge(khat_ready, at(b, khat_ready, c))
                    if c >= 3:
                        act.wait_ge(s_ready, at(b, s_ready, 1 + 2 * (c - 2)))
                    for i, n in enumerate((512, 256)):
                        act.wait_ge(kt_ps, at(b, kt_ps, 2 * c + i + 1))
                        ps = k_banks(c)[i]
                        A.copy(ktok[:, 512 * i:512 * i + n], ps[:, 0:n])
                        A.activation(ksq[:, 512 * i:512 * i + n], ps[:, 0:n], ACT.Square).then_inc(k_sq, 1)
                    for i, n in enumerate((512, 256)):
                        act.wait_ge(qt_ps, at(b, qt_ps, 2 * c + i + 1))
                        A.activation(qsq[:, 512 * i:512 * i + n], q_banks(c)[i][:, 0:n], ACT.Square).then_inc(q_sq, 1)
                    act.wait_ge(ss_ready, at(b, ss_ready, c + 1))
                    A.activation(ssq[:, c, :], ssq[:, c, :], ACT.Ln, bias=eps6[:, 0:1]).then_inc(act_step, 1)
                    act.wait_ge(act_step, step())
                    A.activation(rn[:, c, :], ssq[:, c, :], ACT.Exp, scale=-0.5).then_inc(rn_ready, 1)
                    for g in range(NG):
                        act.wait_ge(l_ps, at(b, l_ps, NG * c + g + 1))
                        if c and g == 0:
                            act.wait_ge(pt_ready, at(b, pt_ready, NG * c))
                        A.activation(dt[:, GH * g:GH * (g + 1), :].rearrange("p h t -> p (h t)"), l_banks(c)[g][:, :], ACT.Exp).then_inc(dt_ready, 1)

                def gram(c):
                    for i, n in enumerate((4, 2)):
                        act.wait_ge(kh_ps, at(b, kh_ps, 2 * c + i + 1))
                        if c >= 2 and i == 0:
                            act.wait_ge(ks_ps, at(b, ks_ps, NG * (c - 1)))
                        A.copy(kh_t[:, c % 2, 4 * i:4 * i + n, :], k_banks(c)[i][:, 0:n * P].rearrange("p (n t) -> p n t", n=n)).then_inc(kh_ready, 1)

                def levels(c):
                    lower = [(slice(32, 64), slice(0, 32)), (slice(96, P), slice(64, 96))]
                    for s in range(3, 8):
                        for g in range(NG):
                            hs = slice(GH * g, GH * (g + 1))
                            act.wait_ge(lv_ps, at(b, lv_ps, 24 * c + NG * s + g + 1))
                            ps = level_bank(s, g)
                            full = ps[:, :].rearrange("p (h t) -> p h t", h=GH)
                            part = ps[:, 0:GH * DK].rearrange("p (h t) -> p h t", h=GH)
                            if s == 3:
                                for r, q in lower:
                                    ins = A.copy(u32[r, hs, q], full[r, :, q])
                            elif s == 4:
                                r, q = lower[0]
                                ins = A.mul(tw[r, hs, q], full[r, :, q], -1.0)
                            elif s == 5:
                                for r, q in lower:
                                    ins = A.mul(xw[q, hs, r], full[q, :, r], -1.0)
                            elif s == 6:
                                ins = A.copy(u64[DK:P, hs, :], part[DK:P])
                            else:
                                ins = A.mul(xw[0:DK, hs, DK:P], part[0:DK], -1.0)
                            ins.then_inc(lv_sb, 1)

                def gate_silu(c):
                    nc.scalar.preload_act_table_set("silu_and_others")
                    for g in range(NG):
                        act.wait_ge(gt_ps, at(b, gt_ps, NG * c + g + 1))
                        A.activation(gate[:, GH * g:GH * (g + 1), :].rearrange("p h v -> p (h v)"), gate_banks[g][:, :], ACT.Silu).then_inc(gate_ready, 1)
                    nc.scalar.preload_act_table_set(EXP_LN)

                def scan(c):
                    for g in range(NG):
                        act.wait_ge(qs_ps, at(b, qs_ps, NG * c + g + 1))
                        ps = low_banks[g]
                        for j, h in enumerate(range(HD)[HS[g]]):
                            ins = A.mul(qse[:, h, :], ps[:, j * P:(j + 1) * P], dec[:, c, 0, h:h + 1])
                        ins.then_inc(qse_ready, 1)
                    for g in range(NG):
                        act.wait_ge(yd_ps, at(b, yd_ps, NG * c + g + 1))
                        ps = high_banks[g]
                        for j, h in enumerate(range(HD)[HS[g]]):
                            ins = A.mul(dl[:, h, :], ps[:, j * P:(j + 1) * P], beta[:, c, h:h + 1])
                        ins.then_inc(dl_ready, 1)

                def rms(c):
                    act.wait_ge(ot_ready, at(b, ot_ready, c + 1))
                    A.activation(fac[:, 0, :], fac[:, 0, :], ACT.Ln, scale=1.0 / DV, bias=eps5[:, 0:1]).then_inc(act_step, 1)
                    act.wait_ge(act_step, step())
                    A.activation(fac[:, 2, :], fac[:, 0, :], ACT.Exp, scale=-0.5).then_inc(of_ready, 1)

                def project(c):
                    act.wait_ge(o_ready, at(b, o_ready, NG * (c + 1)))
                    for g in range(NG):
                        act.wait_ge(og_ps, at(b, og_ps, NG * c + g + 1))
                        A.copy(ogt[:, GH * g:GH * (g + 1), :], og_banks[g][:, :].rearrange("p (h t) -> p h t", h=GH)).then_inc(ogt_ready, 1)

                walk = {"conv": convolve, "values": values, "norm": norm, "gram": gram, "levels": levels, "gate": gate_silu, "scan": scan, "rms": rms, "project": project,
                        "enter_stats": lambda ahead: enter_stats(b, ahead), "enter_qkv": lambda ahead: enter_qkv(b, ahead)}
                for name, c in pe_act_stages:
                    if name in walk:
                        walk[name](c)

                layer_norm(LEAVE)
                act.wait_ge(rt_d, at(b, rt_d, 1))
                A.activation(small[:, 64:96], small[:, 64:96], ACT.Exp).then_inc(rt_e, 1)
                for j in range(FT):
                    act.wait_ge(f_ps, at(b, f_ps, j + 1))
                    A.activation(hid1[:, j, :], f_bank(j)[:, :], ACT.Gelu_apprx_tanh, bias=b1f[:, j:j + 1]).then_inc(f_sb, 1)
                act.wait_ge(x_done, at(b, x_done, 2))
                act.dma_start(out[bass.ds(b, 1), :, :].rearrange("a (c p) d -> p (a c) d", p=P), xs[:, :, :]).then_inc(out_sent, 16)
            act.wait_ge(out_sent, 16 * (NB + 1))

        @block.gpsimd
        def _(pool):
            G = nc.gpsimd
            pro = [0]

            def then(ins):
                pro[0] += 1
                ins.then_inc(pool_pro, 1)
                pool.wait_ge(pool_pro, pro[0])

            def keep(ap, pattern, base, step, fill, op=ALU.is_ge):
                return G.affine_select(out=ap, in_=ap, compare_op=op, fill=fill, base=base, pattern=pattern, channel_multiplier=step)

            m16 = mask16[:, :].rearrange("p (q k i) -> p q k i", q=4, k=2)
            G.memset(ident[:, :], 0.0)
            G.memset(ident_bf[:, :], 0.0)
            G.memset(ones[:, :], 1.0)
            G.memset(v_pad[:, 1:32 - DA], 0.0)
            G.memset(v_pad[:, 0:1], 1.0)
            G.memset(later[:, :], 1.0)
            G.memset(upto[:, :], 1.0)
            G.memset(mask_q[:, :], 0.0)
            G.memset(mask_k[:, :, :], 0.0)
            G.memset(m16[:, :, 0, :], 1.0)
            G.memset(m16[:, :, 1, :], 0.0)
            G.memset(eye16[:, :], 0.0)
            G.memset(eps5[:, :], 1e-5)
            then(G.memset(eps6[:, :], 1e-6))
            G.memset(eye16[:, 0:BS * BS:BS + 1], 1.0)
            keep(ident[:, :], [[-1, P]], 0, 1, 1.0, ALU.not_equal)
            keep(ident_bf[:, :], [[-1, P]], 0, 1, 1.0, ALU.not_equal)
            keep(later[:, :], [[-1, P]], -1, 1, 0.0)
            keep(upto[:, :], [[1, P]], 0, -1, 0.0)
            keep(mask_q[:, :], [[-1, P]], 0, 1, MASKED)
            keep(mask_k[:, :, :], [[0, GH], [1, P]], 0, -1, MASKED)
            then(keep(mask16[:, :].rearrange("p (q i) -> p q i", q=4), [[-32, 4], [0, 32]], -16, 1, 0.0))
            G.iota(iota8[:, :], pattern=[[1, NE]], base=0, channel_multiplier=0, allow_small_or_imprecise_dtypes=True)
            keep(mask16[:, :].rearrange("p (q i) -> p q i", q=4), [[32, 4], [0, 32]], 31, -1, 0.0).then_inc(masks_made, 1)

            def enter_k(b, ahead):
                if ahead:
                    pool.wait_ge(o_ready, at(b, o_ready, NG * NT))
                else:
                    pool.wait_ge(x_done, at(b, x_done, 1))
                pad = v_pad[:, :].unsqueeze(1).unsqueeze(1).to_broadcast([P, NT, HA, 32 - DA])
                G.tensor_tensor(v32[:, :, :, DA:32], pad, pad, ALU.mult).then_inc(v_pads, 1)

            enter_k(0, 0)

            with pool.Fori(0, NB) as b:

                def convolve(i):
                    for n in lots(add_stops)[i]:
                        pool.wait_ge(taps, at(b, taps, n + 1))
                        G.tensor_tensor(acc[:, n % 4, 1:T], acc[:, n % 4, 1:T], acc2[:, n % 3, 0:T - 1], ALU.add).then_inc(taps_added, 1)

                def norm(c):
                    if c == 0:
                        pool.wait_ge(z_ps, at(b, z_ps, NQK))
                        pool.wait_ge(gk_ready, at(b, gk_ready, 1))
                    else:
                        pool.wait_ge(l_ps, at(b, l_ps, NG * c))
                    if c >= 2:
                        pool.wait_ge(lv_ps, at(b, lv_ps, 24 * (c - 2) + 3 * NG))
                    G.tensor_tensor(gm[:, :, :], upto[:, :].unsqueeze(1).to_broadcast([P, HD, P]), wide(gk[:, c, :], [P, HD, P]), ALU.mult).then_inc(gm_ready, 1)

                def gram(c):
                    for g, hs in enumerate(HS):
                        pool.wait_ge(gd_ready, at(b, gd_ready, NG * c + g + 1))
                        G.tensor_tensor(bms[c % 2][:, hs, :], bms[c % 2][:, hs, :], wide(beta[:, c, hs], [P, GH, P]), ALU.mult).then_inc(bm_ready, 1)
                    pool.wait_ge(khat_ready, at(b, khat_ready, c + 1))
                    pool.wait_ge(dec_ready, at(b, dec_ready, 1))
                    if c >= 2:
                        pool.wait_ge(su_ps, at(b, su_ps, 2 * (c - 1)))
                    G.tensor_tensor(kd[:, c % 2, :, :], khat.rearrange("p (h d) -> p h d", d=DK), wide(dec[:, c, 1, :], [P, HD, DK]), ALU.mult).then_inc(kd_ready, 1)

                def scan(c):
                    if c + 1 < NT:
                        pool.wait_ge(s_ready, at(b, s_ready, 2 * c + 1))
                        pool.wait_ge(khat_ready, at(b, khat_ready, min(c + 3, NT)))
                        G.tensor_tensor(sdec, state[:, :, :], wide(dec_end[:, c, :], [P, NP, DV]), ALU.mult).then_inc(sd_ready, 1)

                def rms(c):
                    pool.wait_ge(yd_ps, at(b, yd_ps, NG * (c + 1)))
                    pool.wait_ge(o_ready, at(b, o_ready, NG * (c + 1)))
                    G.tensor_tensor(osq, ob, ob, ALU.mult).then_inc(osq_ready, 1)

                def scale(c):
                    pool.wait_ge(on_ready, at(b, on_ready, c + 1))
                    pool.wait_ge(gate_ready, at(b, gate_ready, NG * (c + 1)))
                    G.tensor_tensor(og, ob, gate[:, :, :], ALU.mult).then_inc(og_ready, 1)

                walk = {"conv": convolve, "norm": norm, "gram": gram, "scan": scan, "rms": rms, "scale": scale,
                        "enter_k": lambda ahead: enter_k(b, ahead)}
                for name, c in pool_stages:
                    if name in walk:
                        walk[name](c)

        @block.sync
        def _(sp):
            for dst, src in const_loads:
                sp.dma_start(dst, src).then_inc(consts_in, 16)
            sp.wait_ge(prologue_sb, 1)
            sp.dma_start(gate_rows, g_rows).then_inc(rows_out, 16)
            sp.wait_ge(prologue_sb, 2 + 2 * NW // 4)
            sp.dma_start(one_rows, k_stack[0:PARTS, :, :].rearrange("p h t -> p (h t)")).then_inc(out_sent, 16)
            sp.dma_start(w1_bounce, w1t.rearrange("p n m -> p (n m)")).then_inc(weights_out, 16)
            sp.dma_start(w2_bounce, w2t.rearrange("p n m -> p (n m)")).then_inc(weights_out, 16)
            sp.wait_ge(rows_out, 16)
            sp.wait_ge(out_sent, 16)
            sp.wait_ge(weights_out, 32)
            sp.wait_ge(silu_c, 1)

            def tokens(b, ahead):
                sp.wait_ge(xin_free, at(b, xin_free, 1, ahead))
                sp.dma_start(xin[:, :, :], L0_attn_x[bass.ds((b + ahead) % NB, 1), :, :].rearrange("a (c p) d -> p (a c) d", p=P)).then_inc(x_in, 16)

            def enter_parts(b, ahead):
                for i in range(2):
                    sp.wait_ge(qk_parts, at(b, qk_parts, i + 1, ahead))
                    sp.dma_start(qk_bounce[i].rearrange("h d n t -> (h d) n t"), qkp[:, i, :, :]).then_inc(parts_out, 16)
                sp.dma_start(k_stack[KS:KS + PARTS, :, :].rearrange("p h t -> p (h t)"), one_rows).then_inc(stacks_in, 16)
                sp.wait_ge(parts_out, at(b, parts_out, 32, ahead))
                for i, stack in enumerate((q_stack, k_stack)):
                    for s in range(PARTS * PARTS):
                        part = s // PARTS if i == 0 else s % PARTS
                        sp.dma_start(stack[DA * s:DA * (s + 1), :, :], qk_bounce[i, :, :, part, :].rearrange("h d t -> d h t")).then_inc(stacks_in, 16)

            tokens(0, 0)
            enter_parts(0, 0)

            with sp.Fori(0, NB) as b:
                sp.wait_ge(x_done, at(b, x_done, 1))
                sp.dma_start(gates[:, :, :].rearrange("p i d -> p (i d)"),
                                gate_rows[bass.ds(b, 1), :].rearrange("a n -> (a n)").partition_broadcast(P)).then_inc(gates_in, 16)
                sp.dma_start(w1t.rearrange("p n m -> p (n m)"), w1_bounce).then_inc(w_in, 16)
                sp.dma_start(w2t.rearrange("p n m -> p (n m)"), w2_bounce).then_inc(w_in, 16)
                nq, nv = HD * DK, HD * DV
                sp.dma_start(wconv[:, 0:nq], L1_attn_Wq).then_inc(wc_in, 16)
                sp.dma_start(wconv[:, nq:2 * nq], L1_attn_Wk).then_inc(wc_in, 16)
                sp.dma_start(wconv[:, 2 * nq:2 * nq + nv], L1_attn_Wv).then_inc(wc_in, 16)
                for hh in range(2):
                    sp.wait_ge(m_sb, at(b, m_sb, hh + 1))
                    sp.dma_start(m_bounce[hh].rearrange("p (a t) -> (p a) t", t=P), m_t[:, :]).then_inc(m_out, 16)
                    sp.wait_ge(m_out, at(b, m_out, 16 * (hh + 1)))
                    sp.dma_start(q_stack[KS:KS + PARTS, 8 * hh:8 * hh + 8, :], m_bounce[hh].rearrange("p (h t) -> p h t", t=T)).then_inc(m_in[hh], 16)
                tokens(b, 1)
                for c in range(NT):
                    sp.wait_ge(bm_ready, at(b, bm_ready, NG * (c + 1)))
                    for q in range(NBK):
                        r = slice(BS * q, BS * (q + 1))
                        sp.dma_start(b_bounce[q].rearrange("h j i -> j h i"), bms[c % 2][r, :, r]).then_inc(b_out, 16)
                    sp.wait_ge(b_out, at(b, b_out, 16 * NBK * (c + 1)))
                    sp.dma_start(blk[:, :], b_bounce.rearrange("q h j i -> (q h) (j i)")).then_inc(b_in, 16)
                    sp.wait_ge(t_ready, at(b, t_ready, c + 1))
                    sp.dma_start(t_bounce[0].rearrange("q h i k -> (q h) (i k)"), blk_t[:, :]).then_inc(t_out, 16)
                    sp.dma_start(t_bounce[1].rearrange("q h i k -> (q h) (i k)"), blk_x[:, :]).then_inc(t_out, 16)
                    sp.wait_ge(t_out, at(b, t_out, 32 * (c + 1)))
                    for q in range(NBK):
                        r = slice(BS * q, BS * (q + 1))
                        sp.dma_start(t16[r, :, r], t_bounce[0, q].rearrange("h i k -> i h k")).then_inc(t_in, 16)
                        sp.dma_start(x16[r, :, r], t_bounce[1, q].rearrange("h i k -> i h k")).then_inc(t_in, 16)
                enter_parts(b, 1)
            sp.wait_ge(stacks_in, at(NB, stacks_in, IN_ROW["stacks_in"]))


_INS = ['L0_attn_x', 'L0_attn_w_qkv', 'L0_attn_b_qkv', 'L0_attn_w_proj', 'L0_attn_b_proj', 'L0_ffn_W1', 'L0_ffn_b1', 'L0_ffn_W2',
        'L0_ffn_b2', 'L0_ffn_Wg', 'L0_ffn_bg', 'L0_c', 'L0_wmod', 'L1_attn_Wq', 'L1_attn_Wk', 'L1_attn_Wv', 'L1_attn_Wg',
        'L1_attn_Wo', 'L1_attn_conv_q', 'L1_attn_conv_k', 'L1_attn_conv_v', 'L1_attn_Wgk', 'L1_attn_Wb', 'L1_attn_b_b',
        'L1_attn_A_log', 'L1_attn_dt_bias', 'L1_attn_g_norm_weight', 'L1_ffn_router_w', 'L1_ffn_w1', 'L1_ffn_b1', 'L1_ffn_w2',
        'L1_ffn_b2', 'L1_c', 'L1_wmod']
_OUT = ((8, 512, 128), 'float32')


def kernel(**inputs):
    import numpy as _np
    import concourse.bacc as _bacc
    from concourse import mybir as _mybir
    from concourse.bass_utils import run_bass_kernel_spmd as _run

    nc = _bacc.Bacc("TRN2", target_bir_lowering=False, num_devices=1)
    arrays, args = {}, []
    for name in _INS:
        a = _np.ascontiguousarray(inputs[name])
        arrays[f"in_{name}_dram"] = a
        args.append(nc.dram_tensor(f"in_{name}_dram", a.shape, _mybir.dt.from_np(a.dtype), kind="ExternalInput").ap())
    shape, dtype = _OUT
    args.append(nc.dram_tensor("out_dram", shape, _mybir.dt.from_np(_np.dtype(dtype)), kind="ExternalOutput").ap())
    adaln_two_layers(nc, *args)
    r = _run(nc, [arrays], core_ids=[0])
    return r.results[0]["out_dram"]
```
